# Optimizing a Trainium2 kernel written in Bass

```python
import numpy as np
import jax
import jax.numpy as jnp

def _softmax(x, axis=-1):
    return jax.nn.softmax(x, axis=axis)

def _gelu(x):
    return jax.nn.gelu(x, approximate=True)

def _silu(x):
    return jax.nn.silu(x)

def _sigmoid(x):
    return jax.nn.sigmoid(x)

def _layernorm(x, axis=-1, eps=1e-05):
    m = jnp.mean(x, axis=axis, keepdims=True)
    v = jnp.var(x, axis=axis, keepdims=True)
    return (x - m) / jnp.sqrt(v + eps)

def _scatter_add(tgt, idx, src, axis=0):
    return tgt.at[idx].add(src)

def _segment_sum(src, seg, n):
    return jax.ops.segment_sum(src, seg, n)
kernel_name = 'mk_decoder_preln_d1_seqx_r4_a0a389'

def setup_inputs(seed: int=0):
    np.random.seed(seed)
    _w = jnp.asarray

    def _rec_inputs():
        import jax
        import jax.numpy as jnp
        _rk = jax.random.key(seed)
        x = 7.22e-05 + 1 * jax.random.normal(jax.random.fold_in(_rk, 1), (4, 512, 256), jnp.float32)
        _lenS = 512 - jax.random.randint(jax.random.fold_in(_rk, 7), (4,), 0, max(1, 512 // 4) + 1, jnp.int32)
        _lenS2 = 512 - jax.random.randint(jax.random.fold_in(_rk, 8), (4,), 0, max(1, 512 // 4) + 1, jnp.int32)
        _ctx_1024P = jax.random.normal(jax.random.fold_in(_rk, 11), (4, 16, 256), jnp.float32)
        _ctx_1024c = jax.random.dirichlet(jax.random.fold_in(_rk, 511), 0.3 * jnp.ones((16,), jnp.float32), (4, 512))
        _ctx_1024t = jnp.einsum('bsk,bkd->bsd', _ctx_1024c, _ctx_1024P)
        _ctx_1024t = _ctx_1024t * jax.lax.rsqrt(jnp.mean(jnp.square(_ctx_1024t)) + 1e-12) * 0.953939
        ctx_1024 = 4.13588e-05 + 0.999923 * (_ctx_1024t + 0.3 * jax.random.normal(jax.random.fold_in(_rk, 611), (4, 512, 256), jnp.float32))
        pos_BxS2 = jnp.broadcast_to(jnp.arange(512, dtype=jnp.int32), (4, 512))
        return (x, ctx_1024, pos_BxS2)
    x, ctx_1024, pos_BxS2 = _rec_inputs()

    def _L0_attn_setup():
        import jax, jax.numpy as jnp
        import numpy as np
        D_MODEL = 256
        NHEAD = 16
        D_K = D_MODEL // NHEAD
        MAX_REL = 256
        key = jax.random.key(seed)
        ks = jax.random.split(key, 6)
        B, S = (4, 512)
        s = 1.0 / np.sqrt(D_MODEL)
        x = jax.random.normal(ks[0], (B, S, D_MODEL), dtype=jnp.float32)
        W_qkv = jax.random.normal(ks[1], (D_MODEL, 3 * D_MODEL), dtype=jnp.float32) * s
        b_qkv = jnp.zeros((3 * D_MODEL,), dtype=jnp.float32)
        W_out = jax.random.normal(ks[2], (D_MODEL, D_MODEL), dtype=jnp.float32) * s
        b_out = jnp.zeros((D_MODEL,), dtype=jnp.float32)
        rel_bias = jax.random.normal(ks[3], (2 * MAX_REL + 1, NHEAD), dtype=jnp.float32) * 0.02
        return {'x': x, 'W_qkv': W_qkv, 'b_qkv': b_qkv, 'W_out': W_out, 'b_out': b_out, 'rel_bias': rel_bias}
    _L0_attn_all = _L0_attn_setup()
    _L0_attn_in = {k: v for k, v in _L0_attn_all.items() if k in ('W_qkv', 'b_qkv', 'W_out', 'b_out', 'rel_bias')}
    del _L0_attn_all

    def _L0_xattn_setup():
        import jax, jax.numpy as jnp
        import numpy as np
        D_MODEL = 256
        NUM_HEADS = 16
        HEAD_DIM = D_MODEL // NUM_HEADS
        THETA = 10000.0
        B, S = (4, 512)

        def _rope(x, pos):
            half = HEAD_DIM // 2
            inv_freq = THETA ** (-(jnp.arange(half, dtype=jnp.float32) * 2.0) / HEAD_DIM)
            ang = pos.astype(jnp.float32)[:, None, :, None] * inv_freq
            cos, sin = (jnp.cos(ang), jnp.sin(ang))
            x1, x2 = (x[..., 0::2], x[..., 1::2])
            r1 = x1 * cos - x2 * sin
            r2 = x1 * sin + x2 * cos
            return jnp.stack([r1, r2], axis=-1).reshape(x.shape)
        key = jax.random.key(seed)
        ks = jax.random.split(key, 12)
        scale = 1.0 / np.sqrt(D_MODEL)
        inp = {'query': jax.random.normal(ks[0], (B, S, D_MODEL), dtype=jnp.float32), 'key': jax.random.normal(ks[1], (B, S, D_MODEL), dtype=jnp.float32), 'value': jax.random.normal(ks[2], (B, S, D_MODEL), dtype=jnp.float32), 'token_positions': jnp.broadcast_to(jnp.arange(S, dtype=jnp.int32), (B, S)), 'w_q': jax.random.normal(ks[3], (D_MODEL, D_MODEL), dtype=jnp.float32) * scale, 'b_q': jnp.zeros((D_MODEL,), dtype=jnp.float32), 'w_k': jax.random.normal(ks[4], (D_MODEL, D_MODEL), dtype=jnp.float32) * scale, 'b_k': jnp.zeros((D_MODEL,), dtype=jnp.float32), 'w_v': jax.random.normal(ks[5], (D_MODEL, D_MODEL), dtype=jnp.float32) * scale, 'b_v': jnp.zeros((D_MODEL,), dtype=jnp.float32), 'w_o': jax.random.normal(ks[6], (D_MODEL, D_MODEL), dtype=jnp.float32) * scale, 'b_o': jnp.zeros((D_MODEL,), dtype=jnp.float32)}
        return inp
    _L0_xattn_all = _L0_xattn_setup()
    _L0_xattn_in = {k: v for k, v in _L0_xattn_all.items() if k in ('w_q', 'b_q', 'w_k', 'b_k', 'w_v', 'b_v', 'w_o', 'b_o')}
    del _L0_xattn_all

    def _L0_ffn_setup():
        import jax, jax.numpy as jnp
        import numpy as np
        H = 256
        I = 128
        E = 32
        TOP_K = 6
        N_GROUP = 8
        TOPK_GROUP = 4
        SCALE = 2.5
        N_SHARED = 2
        SI = I * N_SHARED
        B, S = (2, 256)
        key = jax.random.key(seed)
        ks = jax.random.split(key, 8)
        x = jax.random.normal(ks[0], (B, S, H), jnp.float32)
        gate_weight = jax.random.normal(ks[1], (E, H), jnp.float32) * 0.02
        e_score_correction_bias = jax.random.normal(ks[2], (E,), jnp.float32) * 0.01
        experts_gate_up = jax.random.normal(ks[3], (E, 2 * I, H), jnp.float32) * 0.02
        experts_down = jax.random.normal(ks[4], (E, H, I), jnp.float32) * 0.02
        shared_gate_w = jax.random.normal(ks[5], (SI, H), jnp.float32) * 0.02
        shared_up_w = jax.random.normal(ks[6], (SI, H), jnp.float32) * 0.02
        shared_down_w = jax.random.normal(ks[7], (H, SI), jnp.float32) * 0.02
        return {'x': x, 'gate_weight': gate_weight, 'e_score_correction_bias': e_score_correction_bias, 'experts_gate_up': experts_gate_up, 'experts_down': experts_down, 'shared_gate_w': shared_gate_w, 'shared_up_w': shared_up_w, 'shared_down_w': shared_down_w}
    _L0_ffn_all = _L0_ffn_setup()
    _L0_ffn_in = {k: v for k, v in _L0_ffn_all.items() if k in ('gate_weight', 'e_score_correction_bias', 'experts_gate_up', 'experts_down', 'shared_gate_w', 'shared_up_w', 'shared_down_w')}
    del _L0_ffn_all
    return {'x': x, 'ctx_1024': ctx_1024, 'pos_BxS2': pos_BxS2, 'L0_attn_W_qkv': _L0_attn_in['W_qkv'], 'L0_attn_b_qkv': _L0_attn_in['b_qkv'], 'L0_attn_W_out': _L0_attn_in['W_out'], 'L0_attn_b_out': _L0_attn_in['b_out'], 'L0_attn_rel_bias': _L0_attn_in['rel_bias'], 'L0_xattn_w_q': _L0_xattn_in['w_q'], 'L0_xattn_b_q': _L0_xattn_in['b_q'], 'L0_xattn_w_k': _L0_xattn_in['w_k'], 'L0_xattn_b_k': _L0_xattn_in['b_k'], 'L0_xattn_w_v': _L0_xattn_in['w_v'], 'L0_xattn_b_v': _L0_xattn_in['b_v'], 'L0_xattn_w_o': _L0_xattn_in['w_o'], 'L0_xattn_b_o': _L0_xattn_in['b_o'], 'L0_ffn_gate_weight': _L0_ffn_in['gate_weight'], 'L0_ffn_e_score_correction_bias': _L0_ffn_in['e_score_correction_bias'], 'L0_ffn_experts_gate_up': _L0_ffn_in['experts_gate_up'], 'L0_ffn_experts_down': _L0_ffn_in['experts_down'], 'L0_ffn_shared_gate_w': _L0_ffn_in['shared_gate_w'], 'L0_ffn_shared_up_w': _L0_ffn_in['shared_up_w'], 'L0_ffn_shared_down_w': _L0_ffn_in['shared_down_w']}

def reference(x, ctx_1024, pos_BxS2, L0_attn_W_qkv, L0_attn_b_qkv, L0_attn_W_out, L0_attn_b_out, L0_attn_rel_bias, L0_xattn_w_q, L0_xattn_b_q, L0_xattn_w_k, L0_xattn_b_k, L0_xattn_w_v, L0_xattn_b_v, L0_xattn_w_o, L0_xattn_b_o, L0_ffn_gate_weight, L0_ffn_e_score_correction_bias, L0_ffn_experts_gate_up, L0_ffn_experts_down, L0_ffn_shared_gate_w, L0_ffn_shared_up_w, L0_ffn_shared_down_w):
    import jax
    import jax.numpy as jnp

    def _L0_attn_ref(x, W_qkv, b_qkv, W_out, b_out, rel_bias):
        import jax, jax.numpy as jnp
        import numpy as np
        D_MODEL = 256
        NHEAD = 16
        D_K = D_MODEL // NHEAD
        MAX_REL = 256
        B, S, D = x.shape
        qkv = x @ W_qkv + b_qkv
        qkv = qkv.reshape(B, S, 3, NHEAD, D_K)
        q, k, v = (qkv[:, :, 0], qkv[:, :, 1], qkv[:, :, 2])
        scores = jnp.einsum('bihd,bjhd->bhij', q, k) / jnp.sqrt(jnp.float32(D_K))
        idxs = jnp.arange(S)
        rel = jnp.clip(idxs[:, None] - idxs[None, :] + MAX_REL, 0, 2 * MAX_REL)
        bias = rel_bias[rel]
        scores = scores + jnp.transpose(bias, (2, 0, 1))[None]
        attn = jax.nn.softmax(scores, axis=-1)
        out = jnp.einsum('bhij,bjhd->bihd', attn, v).reshape(B, S, D)
        return out @ W_out + b_out

    def _L0_xattn_ref(query, key, value, token_positions, w_q, b_q, w_k, b_k, w_v, b_v, w_o, b_o):
        import jax, jax.numpy as jnp
        import numpy as np
        D_MODEL = 256
        NUM_HEADS = 16
        HEAD_DIM = D_MODEL // NUM_HEADS
        THETA = 10000.0
        B, S = (4, 512)

        def _rope(x, pos):
            half = HEAD_DIM // 2
            inv_freq = THETA ** (-(jnp.arange(half, dtype=jnp.float32) * 2.0) / HEAD_DIM)
            ang = pos.astype(jnp.float32)[:, None, :, None] * inv_freq
            cos, sin = (jnp.cos(ang), jnp.sin(ang))
            x1, x2 = (x[..., 0::2], x[..., 1::2])
            r1 = x1 * cos - x2 * sin
            r2 = x1 * sin + x2 * cos
            return jnp.stack([r1, r2], axis=-1).reshape(x.shape)
        b, s, _ = query.shape
        Q = query @ w_q + b_q
        K = key @ w_k + b_k
        V = value @ w_v + b_v
        Q = Q.reshape(b, s, NUM_HEADS, HEAD_DIM).transpose(0, 2, 1, 3)
        K = K.reshape(b, s, NUM_HEADS, HEAD_DIM).transpose(0, 2, 1, 3)
        V = V.reshape(b, s, NUM_HEADS, HEAD_DIM).transpose(0, 2, 1, 3)
        Q = _rope(Q, token_positions)
        K = _rope(K, token_positions)
        scores = jnp.einsum('bhqd,bhkd->bhqk', Q, K) / jnp.sqrt(jnp.float32(HEAD_DIM))
        causal = jnp.tril(jnp.ones((s, s), dtype=bool))
        scores = jnp.where(causal, scores, -jnp.inf)
        attn = jax.nn.softmax(scores, axis=-1)
        out = jnp.einsum('bhqk,bhkd->bhqd', attn, V)
        out = out.transpose(0, 2, 1, 3).reshape(b, s, D_MODEL)
        return out @ w_o + b_o

    def _L0_ffn_ref(x, gate_weight, e_score_correction_bias, experts_gate_up, experts_down, shared_gate_w, shared_up_w, shared_down_w):
        import jax, jax.numpy as jnp
        import numpy as np
        H = 256
        I = 128
        E = 32
        TOP_K = 6
        N_GROUP = 8
        TOPK_GROUP = 4
        SCALE = 2.5
        N_SHARED = 2
        SI = I * N_SHARED
        B, S = (2, 256)
        b, s, h = x.shape
        xf = x.reshape(-1, h)
        T = xf.shape[0]
        logits = xf.astype(jnp.float32) @ gate_weight.astype(jnp.float32).T
        scores = jax.nn.sigmoid(logits)
        sfc = scores + e_score_correction_bias[None, :]
        gs = E // N_GROUP
        group_scores = sfc.reshape(T, N_GROUP, gs).max(axis=-1)
        _, gidx = jax.lax.top_k(group_scores, TOPK_GROUP)
        gmask = jnp.zeros((T, N_GROUP), bool).at[jnp.arange(T)[:, None], gidx].set(True)
        smask = jnp.repeat(gmask, gs, axis=1)
        masked = jnp.where(smask, sfc, 0.0)
        _, topk_idx = jax.lax.top_k(masked, TOP_K)
        tw = jnp.take_along_axis(scores, topk_idx, axis=1)
        tw = tw / (tw.sum(-1, keepdims=True) + 1e-20)
        tw = (tw * SCALE).astype(xf.dtype)
        combine = jnp.zeros((T, E), xf.dtype).at[jnp.arange(T)[:, None], topk_idx].add(tw)

        def expert_step(acc, inp):
            gu, dn, c = inp
            g = xf @ gu[:I].T
            u = xf @ gu[I:].T
            o = jax.nn.silu(g) * u @ dn.T
            return (acc + c[:, None] * o, None)
        routed, _ = jax.lax.scan(expert_step, jnp.zeros_like(xf), (experts_gate_up, experts_down, combine.T))
        sh = jax.nn.silu(xf @ shared_gate_w.T) * (xf @ shared_up_w.T)
        shared_out = sh @ shared_down_w.T
        return (routed + shared_out).reshape(b, s, h)
    x = x + _L0_attn_ref(_layernorm(x, axis=-1), L0_attn_W_qkv, L0_attn_b_qkv, L0_attn_W_out, L0_attn_b_out, L0_attn_rel_bias)
    x = x + _L0_xattn_ref(_layernorm(x, axis=-1), ctx_1024, ctx_1024, pos_BxS2, L0_xattn_w_q, L0_xattn_b_q, L0_xattn_w_k, L0_xattn_b_k, L0_xattn_w_v, L0_xattn_b_v, L0_xattn_w_o, L0_xattn_b_o)
    x = x + _L0_ffn_ref(_layernorm(x, axis=-1), L0_ffn_gate_weight, L0_ffn_e_score_correction_bias, L0_ffn_experts_gate_up, L0_ffn_experts_down, L0_ffn_shared_gate_w, L0_ffn_shared_up_w, L0_ffn_shared_down_w)
    return x

_drawn_inputs = setup_inputs


def setup_inputs(seed=0):
    import zlib

    import numpy as np

    out = dict(_drawn_inputs(seed))
    spreads = {'L0_attn_b_qkv': (0.0, 0.1),
     'L0_attn_b_out': (0.0, 0.1),
     'L0_xattn_b_q': (0.0, 0.452),
     'L0_xattn_b_k': (0.0, 0.8),
     'L0_xattn_b_v': (0.0, 0.1),
     'L0_xattn_b_o': (0.0, 0.1)}
    factors = {'L0_attn_rel_bias': 8.0,
     'L0_ffn_gate_weight': 5.931,
     'L0_ffn_e_score_correction_bias': 8.0,
     'L0_ffn_experts_gate_up': 5.307,
     'L0_ffn_experts_down': 5.307,
     'L0_ffn_shared_gate_w': 3.563,
     'L0_ffn_shared_up_w': 3.723,
     'L0_ffn_shared_down_w': 3.544}
    for name, (base, spread) in spreads.items():
        noise = np.random.default_rng([zlib.crc32(name.encode()), seed]).standard_normal(out[name].shape)
        drawn = base * np.exp(spread * noise) if base else spread * noise
        out[name] = jnp.asarray(drawn.astype(out[name].dtype))
    for name, factor in factors.items():
        out[name] = (out[name] * factor).astype(out[name].dtype)
    return out
```

```python
from contextlib import ExitStack

import numpy as np

import concourse.bass as bass
from concourse import mybir

F32 = mybir.dt.float32
F32R = mybir.dt.float32r
I32 = mybir.dt.int32
U32 = mybir.dt.uint32
ALU = mybir.AluOpType
ACT = mybir.ActivationFunctionType
AX_X = mybir.AxisListType.X

P = 128
B, S, D = 4, 512, 256
H, DK = 16, 16
NC = D // P
TB = S // P
NT = B * TB
HG = 4
G = H // HG
GW = HG * DK
U = G * B
MAX_REL = 256
TW = S - P + S
RPW = 1024
RAW_SCALE = float(DK) ** -0.5
EPS = 1e-5
BIG = 1e30
USES = HG * TB + 2
SCORED_0 = 2 * 2 * TB
LOADS = 9
SHIFT_ROW = 64
THETA = 10000.0
INV_FREQ = (np.float32(THETA) ** (-(np.arange(DK // 2, dtype=np.float32) * np.float32(2.0)) / np.float32(DK))).astype(np.float32)
TWO_PI = 2.0 * np.pi
C1 = 6.28125
C2 = float(np.float32(TWO_PI - C1))
C3 = float(np.float32(TWO_PI - C1 - float(np.float32(TWO_PI - C1))))
ROUND = 1.5 * 2.0 ** 23
PI_SAFE = 3.1415925


E, TOPK, NGROUP, TOPG = 32, 6, 8, 4
GE = E // NGROUP
I = 128
SHARED = 2
EA = SHARED + E
WW = NC * 2 * I + D
ROUTED_SCALE = 2.5


def program(nc, x, ctx_t, pos, w_qkv, b_qkv_col, b_v, w_out, b_out, rel_pad, xw_q, xb_q, xw_k, xb_k, xw_v, xb_v, xw_o, xb_o, w_gate, e_bias, w_exp, out):
    with ExitStack() as stack:
        def sb(name, shape, dt=F32):
            return stack.enter_context(nc.sbuf_tensor(name, shape, dt))

        KB = 1024
        ARENA_AT = -(-nc.sbuf_base // KB) * KB
        stack.enter_context(nc.sbuf_tensor("arena", [P, 176 * KB + ARENA_AT - nc.sbuf_base], mybir.dt.uint8))

        def at(name, shape, kb, dt=F32):
            return nc.alloc_sbuf_tensor_at(name, shape, dt, offset=ARENA_AT + int(kb * KB))

        def sem(name):
            return stack.enter_context(nc.semaphore(name))

        def dram(name, shape):
            return nc.dram_tensor(name, shape, F32, kind="Internal")

        qk_hbm = {n: dram(f"{n}_hbm", (2, D, B * S)) for n in ("q1", "k1", "q2", "k2")}
        v_hbm = {n: dram(f"{n}_hbm", (B, G, P, TB, HG * 32)) for n in ("v1", "v2")}
        rel_hbm = dram("rel_hbm", (H, 2, RPW))

        bank = stack.enter_context(nc.psum_tensor("bank", [P, 8, 512], F32))

        X = at("X", [P, NT, D], 0)
        XN = at("XN", [P, NT, D], 16)
        ctx_sb = at("ctx_sb", [P, NC, B * S], 160)
        wqkv = sb("wqkv", [P, NC, 3 * D])
        wout = sb("wout", [P, NC, D])
        wxq = sb("wxq", [P, NC, D])
        wxk = sb("wxk", [P, NC, D])
        wxv = sb("wxv", [P, NC, D])
        wxo = sb("wxo", [P, NC, D])
        bqk_col = sb("bqk_col", [P, 4])
        bxq_col = sb("bxq_col", [P, NC])
        bxk_col = sb("bxk_col", [P, NC])
        bv_row = sb("bv_row", [P, D])
        bo_row = sb("bo_row", [P, D])
        bxv_row = sb("bxv_row", [P, D])
        bxo_row = sb("bxo_row", [P, D])
        ident = sb("ident", [P, P])
        flip = sb("flip", [P, P])
        ident_r = sb("ident_r", [P, P], F32R)
        flip_r = sb("flip_r", [P, P], F32R)
        mask_f = sb("mask_f", [P, 2, P])
        mask_r = sb("mask_r", [P, 2, P], F32R)
        pos_i = sb("pos_i", [P, NT], I32)
        pos_f = sb("pos_f", [P, NT])
        freq = sb("freq", [P, DK // 2])
        ang = [at(f"ang{n}", [P, NT, DK // 2], 152 + n / 2) for n in range(9)]
        trig = at("trig", [P, 2, NT, DK // 2, 2], 157)
        trig8 = at("trig8", [P, 2, NT, P // DK, DK], 104)
        cos_t = at("cos_t", [P, B * S], 32)
        sin_t = at("sin_t", [P, B * S], 40)
        stats = sb("stats", [P, NT, 6])
        mv = sb("mv", [P, NT, 2])
        vare = sb("vare", [P, NT])
        neghalf = sb("neghalf", [P, NT])
        rstd = sb("rstd", [P, NT])
        nT = at("nT", [P, NC, S], 92)
        oT = at("oT", [P, NC, S], 96)
        kf = at("kf", [P, NC, S], 48)
        swap = at("swap", [P, NC, S], 52)
        rot1 = at("rot1", [P, NC, S], 56)
        rot2 = at("rot2", [P, NC, S], 60)
        rot = at("rot", [P, NC, S], 64)
        hl = at("hl", [P, 4, 2, S], 68, F32R)
        vt = at("vt", [P, TB, H, 32], 84)
        rel_in = at("rel_in", [H, RPW], 136)
        rel_max = sb("rel_max", [H, 1])
        rel_s = at("rel_s", [H, RPW], 140)
        rel_hl = at("rel_hl", [H, 2, RPW], 144, F32R)
        QU = [at(f"QU{j}", [P, HG, S], 68 + 8 * j, F32R) for j in range(2)]
        KU = [at(f"KU{j}", [P, HG, S], 84 + 8 * j, F32R) for j in range(2)]
        VU = [at(f"VU{j}", [P, TB, HG, 32], 100 + 2 * j) for j in range(2)]
        toep = at("toep", [P, 2 * HG * 2 * TW], 104, F32R)
        PT = at("PT", [P, 4, 2, S], 48)
        OS = at("OS", [P, 2, S], 64)
        M = sb("M", [P, 2, HG * TB])
        MR = sb("MR", [HG * TB, 2, P], F32R)
        R = sb("R", [P, 2, TB * HG])
        wgate = sb("wgate", [P, NC, E])
        iota_i = sb("iota_i", [P, E], I32)
        nT3 = at("nT3", [P, NC, S], 32)
        nhl = at("nhl", [P, NC, 2, B * S], 140, F32R)
        bias_e = at("bias_e", [P, E], 36)
        iota_e = at("iota_e", [P, E], 36.5)
        score = at("score", [P, NT, E], 37)
        sfc = at("sfc", [P, NT, E], 39)
        masked = at("masked", [P, NT, E], 41)
        gmax = at("gmax", [P, NT, NGROUP], 43)
        gtop = at("gtop", [P, NT, 8], 43.5)
        gidx = at("gidx", [P, NT, 8], 44, U32)
        gidx_f = at("gidx_f", [P, NT, 8], 44.5)
        gmask = at("gmask", [P, NT, NGROUP], 45)
        etop = at("etop", [P, NT, 8], 45.5)
        eidx = at("eidx", [P, NT, 8], 46, U32)
        eidx_f = at("eidx_f", [P, NT, 8], 46.5)
        tws = at("tws", [P, NT], 47)
        twe = at("twe", [P, NT], 47.125)
        twr = at("twr", [P, NT], 47.25)
        gsel = at("gsel", [P, NT, TOPG, NGROUP], 48)
        esel = at("esel", [P, NT, TOPK, E], 50)
        chosen = at("chosen", [P, NT, E], 62)
        picked = at("picked", [P, NT, E], 64)
        comb = at("comb", [P, EA * NT], 100)
        csel = [at(f"csel{j}", [P, NT], 102.5 + j / 4) for j in range(2)]
        wraw = [at(f"wraw{j}", [P, WW], 104 + 3 * j) for j in range(2)]
        whl = [at(f"whl{j}", [P, 2, WW], 110 + 6 * j, F32R) for j in range(2)]
        sg = [at(f"sg{j}", [P, S], 122 + 2 * j) for j in range(2)]
        hid = [at(f"hid{j}", [P, S], 126 + 2 * j) for j in range(2)]
        hhl = [at(f"hhl{j}", [P, 2, S], 130 + 4 * j, F32R) for j in range(2)]

        x_in, pos_in, rel_in_s = sem("x_in"), sem("pos_in"), sem("rel_in_s")
        w_in, ctx_in, ctx_w_in = sem("w_in"), sem("ctx_in"), sem("ctx_w_in")
        const_a, const_b, const_m = sem("const_a"), sem("const_b"), sem("const_m")
        ang_s, ang_act, trig_ready, trig_mm, trig_out = sem("ang_s"), sem("ang_act"), sem("trig_ready"), sem("trig_mm"), sem("trig_out")
        stack_init = sem("stack_init")
        rel_ready, rel_out, t_loaded = sem("rel_ready"), sem("rel_out"), sem("t_loaded")
        vt_init = sem("vt_init")

        NORM = ("stat", "mv", "var", "rstd", "xn", "tr", "trev")
        ROPE = ("kf", "swap", "rot1", "rot2", "rot")

        def sems(n, kinds):
            return {k: sem(f"{n}_{k}") for k in kinds}

        def sent(n, chunks, tiles=0):
            return {"sent": [sem(f"{n}_sent{m}") for m in range(chunks)], "vsent": [sem(f"{n}_vsent{k}") for k in range(tiles)]}

        pj = {
            "ctx": sent("ctx", NC, TB) | sems("ctx", ROPE + ("qk", "hi", "lo", "v", "vt")),
            "self": sent("self", 2 * NC, TB) | sems("self", NORM + ("qk", "hi", "lo", "v", "vt")),
            "xq": sent("xq", NC) | sems("xq", NORM + ROPE + ("qk", "hi", "lo")),
            "moe": sems("moe", NORM),
        }
        out_s = {n: sems(n, ("tr", "trev", "mm", "add", "bias")) for n in ("o1", "o2")}

        def attn_sems(n):
            d = {k: sem(f"{n}_{k}") for k in ("swrote", "sread", "scored", "expd", "pvd", "oevac", "zeroed", "recip")}
            d["loaded"] = [sem(f"{n}_loaded{j}") for j in range(2)]
            d["shift"] = [sem(f"{n}_shift{j}") for j in range(2)]
            return d

        a1 = {"s": attn_sems("a1"), "causal": False, "q": qk_hbm["q1"], "k": qk_hbm["k1"], "v": v_hbm["v1"]}
        a2 = {"s": attn_sems("a2"), "causal": True, "q": qk_hbm["q2"], "k": qk_hbm["k2"], "v": v_hbm["v2"]}
        done_s = sem("done_s")
        mo = sems("moe", ("gate_in", "iota", "logits", "score", "nhi", "nlo", "route", "ones", "w_hi", "w_lo", "sel", "gu", "silu", "h", "hi", "lo", "down", "acc"))
        mo["w_raw"] = [sem(f"moe_w_raw{j}") for j in range(2)]

        block = stack.enter_context(nc.Block())

        x_tiles = x.rearrange("b (t p) d -> p (b t) d", p=P)
        out_tiles = out.rearrange("b (t p) d -> p (b t) d", p=P)

        def bcast(v):
            return v.rearrange("(a n) -> a n", a=1).broadcast_to([P, D])

        def wait(eng, s, value):
            if value > 0:
                eng.wait_ge(s, value)

        def wait_sent(eng, n, batches):
            for m in range({"ctx": NC, "self": 2 * NC, "xq": NC}[n]):
                wait(eng, pj[n]["sent"][m], 16 * batches)
            if n != "xq":
                for k in range(TB):
                    wait(eng, pj[n]["vsent"][k], 16 * batches)

        def batch(t, b):
            return t[:, :, b * S:(b + 1) * S]

        def norm_power(pool, n, b):
            s = pj[n]
            pool.wait_ge(s["var"], b + 1)
            pool.tensor_tensor(rstd[:, b * TB:(b + 1) * TB], vare[:, b * TB:(b + 1) * TB], neghalf[:, 0:TB], ALU.pow).then_inc(s["rstd"], 1)

        @block.sync
        def _(sp):
            sp.dma_start(pos_i[:, :], pos.rearrange("b (t p) -> p (b t)", p=P), allow_slow_non_contiguous=True).then_inc(pos_in, 16)
            for t, w in ((wxk, xw_k), (wxv, xw_v)):
                sp.dma_start(t[:, :, :], w.rearrange("(c p) n -> p c n", p=P)).then_inc(ctx_w_in, 16)
            sp.dma_start(bxk_col[:, :], xb_k).then_inc(ctx_w_in, 16)
            sp.dma_start(bxv_row[:, :], bcast(xb_v)).then_inc(ctx_w_in, 16)
            sp.dma_start(ctx_sb[:, :, :], ctx_t.rearrange("(c p) n -> p c n", p=P)).then_inc(ctx_in, 16)
            sp.dma_start(X[:, :, :], x_tiles).then_inc(x_in, 16)
            sp.dma_start(rel_in[:, :], rel_pad).then_inc(rel_in_s, 16)
            sp.dma_start(wqkv[:, :, :], w_qkv.rearrange("(c p) n -> p c n", p=P)).then_inc(w_in, 16)
            for t, w in ((wout, w_out), (wxq, xw_q), (wxo, xw_o)):
                sp.dma_start(t[:, :, :], w.rearrange("(c p) n -> p c n", p=P)).then_inc(w_in, 16)
            sp.dma_start(wgate[:, :, :], w_gate).then_inc(w_in, 16)
            for t, w in ((bqk_col, b_qkv_col), (bxq_col, xb_q)):
                sp.dma_start(t[:, :], w).then_inc(w_in, 16)
            for t, w in ((bv_row, b_v), (bo_row, b_out), (bxo_row, xb_o)):
                sp.dma_start(t[:, :], bcast(w)).then_inc(w_in, 16)
            sp.wait_ge(rel_ready, 4)
            sp.dma_start(rel_hbm.ap(), rel_hl[:, :, :].bitcast(F32)).then_inc(rel_out, 16)

            def send_qk(n, names, b):
                s = pj[n]
                chunks = NC * len(names)
                for m in range(chunks):
                    sp.wait_ge(s["lo"], chunks * b + m + 1)
                    c = m % NC
                    dst = qk_hbm[names[m // NC]].ap()[:, c * P:(c + 1) * P, b * S:(b + 1) * S].rearrange("s p t -> p s t")
                    sp.dma_start(dst, hl[:, m, :, :].bitcast(F32)).then_inc(s["sent"][m], 16)

            def send_v(n, name, b):
                s = pj[n]
                for k in range(TB):
                    sp.wait_ge(s["vt"], 2 * b + k // 2 + 1)
                    sp.dma_start(v_hbm[name].ap()[b, :, :, k, :].rearrange("g p c -> p g c"),
                                 vt[:, k, :, :].rearrange("p (g h) e -> p g (h e)", g=G)).then_inc(s["vsent"][k], 16)

            def load_unit(a, u, j):
                s = a["s"]
                sp.wait_ge(s["scored"], SCORED_0 + 8 * (u - 1))
                g, b = u // B, u % B

                def part(hbm, half):
                    ap = hbm.ap()[half].rearrange("(g h d) t -> d g h t", g=G, h=HG)
                    return ap[:, bass.ds(g, 1), :, bass.ds(b * S, S)].rearrange("d o h t -> d (o h) t")

                for row, half in enumerate((0, 0, 1, 1)):
                    sp.dma_start(QU[j][DK * row:DK * row + DK, :, :].bitcast(F32), part(a["q"], half)).then_inc(s["loaded"][j], 16)
                for row, half in enumerate((0, 1, 0, 1)):
                    sp.dma_start(KU[j][DK * row:DK * row + DK, :, :].bitcast(F32), part(a["k"], half)).then_inc(s["loaded"][j], 16)
                sp.wait_ge(s["pvd"], SCORED_0 + 8 * (u - 1))
                v_src = a["v"].ap().rearrange("b g p k c -> p (b g) (k c)")[:, bass.ds(b * G + g, 1), :]
                sp.dma_start(VU[j][:, :, :, :].rearrange("p k h e -> p (k h e)"), v_src.rearrange("p o n -> p (o n)")).then_inc(s["loaded"][j], 16)

            def send_shift(a, u, j, first=False):
                s = a["s"]
                sp.wait_ge(s["sread"], USES - 1 if first else USES * u + USES - 2)
                sp.dma_start(QU[j][SHIFT_ROW:SHIFT_ROW + 1, :, :].rearrange("o h (q t) -> o (h q) t", q=TB).bitcast(F32),
                             MR[:, j, :].bitcast(F32)).then_inc(s["shift"][j], 16)

            def attention(a):
                load_unit(a, 0, 0)
                load_unit(a, 1, 1)
                send_shift(a, 0, 0, first=True)
                with sp.Fori(0, (U - 2) // 2) as i:
                    for j in range(2):
                        send_shift(a, 2 * i + (j + 1), (j + 1) % 2)
                        load_unit(a, 2 * i + (j + 2), j)
                send_shift(a, U - 1, (U - 1) % 2)

            for b in range(B):
                send_qk("ctx", ["k2"], b)
                send_v("ctx", "v2", b)
            for b in range(B):
                send_qk("self", ["q1", "k1"], b)
                send_v("self", "v1", b)
            wait_sent(sp, "self", B)
            sp.wait_ge(pj["self"]["v"], 2 * B)
            attention(a1)
            for b in range(B):
                send_qk("xq", ["q2"], b)
            wait_sent(sp, "ctx", B)
            wait_sent(sp, "xq", B)
            sp.wait_ge(pj["xq"]["qk"], NC * B)
            attention(a2)
            sp.wait_ge(a2["s"]["oevac"], U + 1)
            sp.dma_start(bias_e[:, :], e_bias.rearrange("(a n) -> a n", a=1).broadcast_to([P, E])).then_inc(mo["gate_in"], 16)
            w_src = w_exp.rearrange("e p n -> p e n")

            def load_expert(e, j, first=False):
                if not first:
                    sp.wait_ge(mo["w_hi"], e - 1)
                    sp.wait_ge(mo["w_lo"], e - 1)
                sp.dma_start(wraw[j][:, :], w_src[:, bass.ds(e, 1), :].rearrange("p o n -> p (o n)")).then_inc(mo["w_raw"][j], 16)

            for j in range(2):
                load_expert(j, j, first=True)
            with sp.Fori(1, EA // 2) as i:
                for j in range(2):
                    load_expert(2 * i + j, j)
            sp.wait_ge(mo["acc"], TB * B * EA)
            sp.dma_start(out_tiles, X[:, :, :]).then_inc(done_s, 16)
            sp.wait_ge(done_s, 16)

        @block.gpsimd
        def _(pool):
            for n, f in enumerate(INV_FREQ):
                pool.memset(freq[:, n:n + 1], float(f)).then_inc(const_m, 1)
            pool.memset(neghalf[:, :], -0.5).then_inc(const_m, 1)
            pool.iota(iota_i[:, :], pattern=[[1, E]], base=0, channel_multiplier=0).then_inc(mo["iota"], 1)
            pool.memset(ident[:, :], 0.0).then_inc(const_a, 1)
            pool.memset(mask_f[:, :, :], 0.0).then_inc(const_a, 1)
            pool.memset(flip[:, :], 0.0).then_inc(const_a, 1)
            pool.wait_ge(const_a, 3)
            pool.affine_select(out=flip[:, :], in_=flip[:, :], compare_op=ALU.not_equal, fill=1.0, base=-(P - 1),
                               pattern=[[1, P]], channel_multiplier=1).then_inc(const_b, 1)
            pool.affine_select(out=ident[:, :], in_=ident[:, :], compare_op=ALU.not_equal, fill=1.0, base=0,
                               pattern=[[-1, P]], channel_multiplier=1).then_inc(const_b, 1)
            pool.affine_select(out=mask_f[:, 0, :], in_=mask_f[:, 0, :], compare_op=ALU.is_ge, fill=-BIG, base=0,
                               pattern=[[-1, P]], channel_multiplier=1).then_inc(const_b, 1)
            pool.affine_select(out=mask_f[:, 1, :], in_=mask_f[:, 1, :], compare_op=ALU.is_ge, fill=-BIG, base=0,
                               pattern=[[1, P]], channel_multiplier=-1).then_inc(const_b, 1)
            pool.memset(vt[:, :, :, :], 1.0).then_inc(vt_init, 1)

            def rotate_cos(n, b):
                s = pj[n]
                for m in range(NC):
                    wait(pool, s["kf"], NC * b + m + 1)
                    wait(pool, s["rot"], NC * (b - 1) + m + 1)
                    pool.tensor_tensor(rot1[:, m, :], kf[:, m, :], cos_t[:, b * S:(b + 1) * S], ALU.mult).then_inc(s["rot1"], 1)

            pool.wait_ge(const_m, 1 + DK // 2)
            for b in range(B):
                rotate_cos("ctx", b)
                norm_power(pool, "self", b)

            def init_stacks(n):
                for j in range(2):
                    pool.memset(QU[j][64:P, :, :].bitcast(F32), 0.0).then_inc(stack_init, 1)
                    pool.memset(KU[j][64:P, :, :].bitcast(F32), 0.0).then_inc(stack_init, 1)
                pool.wait_ge(stack_init, 6 * n + 4)
                for j in range(2):
                    pool.memset(KU[j][SHIFT_ROW:SHIFT_ROW + 1, :, :].bitcast(F32), 1.0).then_inc(stack_init, 1)
                pool.wait_ge(stack_init, 6 * n + 6)

            def add_bias(n, row):
                pool.tensor_tensor(X[:, :, :], X[:, :, :], row[:, :].rearrange("p (o d) -> p o d", o=1).broadcast_to([P, NT, D]), ALU.add)\
                    .then_inc(out_s[n]["bias"], 1)

            def zero_shift(a, u, j):
                s = a["s"]
                pool.wait_ge(s["scored"], SCORED_0 + 8 * (u - 1))
                ones = KU[j][SHIFT_ROW:SHIFT_ROW + 1, :, :]
                pool.tensor_tensor(QU[j][SHIFT_ROW:SHIFT_ROW + 1, :, :], ones.bitcast(F32), ones.bitcast(F32), ALU.subtract).then_inc(s["zeroed"], 1)

            def load_toeplitz(g):
                src = bass.AP(rel_hbm, g * (HG * 2 * RPW), [[1, P], [RPW, 2 * HG], [1, TW]])
                dst = toep[:, bass.ds((g % 2) * (HG * 2 * TW), HG * 2 * TW)]
                pool.dma_start(dst.rearrange("p (r y) -> p r y", y=TW).bitcast(F32), src).then_inc(t_loaded, 16)

            pool.wait_ge(rel_out, 16)
            pool.wait_ge(trig_mm, 2 * NT)
            load_toeplitz(0)
            pool.wait_ge(pj["self"]["xn"], NT)
            pool.wait_ge(w_in, 16 * 10)
            wait_sent(pool, "self", B)
            pool.wait_ge(pj["self"]["v"], 2 * B)
            init_stacks(0)
            with pool.Fori(0, G - 1) as g:
                for r in range(B):
                    zero_shift(a1, g * B + r, r % 2)
                    if r == 1:
                        pool.wait_ge(t_loaded, 16 * g + 16)
                        load_toeplitz(g + 1)
            for r in range(B):
                zero_shift(a1, (G - 1) * B + r, r % 2)
            pool.wait_ge(a1["s"]["zeroed"], U)
            add_bias("o1", bo_row)
            for b in range(B):
                norm_power(pool, "xq", b)
                rotate_cos("xq", b)
            wait_sent(pool, "xq", B)
            pool.wait_ge(pj["xq"]["qk"], NC * B)
            init_stacks(1)
            with pool.Fori(0, U // 2) as i:
                for j in range(2):
                    zero_shift(a2, 2 * i + j, j)
            pool.wait_ge(a2["s"]["zeroed"], U)
            add_bias("o2", bxo_row)
            pool.wait_ge(a2["s"]["oevac"], U + 1)
            pool.memset(comb[:, 0:SHARED * NT], 1.0).then_inc(mo["ones"], 1)
            for b in range(B):
                norm_power(pool, "moe", b)
                for c in range(NC):
                    pool.wait_ge(mo["nhi"], NC * b + c + 1)
                    pool.tensor_tensor(nhl[:, c, 1, b * S:(b + 1) * S], nT3[:, c, :], nhl[:, c, 0, b * S:(b + 1) * S].bitcast(F32), ALU.subtract).then_inc(mo["nlo"], 1)

            def split_low(e, j):
                pool.wait_ge(mo["w_hi"], e + 1)
                pool.tensor_tensor(whl[j][:, 1, :], wraw[j][:, :], whl[j][:, 0, :].bitcast(F32), ALU.subtract).then_inc(mo["w_lo"], 1)

            with pool.Fori(0, EA // 2) as i:
                for j in range(2):
                    split_low(2 * i + j, j)

        @block.scalar
        def _(act):
            for a in (a1, a2):
                act.sem_inc(a["s"]["oevac"], 1)
            act.wait_ge(const_b, 4)
            act.activation(flip_r[:, :], flip[:, :], ACT.Copy).then_inc(const_m, 1)
            act.activation(ident_r[:, :], ident[:, :], ACT.Copy).then_inc(const_m, 1)
            act.activation(mask_r[:, :, :], mask_f[:, :, :], ACT.Copy).then_inc(const_m, 1)
            act.wait_ge(ang_s, 8)
            act.activation(ang[7][:, :, :], ang[4][:, :, :], ACT.Sin).then_inc(ang_act, 1)
            act.wait_ge(ang_s, 12)
            act.activation(ang[8][:, :, :], ang[6][:, :, :], ACT.Sin).then_inc(ang_act, 1)
            for t in range(NT):
                for w, dst in ((0, cos_t), (1, sin_t)):
                    n = 2 * t + w
                    act.wait_ge(trig_mm, n + 1)
                    act.activation(dst[:, t * P:(t + 1) * P], bank[:, n % 8, 0:P], ACT.Copy).then_inc(trig_out, 1)

            def kf_evac(n, b, col, first_bank):
                s = pj[n]
                for m in range(NC):
                    act.wait_ge(s["qk"], NC * b + m + 1)
                    wait(act, s["rot"], NC * (b - 1) + m + 1)
                    act.activation(kf[:, m, :], bank[:, first_bank + m, :], ACT.Identity, bias=col[:, m:m + 1]).then_inc(s["kf"], 1)

            def hi_rot(n, b):
                s = pj[n]
                for m in range(NC):
                    act.wait_ge(s["rot"], NC * b + m + 1)
                    wait(act, s["sent"][m], 16 * b)
                    act.activation(hl[:, m, 0, :], rot[:, m, :], ACT.Copy).then_inc(s["hi"], 1)

            act.wait_ge(ctx_w_in, 64)
            for b in range(B):
                kf_evac("ctx", b, bxk_col, 0)
                hi_rot("ctx", b)
            s = pj["self"]
            wait_sent(act, "ctx", B)
            act.wait_ge(w_in, 16 * 10)
            for b in range(B):
                for c in range(NC):
                    act.wait_ge(s["tr"], NC * b + c + 1)
                    act.activation(nT[:, c, :], bank[:, 4 + c, :], ACT.Copy).then_inc(s["trev"], 1)
                for m in range(4):
                    act.wait_ge(s["qk"], 4 * b + m + 1)
                    wait(act, s["sent"][m], 16 * b)
                    act.activation(hl[:, m, 0, :], bank[:, m, :], ACT.Identity, bias=bqk_col[:, m:m + 1]).then_inc(s["hi"], 1)

            def o_evac(a, u, j):
                s = a["s"]
                act.wait_ge(s["pvd"], SCORED_0 + 8 * u + 8)
                act.activation(OS[:, j, :], bank[:, 6 + j, :], ACT.Copy).then_inc(s["oevac"], 1)

            def unit(a, u, j, first=False):
                s = a["s"]
                for tau in range(2 * TB):
                    q0 = (tau // 2) * P if a["causal"] else 0
                    act.wait_ge(s["scored"], SCORED_0 + 8 * u + (tau + 1))
                    if not (first and tau < 4):
                        act.wait_ge(s["pvd"], SCORED_0 + 8 * u + (tau - 3))
                    act.activation(PT[:, tau % 4, :, q0:S], bank[:, 2 * (tau % 2):2 * (tau % 2) + 2, q0:S], ACT.Exp, scale=RAW_SCALE).then_inc(s["expd"], 1)
                    if tau == 0 and not first:
                        o_evac(a, u - 1, (j + 1) % 2)

            def attention(a):
                unit(a, 0, 0, first=True)
                with act.Fori(0, (U - 2) // 2) as i:
                    for j in range(2):
                        unit(a, 2 * i + (j + 1), (j + 1) % 2)
                unit(a, U - 1, 1)
                o_evac(a, U - 1, 1)

            def out_evac(n, b):
                s = out_s[n]
                for c in range(NC):
                    act.wait_ge(s["tr"], NC * b + c + 1)
                    wait(act, s["mm"], 2 * b)
                    act.activation(oT[:, c, :], bank[:, c, :], ACT.Copy).then_inc(s["trev"], 1)

            attention(a1)
            for b in range(B):
                out_evac("o1", b)
                s = pj["xq"]
                for c in range(NC):
                    act.wait_ge(s["tr"], NC * b + c + 1)
                    wait(act, s["qk"], NC * b)
                    act.activation(nT[:, c, :], bank[:, 4 + c, :], ACT.Copy).then_inc(s["trev"], 1)
                kf_evac("xq", b, bxq_col, 6)
                hi_rot("xq", b)
            attention(a2)
            s = pj["moe"]
            for b in range(B):
                out_evac("o2", b)
                for c in range(NC):
                    act.wait_ge(s["tr"], NC * b + c + 1)
                    wait(act, mo["logits"], b)
                    wait(act, mo["nlo"], NC * (b - 1) + c + 1)
                    act.activation(nT3[:, c, :], bank[:, 4 + c, :], ACT.Copy).then_inc(s["trev"], 1)
                for c in range(NC):
                    act.wait_ge(s["trev"], NC * b + c + 1)
                    act.activation(nhl[:, c, 0, b * S:(b + 1) * S], nT3[:, c, :], ACT.Copy).then_inc(mo["nhi"], 1)
                act.wait_ge(mo["logits"], b + 1)
                act.activation(score[:, b * TB:(b + 1) * TB, :], bank[:, 6 + b % 2, 0:P].rearrange("p (t e) -> p t e", e=E), ACT.Sigmoid).then_inc(mo["score"], 1)

            def split_high(e, j, k, first=False):
                act.wait_ge(mo["w_raw"][j], 16 * k + 16)
                if not first:
                    act.wait_ge(mo["down"], B * (e - 1))
                act.activation(whl[j][:, 0, :], wraw[j][:, :], ACT.Copy).then_inc(mo["w_hi"], 1)

            def expert_pair(i, first=False, last=False):
                for n in range(2 * B):
                    st, j = 2 * B * i + n, n % 2
                    young = first and n < 2
                    act.wait_ge(mo["gu"], st + 1)
                    if not young:
                        act.wait_ge(mo["h"], st - 1)
                    act.activation(sg[j][:, :], bank[:, j, :], ACT.Silu).then_inc(mo["silu"], 1)
                    act.wait_ge(mo["h"], st + 1)
                    if not young:
                        act.wait_ge(mo["down"], st - 1)
                    act.activation(hhl[j][:, 0, :], hid[j][:, :], ACT.Copy).then_inc(mo["hi"], 1)
                    if n == 1 and not first:
                        split_high(2 * i + 1, 1, i)
                    if n == B + 1 and not last:
                        split_high(2 * i + 2, 0, i + 1)

            split_high(0, 0, 0, first=True)
            split_high(1, 1, 0, first=True)
            expert_pair(0, first=True)
            with act.Fori(1, EA // 2 - 1) as i:
                expert_pair(i)
            expert_pair(EA // 2 - 1, last=True)

        @block.tensor
        def _(pe):
            for a in (a1, a2):
                pe.sem_inc(a["s"]["scored"], SCORED_0)
                pe.sem_inc(a["s"]["pvd"], SCORED_0)
            pe.wait_ge(const_b, 4)
            pe.wait_ge(trig_ready, 2)
            for t in range(NT):
                for w in range(2):
                    n = 2 * t + w
                    wait(pe, trig_out, n - 7)
                    pe.transpose(bank[:, n % 8, 0:P], trig8[:, w, t, :, :].rearrange("p r f -> p (r f)"), ident[:, :]).then_inc(trig_mm, 1)

            def feature_major(n, wt, col0, chunks, src, b, first_bank, freed):
                s = pj[n]
                for m in range(chunks):
                    wait(pe, freed, chunks * (b - 1) + m + 1)
                    for c in range(NC):
                        mm = pe.matmul(bank[:, first_bank + m, :], wt[:, c, col0 + m * P:col0 + (m + 1) * P], src[:, c, :], start=(c == 0), stop=(c == NC - 1))
                    mm.then_inc(s["qk"], 1)

            def token_major(done, wt, col0, src, b, first_bank, freed):
                for k in range(2):
                    wait(pe, freed, 2 * (b - 1) + k + 1)
                    for t in range(2):
                        tok = (2 * k + t) * P
                        for c in range(NC):
                            mm = pe.matmul(bank[:, first_bank + k, t * D:(t + 1) * D], src[:, c, tok:tok + P], wt[:, c, col0:col0 + D],
                                           start=(c == 0), stop=(c == NC - 1))
                    mm.then_inc(done, 1)

            def transposes(src, b, first_bank, done, ready, per_tile, freed):
                for c in range(NC):
                    wait(pe, freed, NC * (b - 1) + c + 1)
                    for t in range(TB):
                        if c == 0 and per_tile:
                            pe.wait_ge(ready, TB * b + t + 1)
                        tr = pe.transpose(bank[:, first_bank + c, t * P:(t + 1) * P], src[:, b * TB + t, c * P:(c + 1) * P], ident[:, :])
                    tr.then_inc(done, 1)

            pe.wait_ge(trig_out, 2 * NT)
            pe.wait_ge(ctx_in, 16)
            pe.wait_ge(ctx_w_in, 64)
            for b in range(B):
                feature_major("ctx", wxk, 0, NC, batch(ctx_sb, b), b, 0, pj["ctx"]["kf"])
                token_major(pj["ctx"]["v"], wxv, 0, batch(ctx_sb, b), b, 2, pj["ctx"]["vt"])
            s = pj["self"]
            pe.wait_ge(w_in, 16 * 10)
            for b in range(B):
                if b == 0:
                    pe.wait_ge(pj["ctx"]["kf"], NC * B)
                    pe.wait_ge(pj["ctx"]["vt"], 2 * B)
                transposes(XN, b, 4, s["tr"], s["xn"], True, s["trev"])
                pe.wait_ge(s["trev"], NC * b + 2)
                feature_major("self", wqkv, 0, 4, nT, b, 0, s["lo"])
                token_major(s["v"], wqkv, 2 * D, nT, b, 6, s["vt"])

            def score_use(a, u, n, first):
                s = a["s"]
                if first:
                    k = USES - 1 + n
                else:
                    k = USES * u + (USES - 2 + n)
                pe.wait_ge(s["sread"], k - 1)
                return bank[:, 4 + (((USES - 1) if first else 0) + n) % 2, :]

            def row_scores(a, dst, j, h, qb):
                keys = P * (qb + 1) if a["causal"] else S
                q = slice(qb * P, (qb + 1) * P)
                mm = pe.matmul(dst[:, 0:keys], QU[j][:, h, q], KU[j][:, h, 0:keys], start=True, stop=not a["causal"])
                if a["causal"]:
                    mm = pe.matmul(dst[:, q], ident_r[:, :], mask_r[:, 0, :], start=False, stop=True)
                mm.then_inc(a["s"]["swrote"], 1)

            def maxima_rows(a, dst, j):
                pe.transpose(dst[0:HG * TB, 0:P], M[:, j, :], ident[:, :]).then_inc(a["s"]["swrote"], 1)

            def outputs_token_major(a, u, dst, j):
                pe.wait_ge(a["s"]["oevac"], u + 2)
                for qb in range(TB):
                    tr = pe.transpose(dst[:, qb * P:(qb + 1) * P], OS[:, j, qb * P:(qb + 1) * P], ident[:, :])
                tr.then_inc(a["s"]["swrote"], 1)

            def key_scores(a, u, tau, j, first):
                s = a["s"]
                kb, half = tau // 2, tau % 2
                q0 = kb * P if a["causal"] else 0
                if not (first and tau < 2):
                    pe.wait_ge(s["expd"], 8 * u + tau - 1)
                for x in range(2):
                    h = 2 * half + x
                    dst = bank[:, 2 * (tau % 2) + x, :]
                    mm = pe.matmul(dst[:, q0:S], KU[j][:, h, kb * P:(kb + 1) * P], QU[j][:, h, q0:S], start=True, stop=False)
                    if a["causal"]:
                        mm = pe.matmul(dst[:, q0:q0 + P], ident_r[:, :], mask_r[:, 1, :], start=False, stop=True)
                    else:
                        for part in range(2):
                            row = (u // B) % 2 * (HG * 2 * TW) + ((2 * h + part) * TW + S - P - kb * P)
                            mm = pe.matmul(dst, flip_r[:, :], toep[:, bass.ds(row, S)], start=False, stop=(part == 1))
                mm.then_inc(s["scored"], 1)
                return mm

            def weigh(a, u, tau, j):
                s = a["s"]
                kb, half = tau // 2, tau % 2
                q0 = kb * P if a["causal"] else 0
                pe.wait_ge(s["expd"], 8 * u + (tau + 1))
                for x in range(2):
                    h = 2 * half + x
                    mm = pe.matmul(bank[32 * h:32 * h + 32, 6 + j, q0:S], VU[j][:, kb, h, :], PT[:, tau % 4, x, q0:S],
                                   start=(kb == 0), stop=(kb == TB - 1), tile_position=(0, 32 * h))
                mm.then_inc(s["pvd"], 1)

            SCORES_AT = {2: 3, 3: 3, 4: 4, 5: 3, 6: 3}

            def unit(a, u, k, j, first=False, last=False):
                s = a["s"]
                n = 0
                done = 0
                pe.wait_ge(s["shift"][j], 16 * k + 16)
                if not a["causal"]:
                    pe.wait_ge(t_loaded, 16 * (u // B) + 16)
                for tau in range(2 * TB):
                    mm = key_scores(a, u, tau, j, first)
                    if tau == 2 and not first:
                        dst = score_use(a, u, n, first)
                        outputs_token_major(a, u - 1, dst, (j + 1) % 2)
                        n += 1
                    if not last and tau in SCORES_AT:
                        jn = (j + 1) % 2
                        if done == 0:
                            pe.wait_ge(s["loaded"][jn], 16 * LOADS * ((k if j == 0 else k + 1) + 1))
                            pe.wait_ge(s["zeroed"], u + 2)
                        for _ in range(SCORES_AT[tau]):
                            row_scores(a, score_use(a, u, n, first), jn, done // TB, done % TB)
                            n += 1
                            done += 1
                    if tau == 7 and not last:
                        dst = score_use(a, u, n, first)
                        pe.wait_ge(s["sread"], (USES - 1 + n) if first else USES * u + (USES - 2 + n))
                        maxima_rows(a, dst, jn)
                        n += 1
                    if tau >= 1:
                        if tau == 1 and not first:
                            pe.wait_ge(s["oevac"], u)
                        weigh(a, u, tau - 1, j)
                weigh(a, u, 7, j)

            def attention(a):
                s = a["s"]
                pe.wait_ge(s["loaded"][0], 16 * LOADS)
                pe.wait_ge(s["zeroed"], 1)
                for n in range(HG * TB):
                    if n >= 2:
                        pe.wait_ge(s["sread"], n - 1)
                    row_scores(a, bank[:, 4 + n % 2, :], 0, n // TB, n % TB)
                pe.wait_ge(s["sread"], HG * TB)
                maxima_rows(a, bank[:, 4, :], 0)
                unit(a, 0, 0, 0, first=True)
                with pe.Fori(0, (U - 2) // 2) as i:
                    for j in range(2):
                        unit(a, 2 * i + (j + 1), i + j, (j + 1) % 2)
                unit(a, U - 1, U // 2 - 1, 1, last=True)
                n = USES * (U - 1) + USES - 2 + 1
                pe.wait_ge(s["sread"], n - 1)
                outputs_token_major(a, U - 1, bank[:, 5, :], 1)

            pe.wait_ge(s["lo"], 4 * B)
            pe.wait_ge(s["vt"], 2 * B)
            pe.wait_ge(const_m, 4 + DK // 2)
            attention(a1)
            s = pj["xq"]
            pe.wait_ge(a1["s"]["sread"], USES * U)
            for b in range(B):
                o = out_s["o1"]
                transposes(XN, b, 0, o["tr"], None, False, o["trev"])
                pe.wait_ge(o["trev"], NC * b + 2)
                token_major(o["mm"], wout, 0, oT, b, 2, o["add"])
                transposes(XN, b, 4, s["tr"], s["xn"], True, s["trev"])
                pe.wait_ge(s["trev"], NC * b + 2)
                feature_major("xq", wxq, 0, NC, nT, b, 6, s["kf"])
            pe.wait_ge(s["kf"], NC * B)
            attention(a2)
            pe.wait_ge(a2["s"]["sread"], USES * U)
            for b in range(B):
                o = out_s["o2"]
                transposes(XN, b, 0, o["tr"], None, False, o["trev"])
                pe.wait_ge(o["trev"], NC * b + 2)
                token_major(o["mm"], wxo, 0, oT, b, 2, o["add"])
                transposes(XN, b, 4, pj["moe"]["tr"], pj["moe"]["xn"], True, pj["moe"]["trev"])
                wait(pe, mo["score"], b - 1)
                for k in range(TB):
                    for c in range(NC):
                        pe.wait_ge(pj["moe"]["trev"], NC * b + c + 1)
                        mm = pe.matmul(bank[:, 6 + b % 2, k * E:(k + 1) * E], nT3[:, c, k * P:(k + 1) * P], wgate[:, c, :],
                                       start=(c == 0), stop=(c == NC - 1))
                mm.then_inc(mo["logits"], 1)

            PRODUCTS = ((0, 0), (0, 1), (1, 0))

            def gate_up(st, j, wj, b, first):
                if not first:
                    pe.wait_ge(mo["h"], st - 1)
                for half in range(2):
                    n = 0
                    for c in range(NC):
                        for x, y in PRODUCTS:
                            col = c * 2 * I + half * I
                            mm = pe.matmul(bank[:, 2 * half + j, :], whl[wj][:, x, col:col + I], nhl[:, c, y, b * S:(b + 1) * S],
                                           start=(n == 0), stop=(n == 3 * NC - 1))
                            n += 1
                mm.then_inc(mo["gu"], 1)

            def down(st, j, wj, first):
                pe.wait_ge(mo["hi"], st + 1)
                pe.wait_ge(mo["lo"], st + 1)
                if not first:
                    pe.wait_ge(mo["acc"], TB * (st - 1))
                for k in range(TB):
                    for n, (x, y) in enumerate(PRODUCTS):
                        mm = pe.matmul(bank[:, 4 + 2 * j + k // 2, (k % 2) * D:(k % 2 + 1) * D], hhl[j][:, x, k * P:(k + 1) * P],
                                       whl[wj][:, y, NC * 2 * I:WW], start=(n == 0), stop=(n == 2))
                mm.then_inc(mo["down"], 1)

            def expert_pair(i, first=False):
                for n in range(2 * B):
                    st, j = 2 * B * i + n, n % 2
                    if n % B == 0:
                        pe.wait_ge(mo["w_hi"], 2 * i + (n // B + 1))
                        pe.wait_ge(mo["w_lo"], 2 * i + (n // B + 1))
                    gate_up(st, j, n // B, n % B, first and n < 2)
                    if not (first and n == 0):
                        down(st - 1, (j + 1) % 2, ((n - 1) % (2 * B)) // B, first and n < 3)

            pe.wait_ge(mo["nlo"], NC * B)
            pe.wait_ge(mo["score"], B)
            pe.wait_ge(out_s["o2"]["add"], 2 * B)
            expert_pair(0, first=True)
            with pe.Fori(1, EA // 2) as i:
                expert_pair(i)
            down(B * EA - 1, 1, 1, False)

        @block.vector
        def _(dve):
            count = {"ang": 0}

            def step(ins):
                count["ang"] += 1
                ins.then_inc(ang_s, 1)
                dve.wait_ge(ang_s, count["ang"])

            dve.wait_ge(pos_in, 16)
            step(dve.tensor_copy(pos_f[:, :], pos_i[:, :]))
            dve.wait_ge(const_m, 1 + DK // 2)
            step(dve.tensor_tensor(ang[0][:, :, :], pos_f[:, :].rearrange("p (t o) -> p t o", o=1).broadcast_to([P, NT, DK // 2]),
                                   freq[:, :].rearrange("p (o f) -> p o f", o=1).broadcast_to([P, NT, DK // 2]), ALU.mult))
            step(dve.tensor_scalar(ang[1][:, :, :], ang[0][:, :, :], 1.0 / TWO_PI, ROUND, ALU.mult, ALU.add))
            step(dve.tensor_scalar(ang[2][:, :, :], ang[1][:, :, :], -ROUND, None, ALU.add))
            step(dve.scalar_tensor_tensor(out=ang[3][:, :, :], in0=ang[2][:, :, :], scalar=-C1, in1=ang[0][:, :, :], op0=ALU.mult, op1=ALU.add))
            step(dve.scalar_tensor_tensor(out=ang[5][:, :, :], in0=ang[2][:, :, :], scalar=-C2, in1=ang[3][:, :, :], op0=ALU.mult, op1=ALU.add))
            step(dve.scalar_tensor_tensor(out=ang[1][:, :, :], in0=ang[2][:, :, :], scalar=-C3, in1=ang[5][:, :, :], op0=ALU.mult, op1=ALU.add))
            step(dve.tensor_scalar(ang[4][:, :, :], ang[1][:, :, :], PI_SAFE, -PI_SAFE, ALU.min, ALU.max))
            step(dve.tensor_scalar(ang[3][:, :, :], ang[1][:, :, :], float(np.pi / 2), None, ALU.add))
            step(dve.tensor_scalar(ang[5][:, :, :], ang[3][:, :, :], float(np.pi), -TWO_PI, ALU.is_gt, ALU.mult))
            step(dve.tensor_tensor(ang[2][:, :, :], ang[3][:, :, :], ang[5][:, :, :], ALU.add))
            step(dve.tensor_scalar(ang[6][:, :, :], ang[2][:, :, :], PI_SAFE, -PI_SAFE, ALU.min, ALU.max))
            dve.wait_ge(ang_act, 2)
            step(dve.tensor_copy(trig[:, 0, :, :, :], ang[8][:, :, :].rearrange("p t (f o) -> p t f o", o=1).broadcast_to([P, NT, DK // 2, 2])))
            step(dve.tensor_scalar(trig[:, 1, :, :, 0], ang[7][:, :, :], -1.0, None, ALU.mult))
            step(dve.tensor_scalar(trig[:, 1, :, :, 1], ang[7][:, :, :], 1.0, None, ALU.mult))
            for w in range(2):
                dve.tensor_copy(trig8[:, w, :, :, :], trig[:, w, :, :, :].rearrange("p t (o f) e -> p t o (f e)", o=1).broadcast_to([P, NT, P // DK, DK]))\
                    .then_inc(trig_ready, 1)
            dve.wait_ge(rel_in_s, 16)
            dve.tensor_reduce(rel_max[:, :], rel_in[:, :], AX_X, ALU.max).then_inc(rel_ready, 1)
            dve.wait_ge(rel_ready, 1)
            dve.tensor_scalar(rel_s[:, :], rel_in[:, :], rel_max[:, 0:1], 1.0 / RAW_SCALE, ALU.subtract, ALU.mult).then_inc(rel_ready, 1)
            dve.wait_ge(rel_ready, 2)
            dve.tensor_copy(rel_hl[:, 0, :], rel_s[:, :]).then_inc(rel_ready, 1)
            dve.wait_ge(rel_ready, 3)
            dve.tensor_tensor(rel_hl[:, 1, :], rel_s[:, :], rel_hl[:, 0, :].bitcast(F32), ALU.subtract).then_inc(rel_ready, 1)

            def layer_norm(n, dst, b):
                s = pj[n]
                for k in range(TB):
                    t = TB * b + k
                    dve.bn_stats(stats[:, t, :], X[:, t, :]).then_inc(s["stat"], 1)
                for k in range(TB):
                    t = TB * b + k
                    dve.wait_ge(s["stat"], t + 1)
                    dve.bn_aggr(mv[:, t, :], stats[:, t, :]).then_inc(s["mv"], 1)
                tiles = slice(TB * b, TB * (b + 1))
                dve.wait_ge(s["mv"], TB * (b + 1))
                dve.tensor_scalar(vare[:, tiles], mv[:, tiles, 1], EPS, None, ALU.add).then_inc(s["var"], 1)

            def normalise(n, dst, b):
                s = pj[n]
                dve.wait_ge(s["rstd"], b + 1)
                for k in range(TB):
                    t = TB * b + k
                    dve.tensor_scalar(dst[:, t, :], X[:, t, :], mv[:, t, 0:1], rstd[:, t:t + 1], ALU.subtract, ALU.mult).then_inc(s["xn"], 1)

            def rotate(n, b):
                s = pj[n]
                for m in range(NC):
                    dve.wait_ge(s["kf"], NC * b + m + 1)
                    dve.stream_shuffle(swap[:, m, :], kf[:, m, :], [p ^ 1 for p in range(32)]).then_inc(s["swap"], 1)
                for m in range(NC):
                    dve.wait_ge(s["swap"], NC * b + m + 1)
                    dve.tensor_tensor(rot2[:, m, :], swap[:, m, :], sin_t[:, b * S:(b + 1) * S], ALU.mult).then_inc(s["rot2"], 1)
                for m in range(NC):
                    dve.wait_ge(s["rot2"], NC * b + m + 1)
                    dve.wait_ge(s["rot1"], NC * b + m + 1)
                    dve.tensor_tensor(rot[:, m, :], rot1[:, m, :], rot2[:, m, :], ALU.add).then_inc(s["rot"], 1)

            def low_rot(n, b):
                s = pj[n]
                for m in range(NC):
                    dve.wait_ge(s["hi"], NC * b + m + 1)
                    dve.tensor_tensor(hl[:, m, 1, :], rot[:, m, :], hl[:, m, 0, :].bitcast(F32), ALU.subtract).then_inc(s["lo"], 1)

            def values(n, row, b, first_bank):
                s = pj[n]
                for k in range(2):
                    dve.wait_ge(s["v"], 2 * b + k + 1)
                    wait(dve, s["vsent"][2 * k], 16 * b)
                    wait(dve, s["vsent"][2 * k + 1], 16 * b)
                    dve.tensor_tensor(vt[:, 2 * k:2 * k + 2, :, 0:DK], bank[:, first_bank + k, :].rearrange("p (t h d) -> p t h d", t=2, h=H),
                                      row[:, :].rearrange("p (o h d) -> p o h d", o=1, h=H).broadcast_to([P, 2, H, DK]), ALU.add).then_inc(s["vt"], 1)

            dve.wait_ge(trig_out, 2 * NT)
            dve.wait_ge(vt_init, 1)
            dve.wait_ge(ctx_w_in, 64)
            for b in range(B):
                rotate("ctx", b)
                if b == 0:
                    dve.wait_ge(x_in, 16)
                layer_norm("self", XN, b)
                values("ctx", bxv_row, b, 2)
                low_rot("ctx", b)
                normalise("self", XN, b)
            dve.wait_ge(w_in, 16 * 10)
            s = pj["self"]
            for b in range(B):
                for m in range(4):
                    dve.wait_ge(s["hi"], 4 * b + m + 1)
                    dve.scalar_tensor_tensor(out=hl[:, m, 1, :], in0=bank[:, m, :], scalar=bqk_col[:, m:m + 1], in1=hl[:, m, 0, :].bitcast(F32),
                                             op0=ALU.add, op1=ALU.subtract).then_inc(s["lo"], 1)
                values("self", bv_row, b, 6)

            def outputs(a, u, n, slot_bank, j, dst, first):
                s = a["s"]
                dve.wait_ge(s["swrote"], n)
                src = bank[:, slot_bank, :].rearrange("p (q h e) -> p q h e", q=TB, h=HG)
                dve.reciprocal(R[:, j, :].rearrange("p (q h) -> p q h", q=TB), src[:, :, :, DK]).then_inc(s["recip"], 1)
                dve.wait_ge(s["recip"], u + 1)
                g, b = u // B, u % B
                to = unit_columns(dst, b * (TB * D) + g * GW)
                dve.tensor_tensor(to, src[:, :, :, 0:DK],
                                  R[:, j, :].rearrange("p (q h o) -> p q h o", q=TB, o=1).broadcast_to([P, TB, HG, DK]), ALU.mult).then_inc(s["sread"], 1)

            def unit_columns(dst, col):
                full = dst[:, 0:TB, 0:GW].rearrange("p t (h d) -> p t h d", h=HG)
                return bass.AP(full.tensor, full.offset + col, full.ap)

            def row_max(a, n, slot_bank, j, c):
                s = a["s"]
                keys = P * (c % TB + 1) if a["causal"] else S
                dve.wait_ge(s["swrote"], n)
                dve.tensor_reduce(M[:, j, c:c + 1], bank[:, slot_bank, 0:keys], AX_X, ALU.max).then_inc(s["sread"], 1)

            def shift_rows(a, n, slot_bank, j):
                dve.wait_ge(a["s"]["swrote"], n)
                dve.tensor_scalar(MR[:, j, :], bank[0:HG * TB, slot_bank, 0:P], -1.0, None, ALU.mult).then_inc(a["s"]["sread"], 1)

            def unit(a, u, j, dst, first=False, last=False):
                base = (USES - 1) if first else USES * u + (USES - 2)
                slot = 1 if first else 0
                n = 0
                if not first:
                    outputs(a, u - 1, base + 1, 4 + slot, (j + 1) % 2, dst, first)
                    n = 1
                if not last:
                    for c in range(HG * TB):
                        row_max(a, base + (n + 1), 4 + (slot + n) % 2, (j + 1) % 2, c)
                        n += 1
                    shift_rows(a, base + (n + 1), 4 + (slot + n) % 2, (j + 1) % 2)

            def attention(a, dst):
                for c in range(HG * TB):
                    row_max(a, c + 1, 4 + c % 2, 0, c)
                shift_rows(a, HG * TB + 1, 4, 0)
                unit(a, 0, 0, dst, first=True)
                with dve.Fori(0, (U - 2) // 2) as i:
                    for j in range(2):
                        unit(a, 2 * i + (j + 1), (j + 1) % 2, dst)
                unit(a, U - 1, 1, dst, last=True)
                outputs(a, U - 1, USES * (U - 1) + USES - 2 + 2, 5, 1, dst, False)

            def residual(n, b):
                s = out_s[n]
                if b == 0:
                    dve.wait_ge(s["bias"], 1)
                for k in range(2):
                    t = TB * b + 2 * k
                    dve.wait_ge(s["mm"], 2 * b + k + 1)
                    dve.tensor_tensor(X[:, t:t + 2, :], X[:, t:t + 2, :], bank[:, 2 + k, :].rearrange("p (t d) -> p t d", t=2), ALU.add).then_inc(s["add"], 1)

            attention(a1, XN)
            for b in range(B):
                residual("o1", b)
                dve.wait_ge(out_s["o1"]["add"], 2 * b + 2)
                layer_norm("xq", XN, b)
                normalise("xq", XN, b)
                rotate("xq", b)
                low_rot("xq", b)
            attention(a2, XN)
            for b in range(B):
                residual("o2", b)
                dve.wait_ge(out_s["o2"]["add"], 2 * b + 2)
                layer_norm("moe", XN, b)
                normalise("moe", XN, b)

            steps = {"n": 0}

            def route(ins):
                steps["n"] += 1
                ins.then_inc(mo["route"], 1)
                dve.wait_ge(mo["route"], steps["n"])

            def tiles_route(make):
                for t in range(NT):
                    steps["n"] += 1
                    make(t).then_inc(mo["route"], 1)
                dve.wait_ge(mo["route"], steps["n"])

            def one_hot(sel, idx, k, n):
                return dve.tensor_tensor(sel[:, :, :, :], iota_e[:, 0:n].rearrange("p (a b n) -> p a b n", a=1, b=1).broadcast_to([P, NT, k, n]),
                                         idx[:, :, 0:k].rearrange("p t (k o) -> p t k o", o=1).broadcast_to([P, NT, k, n]), ALU.is_equal)

            dve.wait_ge(mo["iota"], 1)
            dve.wait_ge(a2["s"]["oevac"], U + 1)
            route(dve.tensor_copy(iota_e[:, :], iota_i[:, :]))
            dve.wait_ge(mo["score"], B)
            dve.wait_ge(mo["gate_in"], 16)
            route(dve.tensor_tensor(sfc[:, :, :], score[:, :, :], bias_e[:, :].rearrange("p (o e) -> p o e", o=1).broadcast_to([P, NT, E]), ALU.add))
            route(dve.tensor_reduce(gmax[:, :, :], sfc[:, :, :].rearrange("p t (g e) -> p t g e", g=NGROUP), AX_X, ALU.max))
            tiles_route(lambda t: dve.max(gtop[:, t, :], gmax[:, t, :]))
            tiles_route(lambda t: dve.max_index(gidx[:, t, :], gtop[:, t, :], gmax[:, t, :]))
            route(dve.tensor_copy(gidx_f[:, :, :], gidx[:, :, :]))
            route(one_hot(gsel, gidx_f, TOPG, NGROUP))
            route(dve.tensor_reduce(gmask[:, :, :], gsel[:, :, :, :].rearrange("p t k g -> p t g k"), AX_X, ALU.add))
            route(dve.tensor_tensor(masked[:, :, :].rearrange("p t (g e) -> p t g e", g=NGROUP), sfc[:, :, :].rearrange("p t (g e) -> p t g e", g=NGROUP),
                                    gmask[:, :, :].rearrange("p t (g o) -> p t g o", o=1).broadcast_to([P, NT, NGROUP, GE]), ALU.mult))
            tiles_route(lambda t: dve.max(etop[:, t, :], masked[:, t, :]))
            tiles_route(lambda t: dve.max_index(eidx[:, t, :], etop[:, t, :], masked[:, t, :]))
            route(dve.tensor_copy(eidx_f[:, :, :], eidx[:, :, :]))
            route(one_hot(esel, eidx_f, TOPK, E))
            route(dve.tensor_reduce(chosen[:, :, :], esel[:, :, :, :].rearrange("p t k e -> p t e k"), AX_X, ALU.add))
            route(dve.tensor_tensor(picked[:, :, :], chosen[:, :, :], score[:, :, :], ALU.mult))
            route(dve.tensor_reduce(tws[:, :], picked[:, :, :], AX_X, ALU.add))
            route(dve.tensor_scalar(twe[:, :], tws[:, :], 1e-20, None, ALU.add))
            route(dve.reciprocal(twr[:, :], twe[:, :]))
            route(dve.scalar_tensor_tensor(out=comb[:, SHARED * NT:].rearrange("p (e t) -> p t e", t=NT), in0=picked[:, :, :], scalar=ROUTED_SCALE,
                                           in1=twr[:, :].rearrange("p (t o) -> p t o", o=1).broadcast_to([P, NT, E]), op0=ALU.mult, op1=ALU.mult))
            dve.wait_ge(mo["ones"], 1)

            def accumulate(st, j, ej, b, first):
                dve.wait_ge(mo["down"], st + 1)
                if not first:
                    dve.wait_ge(mo["acc"], TB * (st - (B - 1)))
                for k in range(TB):
                    t = TB * b + k
                    dve.scalar_tensor_tensor(out=X[:, t, :], in0=bank[:, 4 + 2 * j + k // 2, (k % 2) * D:(k % 2 + 1) * D], scalar=csel[ej][:, t:t + 1],
                                             in1=X[:, t, :], op0=ALU.mult, op1=ALU.add).then_inc(mo["acc"], 1)

            def expert_pair(i, first=False):
                for n in range(2 * B):
                    st, j = 2 * B * i + n, n % 2
                    dve.wait_ge(mo["silu"], st + 1)
                    if not (first and n < 2):
                        dve.wait_ge(mo["hi"], st - 1)
                    dve.tensor_tensor(hid[j][:, :], sg[j][:, :], bank[:, 2 + j, :], ALU.mult).then_inc(mo["h"], 1)
                    if not (first and n == 0):
                        accumulate(st - 1, (j + 1) % 2, ((n - 1) % (2 * B)) // B, (n - 1) % B, first and n <= B)
                    if n % B == 0:
                        e = 2 * i + n // B
                        if not first:
                            dve.wait_ge(mo["acc"], TB * B * (e - 1))
                        dve.tensor_copy(csel[n // B][:, :], comb[:, bass.ds(e * NT, NT)]).then_inc(mo["sel"], 1)
                        dve.wait_ge(mo["sel"], e + 1)
                    dve.wait_ge(mo["hi"], st + 1)
                    dve.tensor_tensor(hhl[j][:, 1, :], hid[j][:, :], hhl[j][:, 0, :].bitcast(F32), ALU.subtract).then_inc(mo["lo"], 1)

            expert_pair(0, first=True)
            with dve.Fori(1, EA // 2) as i:
                expert_pair(i)
            accumulate(B * EA - 1, 1, 1, B - 1, False)


def kernel(**inputs):
    import numpy as _np
    import concourse.bacc as _bacc
    from concourse import mybir as _mybir
    from concourse.bass_utils import run_bass_kernel_spmd as _run

    def f(name):
        return _np.asarray(inputs[name])

    gate_up = _np.concatenate([_np.stack([f("L0_ffn_shared_gate_w"), f("L0_ffn_shared_up_w")]).reshape(2, SHARED, I, NC, P).transpose(1, 0, 2, 3, 4),
                               f("L0_ffn_experts_gate_up").reshape(E, 2, I, NC, P)])
    down = _np.concatenate([f("L0_ffn_shared_down_w").reshape(D, SHARED, I).transpose(1, 0, 2), f("L0_ffn_experts_down")])
    laid = {
        "x": f("x"),
        "ctx_t": f("ctx_1024").reshape(B * S, D).T,
        "pos": f("pos_BxS2"),
        "w_qkv": f("L0_attn_W_qkv"),
        "b_qkv_col": f("L0_attn_b_qkv")[0:2 * D].reshape(2 * NC, P).T,
        "b_v": f("L0_attn_b_qkv")[2 * D:],
        "w_out": f("L0_attn_W_out"),
        "b_out": f("L0_attn_b_out"),
        "rel_pad": _np.pad(f("L0_attn_rel_bias").T, ((0, 0), (MAX_REL - 1, RPW - (2 * MAX_REL + 1) - (MAX_REL - 1))), mode="edge"),
        "xw_q": f("L0_xattn_w_q"), "xb_q": f("L0_xattn_b_q").reshape(NC, P).T,
        "xw_k": f("L0_xattn_w_k"), "xb_k": f("L0_xattn_b_k").reshape(NC, P).T,
        "xw_v": f("L0_xattn_w_v"), "xb_v": f("L0_xattn_b_v"),
        "xw_o": f("L0_xattn_w_o"), "xb_o": f("L0_xattn_b_o"),
        "w_gate": f("L0_ffn_gate_weight").reshape(E, NC, P).transpose(2, 1, 0),
        "e_bias": f("L0_ffn_e_score_correction_bias"),
        "w_exp": _np.concatenate([gate_up.transpose(0, 4, 3, 1, 2).reshape(EA, P, NC * 2 * I), down.transpose(0, 2, 1)], axis=2),
    }
    nc = _bacc.Bacc("TRN2", target_bir_lowering=False, num_devices=1)
    arrays, args = {}, []
    for name, a in laid.items():
        a = _np.ascontiguousarray(a)
        arrays[f"in_{name}"] = a
        args.append(nc.dram_tensor(f"in_{name}", a.shape, _mybir.dt.from_np(a.dtype), kind="ExternalInput").ap())
    args.append(nc.dram_tensor("out_x", (B, S, D), _mybir.dt.float32, kind="ExternalOutput").ap())
    program(nc, *args)
    r = _run(nc, [arrays], core_ids=[0])
    return r.results[0]["out_x"]
```

```python
from contextlib import ExitStack

import numpy as np

import concourse.bass as bass
from concourse import mybir

F32 = mybir.dt.float32
F32R = mybir.dt.float32r
I32 = mybir.dt.int32
U32 = mybir.dt.uint32
ALU = mybir.AluOpType
ACT = mybir.ActivationFunctionType
AX_X = mybir.AxisListType.X

P = 128
B, S, D = 4, 512, 256
H, DK = 16, 16
NC = D // P
TB = S // P
NT = B * TB
HG = 4
G = H // HG
GW = HG * DK
U = G * B
MAX_REL = 256
TW = S - P + S
RPW = 1024
RAW_SCALE = float(DK) ** -0.5
EPS = 1e-5
BIG = 1e30
USES = HG * TB + 2
RING = 3
LOOPS = (U - 2) // RING
LOADS = 9
TAUS = 2 * TB
SHIFT_ROW = 64
THETA = 10000.0
INV_FREQ = (np.float32(THETA) ** (-(np.arange(DK // 2, dtype=np.float32) * np.float32(2.0)) / np.float32(DK))).astype(np.float32)
TWO_PI = 2.0 * np.pi
C1 = 6.28125
C2 = float(np.float32(TWO_PI - C1))
C3 = float(np.float32(TWO_PI - C1 - float(np.float32(TWO_PI - C1))))
ROUND = 1.5 * 2.0 ** 23
PI_SAFE = 3.1415925


E, TOPK, NGROUP, TOPG = 32, 6, 8, 4
GE = E // NGROUP
I = 128
SHARED = 2
EA = SHARED + E
WW = NC * 2 * I + D
ROUTED_SCALE = 2.5


def program(nc, x, ctx_t, pos, w_qkv, b_qkv_col, b_v, w_out, b_out, rel_pad, xw_q, xb_q, xw_k, xb_k, xw_v, xb_v, xw_o, xb_o, w_gate, e_bias, w_exp, out):
    with ExitStack() as stack:
        def sb(name, shape, dt=F32):
            return stack.enter_context(nc.sbuf_tensor(name, shape, dt))

        KB = 1024
        ARENA_AT = -(-nc.sbuf_base // KB) * KB
        stack.enter_context(nc.sbuf_tensor("arena", [P, 176 * KB + ARENA_AT - nc.sbuf_base], mybir.dt.uint8))

        def at(name, shape, kb, dt=F32):
            return nc.alloc_sbuf_tensor_at(name, shape, dt, offset=ARENA_AT + int(kb * KB))

        def sem(name):
            return stack.enter_context(nc.semaphore(name))

        def dram(name, shape):
            return nc.dram_tensor(name, shape, F32, kind="Internal")

        qk_hbm = {n: dram(f"{n}_hbm", (2, D, B * S)) for n in ("q1", "k1", "q2", "k2")}
        v_hbm = {n: dram(f"{n}_hbm", (B, G, P, TB, HG * 32)) for n in ("v1", "v2")}
        rel_hbm = dram("rel_hbm", (H, 2, RPW))

        bank = stack.enter_context(nc.psum_tensor("bank", [P, 8, 512], F32))

        X = at("X", [P, NT, D], 0)
        XN = at("XN", [P, NT, D], 16)
        ctx_sb = at("ctx_sb", [P, NC, B * S], 160)
        wqkv = sb("wqkv", [P, NC, 3 * D])
        wout = sb("wout", [P, NC, D])
        wxq = sb("wxq", [P, NC, D])
        wxk = sb("wxk", [P, NC, D])
        wxv = sb("wxv", [P, NC, D])
        wxo = sb("wxo", [P, NC, D])
        bqk_col = sb("bqk_col", [P, 4])
        bxq_col = sb("bxq_col", [P, NC])
        bxk_col = sb("bxk_col", [P, NC])
        bv_row = sb("bv_row", [P, D])
        bo_row = sb("bo_row", [P, D])
        bxv_row = sb("bxv_row", [P, D])
        bxo_row = sb("bxo_row", [P, D])
        ident = sb("ident", [P, P])
        flip = sb("flip", [P, P])
        ident_r = sb("ident_r", [P, P], F32R)
        flip_r = sb("flip_r", [P, P], F32R)
        mask_f = sb("mask_f", [P, 2, P])
        mask_r = sb("mask_r", [P, 2, P], F32R)
        pos_i = sb("pos_i", [P, NT], I32)
        pos_f = sb("pos_f", [P, NT])
        freq = sb("freq", [P, DK // 2])
        ang = [at(f"ang{n}", [P, NT, DK // 2], 152 + n / 2) for n in range(9)]
        trig = at("trig", [P, 2, NT, DK // 2, 2], 157)
        trig8 = at("trig8", [P, 2, NT, P // DK, DK], 120)
        cos_t = at("cos_t", [P, B * S], 32)
        sin_t = at("sin_t", [P, B * S], 40)
        stats = sb("stats", [P, NT, 6])
        mv = sb("mv", [P, NT, 2])
        vare = sb("vare", [P, NT])
        neghalf = sb("neghalf", [P, NT])
        rstd = sb("rstd", [P, NT])
        nT = at("nT", [P, NC, S], 112)
        oT = at("oT", [P, NC, S], 116)
        kf = at("kf", [P, NC, S], 48)
        swap = at("swap", [P, NC, S], 52)
        rot1 = at("rot1", [P, NC, S], 56)
        rot2 = at("rot2", [P, NC, S], 60)
        hl = at("hl", [P, 4, 2, S], 88, F32R)
        vt = at("vt", [P, TB, H, 32], 104)
        rel_in = at("rel_in", [H, RPW], 136)
        rel_max = sb("rel_max", [H, 1])
        rel_s = at("rel_s", [H, RPW], 140)
        rel_hl = at("rel_hl", [H, 2, RPW], 144, F32R)
        QU = [at(f"QU{j}", [P, HG, S], (66, 88, 104)[j], F32R) for j in range(RING)]
        KU = [at(f"KU{j}", [P, HG, S], (74, 96, 112)[j], F32R) for j in range(RING)]
        VU = [at(f"VU{j}", [P, TB, HG, 32], 82 + 2 * j) for j in range(RING)]
        toep = at("toep", [P, 2 * HG * 2 * TW], 120, F32R)
        PT = at("PT", [P, 4, 2, S], 48)
        OS = at("OS", [P, S], 64)
        M = sb("M", [P, 2, HG * TB])
        MR = sb("MR", [HG * TB, 2, P], F32R)
        R = sb("R", [P, TB * HG])
        wgate = sb("wgate", [P, NC, E])
        iota_i = sb("iota_i", [P, E], I32)
        nT3 = at("nT3", [P, NC, S], 32)
        nhl = at("nhl", [P, NC, 2, B * S], 140, F32R)
        bias_e = at("bias_e", [P, E], 36)
        iota_e = at("iota_e", [P, E], 36.5)
        score = at("score", [P, NT, E], 37)
        sfc = at("sfc", [P, NT, E], 39)
        masked = at("masked", [P, NT, E], 41)
        gmax = at("gmax", [P, NT, NGROUP], 43)
        gtop = at("gtop", [P, NT, 8], 43.5)
        gidx = at("gidx", [P, NT, 8], 44, U32)
        gidx_f = at("gidx_f", [P, NT, 8], 44.5)
        gmask = at("gmask", [P, NT, NGROUP], 45)
        etop = at("etop", [P, NT, 8], 45.5)
        eidx = at("eidx", [P, NT, 8], 46, U32)
        eidx_f = at("eidx_f", [P, NT, 8], 46.5)
        tws = at("tws", [P, NT], 47)
        twe = at("twe", [P, NT], 47.125)
        twr = at("twr", [P, NT], 47.25)
        gsel = at("gsel", [P, NT, TOPG, NGROUP], 48)
        esel = at("esel", [P, NT, TOPK, E], 50)
        chosen = at("chosen", [P, NT, E], 62)
        picked = at("picked", [P, NT, E], 64)
        comb = at("comb", [P, EA * NT], 100)
        csel = [at(f"csel{j}", [P, NT], 102.5 + j / 4) for j in range(2)]
        wraw = [at(f"wraw{j}", [P, WW], 104 + 3 * j) for j in range(2)]
        whl = [at(f"whl{j}", [P, 2, WW], 110 + 6 * j, F32R) for j in range(2)]
        sg = [at(f"sg{j}", [P, S], 122 + 2 * j) for j in range(2)]
        hid = [at(f"hid{j}", [P, S], 126 + 2 * j) for j in range(2)]
        hhl = [at(f"hhl{j}", [P, 2, S], 130 + 4 * j, F32R) for j in range(2)]

        x_in, pos_in, rel_in_s = sem("x_in"), sem("pos_in"), sem("rel_in_s")
        w_in, ctx_in, ctx_w_in = sem("w_in"), sem("ctx_in"), sem("ctx_w_in")
        const_a, const_b, const_m = sem("const_a"), sem("const_b"), sem("const_m")
        ang_s, ang_act, trig_ready, trig_mm, trig_out = sem("ang_s"), sem("ang_act"), sem("trig_ready"), sem("trig_mm"), sem("trig_out")
        stack_zero, stack_init = sem("stack_zero"), sem("stack_init")
        rel_ready, rel_out, t_loaded = sem("rel_ready"), sem("rel_out"), sem("t_loaded")
        vt_init = sem("vt_init")

        NORM = ("stat", "mv", "var", "rstd", "xn", "tr", "trev")
        ROPE = ("kf", "swap", "rot1", "rot2", "rot")

        def sems(n, kinds):
            return {k: sem(f"{n}_{k}") for k in kinds}

        def sent(n, chunks, tiles=0):
            return {"sent": [sem(f"{n}_sent{m}") for m in range(chunks)], "vsent": [sem(f"{n}_vsent{k}") for k in range(tiles)]}

        pj = {
            "ctx": sent("ctx", NC, TB) | sems("ctx", ROPE + ("qk", "hi", "lo", "v", "vt")),
            "self": sent("self", 2 * NC, TB) | sems("self", NORM + ("qk", "hi", "lo", "v", "vt")),
            "xq": sent("xq", NC) | sems("xq", NORM + ROPE + ("qk", "hi", "lo")),
            "moe": sems("moe", NORM),
        }
        out_s = {n: sems(n, ("tr", "trev", "mm", "add", "bias")) for n in ("o1", "o2")}

        def attn_sems(n):
            d = {k: sem(f"{n}_{k}") for k in ("swrote", "sread", "scored", "expd", "pvd", "oevac", "zeroed", "recip")}
            d["loaded"] = [sem(f"{n}_loaded{j}") for j in range(RING)]
            d["shift"] = [sem(f"{n}_shift{j}") for j in range(RING)]
            return d

        USES_SELF = ("rr", "orr", "rrr", "rrr", "rrr", "rrr", "m", "")
        USES_CAUSAL = ("rrr", "orrr", "rrrr", "rrr", "rrr", "m", "", "")

        a1 = {"s": attn_sems("a1"), "causal": False, "uses": USES_SELF, "out_use": "".join(USES_SELF).index("o"), "q": qk_hbm["q1"], "k": qk_hbm["k1"], "v": v_hbm["v1"]}
        a2 = {"s": attn_sems("a2"), "causal": True, "uses": USES_CAUSAL, "out_use": "".join(USES_CAUSAL).index("o"), "q": qk_hbm["q2"], "k": qk_hbm["k2"], "v": v_hbm["v2"]}
        done_s = sem("done_s")
        mo = sems("moe", ("gate_in", "iota", "logits", "score", "nhi", "nlo", "route", "ones", "w_hi", "w_lo", "sel", "gu", "silu", "h", "hi", "lo", "down", "acc"))
        mo["w_raw"] = [sem(f"moe_w_raw{j}") for j in range(2)]

        block = stack.enter_context(nc.Block())

        x_tiles = x.rearrange("b (t p) d -> p (b t) d", p=P)
        out_tiles = out.rearrange("b (t p) d -> p (b t) d", p=P)

        def bcast(v):
            return v.rearrange("(a n) -> a n", a=1).broadcast_to([P, D])

        def wait(eng, s, value):
            if value > 0:
                eng.wait_ge(s, value)

        def wait_sent(eng, n, batches):
            for m in range({"ctx": NC, "self": 2 * NC, "xq": NC}[n]):
                wait(eng, pj[n]["sent"][m], 16 * batches)
            if n != "xq":
                for k in range(TB):
                    wait(eng, pj[n]["vsent"][k], 16 * batches)

        def batch(t, b):
            return t[:, :, b * S:(b + 1) * S]

        def first_use(u):
            return USES - 1 if isinstance(u, int) and u == 0 else USES * u + (USES - 2)

        def slot(n):
            return 4 + n % RING

        def slot_of(u, n):
            return slot(USES - 1 + n if isinstance(u, int) and u == 0 else USES - 2 + n)

        def units(eng, body):
            body(0, 0)
            with eng.Fori(0, LOOPS) as i:
                for r in range(1, RING + 1):
                    body(RING * i + r, r % RING)
            for u in range(RING * LOOPS + 1, U):
                body(u, u % RING)

        def norm_power(pool, n, b):
            s = pj[n]
            pool.wait_ge(s["var"], b + 1)
            pool.tensor_tensor(rstd[:, b * TB:(b + 1) * TB], vare[:, b * TB:(b + 1) * TB], neghalf[:, 0:TB], ALU.pow).then_inc(s["rstd"], 1)

        @block.sync
        def _(sp):
            sp.dma_start(pos_i[:, :], pos.rearrange("b (t p) -> p (b t)", p=P), allow_slow_non_contiguous=True).then_inc(pos_in, 16)
            for t, w in ((wxk, xw_k), (wxv, xw_v)):
                sp.dma_start(t[:, :, :], w.rearrange("(c p) n -> p c n", p=P)).then_inc(ctx_w_in, 16)
            sp.dma_start(bxk_col[:, :], xb_k).then_inc(ctx_w_in, 16)
            sp.dma_start(bxv_row[:, :], bcast(xb_v)).then_inc(ctx_w_in, 16)
            sp.dma_start(ctx_sb[:, :, :], ctx_t.rearrange("(c p) n -> p c n", p=P)).then_inc(ctx_in, 16)
            sp.dma_start(X[:, :, :], x_tiles).then_inc(x_in, 16)
            sp.dma_start(rel_in[:, :], rel_pad).then_inc(rel_in_s, 16)
            sp.dma_start(wqkv[:, :, :], w_qkv.rearrange("(c p) n -> p c n", p=P)).then_inc(w_in, 16)
            for t, w in ((wout, w_out), (wxq, xw_q), (wxo, xw_o)):
                sp.dma_start(t[:, :, :], w.rearrange("(c p) n -> p c n", p=P)).then_inc(w_in, 16)
            sp.dma_start(wgate[:, :, :], w_gate).then_inc(w_in, 16)
            for t, w in ((bqk_col, b_qkv_col), (bxq_col, xb_q)):
                sp.dma_start(t[:, :], w).then_inc(w_in, 16)
            for t, w in ((bv_row, b_v), (bo_row, b_out), (bxo_row, xb_o)):
                sp.dma_start(t[:, :], bcast(w)).then_inc(w_in, 16)
            sp.wait_ge(rel_ready, 4)
            sp.dma_start(rel_hbm.ap(), rel_hl[:, :, :].bitcast(F32)).then_inc(rel_out, 16)

            def send_qk(n, names, b):
                s = pj[n]
                chunks = NC * len(names)
                for m in range(chunks):
                    sp.wait_ge(s["lo"], chunks * b + m + 1)
                    c = m % NC
                    dst = qk_hbm[names[m // NC]].ap()[:, c * P:(c + 1) * P, b * S:(b + 1) * S].rearrange("s p t -> p s t")
                    sp.dma_start(dst, hl[:, m, :, :].bitcast(F32)).then_inc(s["sent"][m], 16)

            def send_v(n, name, b):
                s = pj[n]
                for k in range(TB):
                    sp.wait_ge(s["vt"], 2 * b + k // 2 + 1)
                    sp.dma_start(v_hbm[name].ap()[b, :, :, k, :].rearrange("g p c -> p g c"),
                                 vt[:, k, :, :].rearrange("p (g h) e -> p g (h e)", g=G)).then_inc(s["vsent"][k], 16)

            def load_unit(a, u, j):
                s = a["s"]
                if not (isinstance(u, int) and u < RING):
                    sp.wait_ge(s["scored"], TAUS * (u - (RING - 1)))
                g, b = u // B, u % B

                def part(hbm, half):
                    ap = hbm.ap()[half].rearrange("(g h d) t -> d g h t", g=G, h=HG)
                    return ap[:, bass.ds(g, 1), :, bass.ds(b * S, S)].rearrange("d o h t -> d (o h) t")

                for row, half in enumerate((0, 0, 1, 1)):
                    sp.dma_start(QU[j][DK * row:DK * row + DK, :, :].bitcast(F32), part(a["q"], half)).then_inc(s["loaded"][j], 16)
                for row, half in enumerate((0, 1, 0, 1)):
                    sp.dma_start(KU[j][DK * row:DK * row + DK, :, :].bitcast(F32), part(a["k"], half)).then_inc(s["loaded"][j], 16)
                if not (isinstance(u, int) and u < RING):
                    sp.wait_ge(s["pvd"], TAUS * (u - (RING - 1)))
                v_src = a["v"].ap().rearrange("b g p k c -> p (b g) (k c)")[:, bass.ds(b * G + g, 1), :]
                sp.dma_start(VU[j][:, :, :, :].rearrange("p k h e -> p (k h e)"), v_src.rearrange("p o n -> p (o n)")).then_inc(s["loaded"][j], 16)

            def send_shift(a, u, j, mj):
                s = a["s"]
                if isinstance(u, int) and u == 0:
                    sp.wait_ge(s["sread"], USES - 1)
                else:
                    sp.wait_ge(s["sread"], USES * u + (USES - 2))
                sp.dma_start(QU[j][SHIFT_ROW:SHIFT_ROW + 1, :, :].rearrange("o h (q t) -> o (h q) t", q=TB).bitcast(F32),
                             MR[:, mj, :].bitcast(F32)).then_inc(s["shift"][j], 16)

            def attention(a):
                for u in range(1, RING):
                    load_unit(a, u, u)
                send_shift(a, 0, 0, 0)
                with sp.Fori(0, LOOPS) as i:
                    for r in range(RING):
                        send_shift(a, RING * i + (r + 1), (r + 1) % RING, 0)
                        load_unit(a, RING * i + (r + RING), r)
                for u in range(RING * LOOPS, U):
                    if u + 1 < U:
                        send_shift(a, u + 1, (u + 1) % RING, 0)
                    if u + RING < U:
                        load_unit(a, u + RING, u % RING)

            for b in range(B):
                send_qk("ctx", ["k2"], b)
                send_v("ctx", "v2", b)
            for b in range(B):
                if b == B - 1:
                    wait_sent(sp, "self", 1)
                    load_unit(a1, 0, 0)
                send_qk("self", ["q1", "k1"], b)
                send_v("self", "v1", b)
            wait_sent(sp, "self", B)
            sp.wait_ge(pj["self"]["v"], 2 * B)
            attention(a1)
            wait_sent(sp, "ctx", B)
            sp.wait_ge(a1["s"]["pvd"], TAUS * U)
            for b in range(B):
                if b == B - 1:
                    wait_sent(sp, "xq", 1)
                    load_unit(a2, 0, 0)
                send_qk("xq", ["q2"], b)
            wait_sent(sp, "xq", B)
            sp.wait_ge(pj["xq"]["qk"], NC * B)
            attention(a2)
            sp.wait_ge(a2["s"]["oevac"], U)
            sp.dma_start(bias_e[:, :], e_bias.rearrange("(a n) -> a n", a=1).broadcast_to([P, E])).then_inc(mo["gate_in"], 16)
            w_src = w_exp.rearrange("e p n -> p e n")

            def load_expert(e, j, first=False):
                if not first:
                    sp.wait_ge(mo["w_hi"], e - 1)
                    sp.wait_ge(mo["w_lo"], e - 1)
                sp.dma_start(wraw[j][:, :], w_src[:, bass.ds(e, 1), :].rearrange("p o n -> p (o n)")).then_inc(mo["w_raw"][j], 16)

            for j in range(2):
                load_expert(j, j, first=True)
            with sp.Fori(1, EA // 2) as i:
                for j in range(2):
                    load_expert(2 * i + j, j)
            sp.wait_ge(mo["acc"], TB * B * EA)
            sp.dma_start(out_tiles, X[:, :, :]).then_inc(done_s, 16)
            sp.wait_ge(done_s, 16)

        @block.gpsimd
        def _(pool):
            for n, f in enumerate(INV_FREQ):
                pool.memset(freq[:, n:n + 1], float(f)).then_inc(const_m, 1)
            pool.memset(neghalf[:, :], -0.5).then_inc(const_m, 1)
            pool.iota(iota_i[:, :], pattern=[[1, E]], base=0, channel_multiplier=0).then_inc(mo["iota"], 1)
            pool.memset(ident[:, :], 0.0).then_inc(const_a, 1)
            pool.memset(mask_f[:, :, :], 0.0).then_inc(const_a, 1)
            pool.memset(flip[:, :], 0.0).then_inc(const_a, 1)
            pool.wait_ge(const_a, 3)
            pool.affine_select(out=flip[:, :], in_=flip[:, :], compare_op=ALU.not_equal, fill=1.0, base=-(P - 1),
                               pattern=[[1, P]], channel_multiplier=1).then_inc(const_b, 1)
            pool.affine_select(out=ident[:, :], in_=ident[:, :], compare_op=ALU.not_equal, fill=1.0, base=0,
                               pattern=[[-1, P]], channel_multiplier=1).then_inc(const_b, 1)
            pool.affine_select(out=mask_f[:, 0, :], in_=mask_f[:, 0, :], compare_op=ALU.is_ge, fill=-BIG, base=0,
                               pattern=[[-1, P]], channel_multiplier=1).then_inc(const_b, 1)
            pool.affine_select(out=mask_f[:, 1, :], in_=mask_f[:, 1, :], compare_op=ALU.is_ge, fill=-BIG, base=0,
                               pattern=[[1, P]], channel_multiplier=-1).then_inc(const_b, 1)
            pool.memset(vt[:, :, :, :], 1.0).then_inc(vt_init, 1)

            def rotate_cos(n, b):
                s = pj[n]
                for m in range(NC):
                    wait(pool, s["kf"], NC * b + m + 1)
                    wait(pool, s["rot"], NC * (b - 1) + m + 1)
                    pool.tensor_tensor(rot1[:, m, :], kf[:, m, :], cos_t[:, b * S:(b + 1) * S], ALU.mult).then_inc(s["rot1"], 1)

            inits = {"n": 0}
            pool.wait_ge(const_m, 1 + DK // 2)
            for b in range(B):
                rotate_cos("ctx", b)
                norm_power(pool, "self", b)

            def init_stack(j):
                wait(pool, stack_init, inits["n"])
                pool.memset(KU[j][64:P, :, :].bitcast(F32), 0.0).then_inc(stack_zero, 1)
                pool.memset(QU[j][64:P, :, :].bitcast(F32), 0.0).then_inc(stack_zero, 1)
                inits["n"] += 1
                pool.wait_ge(stack_zero, 2 * inits["n"])
                pool.memset(KU[j][SHIFT_ROW:SHIFT_ROW + 1, :, :].bitcast(F32), 1.0).then_inc(stack_init, 1)

            def stacks_ready(a):
                pool.wait_ge(stack_init, inits["n"])
                pool.sem_inc(a["s"]["zeroed"], 1)

            def add_bias(n, row):
                pool.tensor_tensor(X[:, :, :], X[:, :, :], row[:, :].rearrange("p (o d) -> p o d", o=1).broadcast_to([P, NT, D]), ALU.add)\
                    .then_inc(out_s[n]["bias"], 1)

            def zero_shift(a, u, j):
                s = a["s"]
                pool.wait_ge(s["scored"], TAUS * (u - (RING - 1)))
                ones = KU[j][SHIFT_ROW:SHIFT_ROW + 1, :, :]
                pool.tensor_tensor(QU[j][SHIFT_ROW:SHIFT_ROW + 1, :, :], ones.bitcast(F32), ones.bitcast(F32), ALU.subtract).then_inc(s["zeroed"], 1)

            def load_toeplitz(g):
                src = bass.AP(rel_hbm, g * (HG * 2 * RPW), [[1, P], [RPW, 2 * HG], [1, TW]])
                dst = toep[:, bass.ds((g % 2) * (HG * 2 * TW), HG * 2 * TW)]
                pool.dma_start(dst.rearrange("p (r y) -> p r y", y=TW).bitcast(F32), src).then_inc(t_loaded, 16)

            pool.wait_ge(pj["self"]["rstd"], B)
            init_stack(0)
            pool.wait_ge(rel_out, 16)
            pool.wait_ge(trig_mm, 2 * NT)
            wait_sent(pool, "ctx", B)
            load_toeplitz(0)
            pool.wait_ge(pj["self"]["xn"], NT)
            pool.wait_ge(w_in, 16 * 10)
            wait_sent(pool, "self", B)
            pool.wait_ge(pj["self"]["v"], 2 * B)
            for j in range(1, RING):
                init_stack(j)
            stacks_ready(a1)
            pool.wait_ge(t_loaded, 16)
            load_toeplitz(1)
            for u in range(RING, U):
                if u % B == 2 and u // B + 1 < G:
                    pool.wait_ge(t_loaded, 16 * (u // B + 1))
                    pool.wait_ge(a1["s"]["scored"], TAUS * B * (u // B))
                    load_toeplitz(u // B + 1)
                zero_shift(a1, u, u % RING)
            pool.wait_ge(a1["s"]["zeroed"], U - RING + 1)
            add_bias("o1", bo_row)
            norm_power(pool, "xq", 0)
            for b in range(B):
                if b + 1 < B:
                    norm_power(pool, "xq", b + 1)
                rotate_cos("xq", b)
            wait_sent(pool, "xq", B)
            pool.wait_ge(pj["xq"]["qk"], NC * B)
            pool.wait_ge(pj["xq"]["rot1"], NC * B)
            for j in range(1, RING):
                init_stack(j)
            stacks_ready(a2)
            with pool.Fori(1, LOOPS + 1) as i:
                for j in range(RING):
                    zero_shift(a2, RING * i + j, j)
            for u in range(RING * (LOOPS + 1), U):
                zero_shift(a2, u, u % RING)
            pool.wait_ge(a2["s"]["zeroed"], U - RING + 1)
            add_bias("o2", bxo_row)
            pool.wait_ge(a2["s"]["oevac"], U)
            pool.memset(comb[:, 0:SHARED * NT], 1.0).then_inc(mo["ones"], 1)
            for b in range(B):
                norm_power(pool, "moe", b)
                for c in range(NC):
                    pool.wait_ge(mo["nhi"], NC * b + c + 1)
                    pool.tensor_tensor(nhl[:, c, 1, b * S:(b + 1) * S], nT3[:, c, :], nhl[:, c, 0, b * S:(b + 1) * S].bitcast(F32), ALU.subtract).then_inc(mo["nlo"], 1)

            def split_low(e, j):
                pool.wait_ge(mo["w_hi"], e + 1)
                pool.tensor_tensor(whl[j][:, 1, :], wraw[j][:, :], whl[j][:, 0, :].bitcast(F32), ALU.subtract).then_inc(mo["w_lo"], 1)

            with pool.Fori(0, EA // 2) as i:
                for j in range(2):
                    split_low(2 * i + j, j)

        @block.scalar
        def _(act):
            act.wait_ge(const_b, 4)
            act.activation(flip_r[:, :], flip[:, :], ACT.Copy).then_inc(const_m, 1)
            act.activation(ident_r[:, :], ident[:, :], ACT.Copy).then_inc(const_m, 1)
            act.activation(mask_r[:, :, :], mask_f[:, :, :], ACT.Copy).then_inc(const_m, 1)
            act.wait_ge(ang_s, 8)
            act.activation(ang[7][:, :, :], ang[4][:, :, :], ACT.Sin).then_inc(ang_act, 1)
            act.wait_ge(ang_s, 12)
            act.activation(ang[8][:, :, :], ang[6][:, :, :], ACT.Sin).then_inc(ang_act, 1)
            for t in range(NT):
                for w, dst in ((0, cos_t), (1, sin_t)):
                    n = 2 * t + w
                    act.wait_ge(trig_mm, n + 1)
                    act.activation(dst[:, t * P:(t + 1) * P], bank[:, n % 8, 0:P], ACT.Copy).then_inc(trig_out, 1)

            def kf_evac(n, b, col, first_bank):
                s = pj[n]
                for m in range(NC):
                    act.wait_ge(s["qk"], NC * b + m + 1)
                    wait(act, s["rot"], NC * (b - 1) + m + 1)
                    act.activation(kf[:, m, :], bank[:, first_bank + m, :], ACT.Identity, bias=col[:, m:m + 1]).then_inc(s["kf"], 1)

            def hi_rot(n, b):
                s = pj[n]
                for m in range(NC):
                    act.wait_ge(s["rot"], NC * b + m + 1)
                    wait(act, s["sent"][m], 16 * b)
                    act.activation(hl[:, m, 0, :], swap[:, m, :], ACT.Copy).then_inc(s["hi"], 1)

            act.wait_ge(ctx_w_in, 64)
            for b in range(B):
                kf_evac("ctx", b, bxk_col, 0)
                hi_rot("ctx", b)
            s = pj["self"]
            wait_sent(act, "ctx", B)
            act.wait_ge(w_in, 16 * 10)
            for b in range(B):
                for c in range(NC):
                    act.wait_ge(s["tr"], NC * b + c + 1)
                    act.activation(nT[:, c, :], bank[:, 4 + c, :], ACT.Copy).then_inc(s["trev"], 1)
                for m in range(4):
                    act.wait_ge(s["qk"], 4 * b + m + 1)
                    wait(act, s["sent"][m], 16 * b)
                    act.activation(hl[:, m, 0, :], bank[:, m, :], ACT.Identity, bias=bqk_col[:, m:m + 1]).then_inc(s["hi"], 1)

            def o_evac(a, u):
                s = a["s"]
                act.wait_ge(s["pvd"], TAUS * u + TAUS)
                if not (isinstance(u, int) and u == 0):
                    last = isinstance(u, int) and u == U - 1
                    act.wait_ge(s["swrote"], first_use(u) + ((0 if last else a["out_use"]) + 1))
                act.activation(OS[:, :], bank[:, 7, :], ACT.Copy).then_inc(s["oevac"], 1)

            def unit(a, u, j):
                s = a["s"]
                first = isinstance(u, int) and u == 0
                if not first:
                    o_evac(a, u - 1)
                for tau in range(TAUS):
                    q0 = (tau // 2) * P if a["causal"] else 0
                    act.wait_ge(s["scored"], TAUS * u + (tau + 1))
                    if not (first and tau < 4):
                        act.wait_ge(s["pvd"], TAUS * u + (tau - 3))
                    act.activation(PT[:, tau % 4, :, q0:S], bank[:, 2 * (tau % 2):2 * (tau % 2) + 2, q0:S], ACT.Exp, scale=RAW_SCALE).then_inc(s["expd"], 1)

            def attention(a):
                units(act, lambda u, j: unit(a, u, j))
                o_evac(a, U - 1)

            def out_evac(n, b):
                s = out_s[n]
                for c in range(NC):
                    act.wait_ge(s["tr"], NC * b + c + 1)
                    wait(act, s["mm"], 2 * b)
                    act.activation(oT[:, c, :], bank[:, c, :], ACT.Copy).then_inc(s["trev"], 1)

            attention(a1)

            def query_evac(b):
                s = pj["xq"]
                for c in range(NC):
                    act.wait_ge(s["tr"], NC * b + c + 1)
                    wait(act, s["qk"], NC * b)
                    act.activation(nT[:, c, :], bank[:, 4 + c, :], ACT.Copy).then_inc(s["trev"], 1)
                kf_evac("xq", b, bxq_col, 6)
                hi_rot("xq", b)

            def moe_evac(b):
                s = pj["moe"]
                for c in range(NC):
                    act.wait_ge(s["tr"], NC * b + c + 1)
                    wait(act, mo["logits"], b)
                    wait(act, mo["nlo"], NC * (b - 1) + c + 1)
                    act.activation(nT3[:, c, :], bank[:, 4 + c, :], ACT.Copy).then_inc(s["trev"], 1)
                for c in range(NC):
                    act.wait_ge(s["trev"], NC * b + c + 1)
                    act.activation(nhl[:, c, 0, b * S:(b + 1) * S], nT3[:, c, :], ACT.Copy).then_inc(mo["nhi"], 1)
                act.wait_ge(mo["logits"], b + 1)
                act.activation(score[:, b * TB:(b + 1) * TB, :], bank[:, 6 + b % 2, 0:P].rearrange("p (t e) -> p t e", e=E), ACT.Sigmoid).then_inc(mo["score"], 1)

            out_evac("o1", 0)
            for b in range(B):
                if b + 1 < B:
                    out_evac("o1", b + 1)
                query_evac(b)
            attention(a2)
            out_evac("o2", 0)
            for b in range(B):
                if b + 1 < B:
                    out_evac("o2", b + 1)
                moe_evac(b)

            def split_high(e, j, k, first=False):
                act.wait_ge(mo["w_raw"][j], 16 * k + 16)
                if not first:
                    act.wait_ge(mo["down"], B * (e - 1))
                act.activation(whl[j][:, 0, :], wraw[j][:, :], ACT.Copy).then_inc(mo["w_hi"], 1)

            def expert_pair(i, first=False, last=False):
                for n in range(2 * B):
                    st, j = 2 * B * i + n, n % 2
                    young = first and n < 2
                    act.wait_ge(mo["gu"], st + 1)
                    if not young:
                        act.wait_ge(mo["h"], st - 1)
                    act.activation(sg[j][:, :], bank[:, j, :], ACT.Silu).then_inc(mo["silu"], 1)
                    act.wait_ge(mo["h"], st + 1)
                    if not young:
                        act.wait_ge(mo["down"], st - 1)
                    act.activation(hhl[j][:, 0, :], hid[j][:, :], ACT.Copy).then_inc(mo["hi"], 1)
                    if n == 1 and not first:
                        split_high(2 * i + 1, 1, i)
                    if n == B + 1 and not last:
                        split_high(2 * i + 2, 0, i + 1)

            split_high(0, 0, 0, first=True)
            split_high(1, 1, 0, first=True)
            expert_pair(0, first=True)
            with act.Fori(1, EA // 2 - 1) as i:
                expert_pair(i)
            expert_pair(EA // 2 - 1, last=True)

        @block.tensor
        def _(pe):
            pe.wait_ge(const_b, 4)
            pe.wait_ge(trig_ready, 2)
            for t in range(NT):
                for w in range(2):
                    n = 2 * t + w
                    wait(pe, trig_out, n - 7)
                    pe.transpose(bank[:, n % 8, 0:P], trig8[:, w, t, :, :].rearrange("p r f -> p (r f)"), ident[:, :]).then_inc(trig_mm, 1)

            def feature_major(n, wt, col0, chunks, src, b, first_bank, freed):
                s = pj[n]
                for m in range(chunks):
                    wait(pe, freed, chunks * (b - 1) + m + 1)
                    for c in range(NC):
                        mm = pe.matmul(bank[:, first_bank + m, :], wt[:, c, col0 + m * P:col0 + (m + 1) * P], src[:, c, :], start=(c == 0), stop=(c == NC - 1))
                    mm.then_inc(s["qk"], 1)

            def token_major(done, wt, col0, src, b, first_bank, freed):
                for k in range(2):
                    wait(pe, freed, 2 * (b - 1) + k + 1)
                    for t in range(2):
                        tok = (2 * k + t) * P
                        for c in range(NC):
                            mm = pe.matmul(bank[:, first_bank + k, t * D:(t + 1) * D], src[:, c, tok:tok + P], wt[:, c, col0:col0 + D],
                                           start=(c == 0), stop=(c == NC - 1))
                    mm.then_inc(done, 1)

            def transposes(src, b, first_bank, done, ready, per_tile, freed):
                for c in range(NC):
                    wait(pe, freed, NC * (b - 1) + c + 1)
                    for t in range(TB):
                        if c == 0 and per_tile:
                            pe.wait_ge(ready, TB * b + t + 1)
                        tr = pe.transpose(bank[:, first_bank + c, t * P:(t + 1) * P], src[:, b * TB + t, c * P:(c + 1) * P], ident[:, :])
                    tr.then_inc(done, 1)

            pe.wait_ge(trig_out, 2 * NT)
            pe.wait_ge(ctx_in, 16)
            pe.wait_ge(ctx_w_in, 64)
            for b in range(B):
                feature_major("ctx", wxk, 0, NC, batch(ctx_sb, b), b, 0, pj["ctx"]["kf"])
                token_major(pj["ctx"]["v"], wxv, 0, batch(ctx_sb, b), b, 2, pj["ctx"]["vt"])
            s = pj["self"]
            pe.wait_ge(w_in, 16 * 10)
            for b in range(B):
                if b == 0:
                    pe.wait_ge(pj["ctx"]["kf"], NC * B)
                    pe.wait_ge(pj["ctx"]["vt"], 2 * B)
                transposes(XN, b, 4, s["tr"], s["xn"], True, s["trev"])
                pe.wait_ge(s["trev"], NC * b + 2)
                feature_major("self", wqkv, 0, 4, nT, b, 0, s["lo"])
                token_major(s["v"], wqkv, 2 * D, nT, b, 6, s["vt"])

            def row_scores(a, dst, j, h, qb):
                keys = P * (qb + 1) if a["causal"] else S
                q = slice(qb * P, (qb + 1) * P)
                mm = pe.matmul(dst[:, 0:keys], QU[j][:, h, q], KU[j][:, h, 0:keys], start=True, stop=not a["causal"])
                if a["causal"]:
                    mm = pe.matmul(dst[:, q], ident_r[:, :], mask_r[:, 0, :], start=False, stop=True)
                mm.then_inc(a["s"]["swrote"], 1)

            def maxima_rows(a, dst):
                pe.transpose(dst[0:HG * TB, 0:P], M[:, 0, :], ident[:, :]).then_inc(a["s"]["swrote"], 1)

            def outputs_token_major(a, u, dst):
                pe.wait_ge(a["s"]["oevac"], u + 1)
                for qb in range(TB):
                    tr = pe.transpose(dst[:, qb * P:(qb + 1) * P], OS[:, qb * P:(qb + 1) * P], ident[:, :])
                tr.then_inc(a["s"]["swrote"], 1)

            def key_scores(a, u, tau, x, j):
                s = a["s"]
                kb, h = tau // 2, 2 * (tau % 2) + x
                q0 = kb * P if a["causal"] else 0
                if x == 0 and not (isinstance(u, int) and u == 0 and tau < 2):
                    pe.wait_ge(s["expd"], TAUS * u + (tau - 1))
                dst = bank[:, 2 * (tau % 2) + x, :]
                mm = pe.matmul(dst[:, q0:S], KU[j][:, h, kb * P:(kb + 1) * P], QU[j][:, h, q0:S], start=True, stop=False)
                if a["causal"]:
                    mm = pe.matmul(dst[:, q0:q0 + P], ident_r[:, :], mask_r[:, 1, :], start=False, stop=True)
                else:
                    for part in range(2):
                        row = (u // B) % 2 * (HG * 2 * TW) + ((2 * h + part) * TW + S - P - kb * P)
                        mm = pe.matmul(dst, flip_r[:, :], toep[:, bass.ds(row, S)], start=False, stop=(part == 1))
                if x == 1:
                    mm.then_inc(s["scored"], 1)

            def weigh(a, u, tau, j):
                s = a["s"]
                kb, half = tau // 2, tau % 2
                q0 = kb * P if a["causal"] else 0
                if tau == 0 and not (isinstance(u, int) and u == 0):
                    pe.wait_ge(s["oevac"], u)
                pe.wait_ge(s["expd"], TAUS * u + (tau + 1))
                for x in range(2):
                    h = 2 * half + x
                    mm = pe.matmul(bank[32 * h:32 * h + 32, 7, q0:S], VU[j][:, kb, h, :], PT[:, tau % 4, x, q0:S],
                                   start=(kb == 0), stop=(kb == TB - 1), tile_position=(0, 32 * h))
                mm.then_inc(s["pvd"], 1)

            def unit(a, u, j):
                s = a["s"]
                first = isinstance(u, int) and u == 0
                last = isinstance(u, int) and u == U - 1
                jn = (j + 1) % RING
                n = done = 0
                pe.wait_ge(s["shift"][j], 16 * (u // RING) + 16)
                if not a["causal"]:
                    pe.wait_ge(t_loaded, 16 * (u // B) + 16)

                def ring_use(kind):
                    nonlocal n, done
                    if (kind == "o" and first) or (kind != "o" and last):
                        return
                    pe.wait_ge(s["sread"], first_use(u) + (n - (RING - 1)))
                    dst = bank[:, slot_of(u, n), :]
                    if kind == "o":
                        outputs_token_major(a, u - 1, dst)
                    elif kind == "r":
                        if done == 0:
                            pe.wait_ge(s["loaded"][jn], 16 * LOADS * ((u + 1) // RING) + 16 * LOADS)
                            pe.wait_ge(s["zeroed"], 1 if isinstance(u, int) and u == 0 else u)
                        row_scores(a, dst, jn, done // TB, done % TB)
                        done += 1
                    else:
                        pe.wait_ge(s["sread"], first_use(u) + n)
                        maxima_rows(a, dst)
                    n += 1

                for tau in range(TAUS):
                    uses = list(a["uses"][tau])
                    key_scores(a, u, tau, 0, j)
                    if uses:
                        ring_use(uses.pop(0))
                    key_scores(a, u, tau, 1, j)
                    if uses:
                        ring_use(uses.pop(0))
                    if tau >= 1:
                        weigh(a, u, tau - 1, j)
                    for kind in uses:
                        ring_use(kind)
                weigh(a, u, TAUS - 1, j)

            def attention(a):
                s = a["s"]
                pe.wait_ge(s["loaded"][0], 16 * LOADS)
                for n in range(HG * TB):
                    wait(pe, s["sread"], n - (RING - 1))
                    row_scores(a, bank[:, slot(n), :], 0, n // TB, n % TB)
                pe.wait_ge(s["sread"], HG * TB)
                maxima_rows(a, bank[:, slot(HG * TB), :])
                units(pe, lambda u, j: unit(a, u, j))
                outputs_token_major(a, U - 1, bank[:, slot_of(U - 1, 1), :])

            pe.wait_ge(s["lo"], 4 * B)
            pe.wait_ge(s["vt"], 2 * B)
            pe.wait_ge(const_m, 4 + DK // 2)
            pe.wait_ge(stack_init, 1)
            attention(a1)
            def out_projection(n, wt, b):
                o = out_s[n]
                transposes(XN, b, 0, o["tr"], None, False, o["trev"])
                pe.wait_ge(o["trev"], NC * b + 2)
                token_major(o["mm"], wt, 0, oT, b, 2, o["add"])

            def queries(b):
                s = pj["xq"]
                transposes(XN, b, 4, s["tr"], s["xn"], True, s["trev"])
                pe.wait_ge(s["trev"], NC * b + 2)
                feature_major("xq", wxq, 0, NC, nT, b, 6, s["kf"])

            def routing_logits(b):
                transposes(XN, b, 4, pj["moe"]["tr"], pj["moe"]["xn"], True, pj["moe"]["trev"])
                wait(pe, mo["score"], b - 1)
                for k in range(TB):
                    for c in range(NC):
                        pe.wait_ge(pj["moe"]["trev"], NC * b + c + 1)
                        mm = pe.matmul(bank[:, 6 + b % 2, k * E:(k + 1) * E], nT3[:, c, k * P:(k + 1) * P], wgate[:, c, :],
                                       start=(c == 0), stop=(c == NC - 1))
                mm.then_inc(mo["logits"], 1)

            pe.wait_ge(a1["s"]["sread"], USES * U)
            out_projection("o1", wout, 0)
            for b in range(B):
                if b + 1 < B:
                    out_projection("o1", wout, b + 1)
                queries(b)
            pe.wait_ge(pj["xq"]["kf"], NC * B)
            attention(a2)
            pe.wait_ge(a2["s"]["sread"], USES * U)
            out_projection("o2", wxo, 0)
            for b in range(B):
                if b + 1 < B:
                    out_projection("o2", wxo, b + 1)
                routing_logits(b)

            PRODUCTS = ((0, 0), (0, 1), (1, 0))

            def gate_up(st, j, wj, b, first):
                if not first:
                    pe.wait_ge(mo["h"], st - 1)
                for half in range(2):
                    n = 0
                    for c in range(NC):
                        for x, y in PRODUCTS:
                            col = c * 2 * I + half * I
                            mm = pe.matmul(bank[:, 2 * half + j, :], whl[wj][:, x, col:col + I], nhl[:, c, y, b * S:(b + 1) * S],
                                           start=(n == 0), stop=(n == 3 * NC - 1))
                            n += 1
                mm.then_inc(mo["gu"], 1)

            def down(st, j, wj, first):
                pe.wait_ge(mo["hi"], st + 1)
                pe.wait_ge(mo["lo"], st + 1)
                if not first:
                    pe.wait_ge(mo["acc"], TB * (st - 1))
                for k in range(TB):
                    for n, (x, y) in enumerate(PRODUCTS):
                        mm = pe.matmul(bank[:, 4 + 2 * j + k // 2, (k % 2) * D:(k % 2 + 1) * D], hhl[j][:, x, k * P:(k + 1) * P],
                                       whl[wj][:, y, NC * 2 * I:WW], start=(n == 0), stop=(n == 2))
                mm.then_inc(mo["down"], 1)

            def expert_pair(i, first=False):
                for n in range(2 * B):
                    st, j = 2 * B * i + n, n % 2
                    if n % B == 0:
                        pe.wait_ge(mo["w_hi"], 2 * i + (n // B + 1))
                        pe.wait_ge(mo["w_lo"], 2 * i + (n // B + 1))
                    gate_up(st, j, n // B, n % B, first and n < 2)
                    if not (first and n == 0):
                        down(st - 1, (j + 1) % 2, ((n - 1) % (2 * B)) // B, first and n < 3)

            pe.wait_ge(mo["nlo"], NC * B)
            pe.wait_ge(mo["score"], B)
            pe.wait_ge(out_s["o2"]["add"], 2 * B)
            expert_pair(0, first=True)
            with pe.Fori(1, EA // 2) as i:
                expert_pair(i)
            down(B * EA - 1, 1, 1, False)

        @block.vector
        def _(dve):
            count = {"ang": 0}

            def step(ins):
                count["ang"] += 1
                ins.then_inc(ang_s, 1)
                dve.wait_ge(ang_s, count["ang"])

            dve.wait_ge(pos_in, 16)
            step(dve.tensor_copy(pos_f[:, :], pos_i[:, :]))
            dve.wait_ge(const_m, 1 + DK // 2)
            step(dve.tensor_tensor(ang[0][:, :, :], pos_f[:, :].rearrange("p (t o) -> p t o", o=1).broadcast_to([P, NT, DK // 2]),
                                   freq[:, :].rearrange("p (o f) -> p o f", o=1).broadcast_to([P, NT, DK // 2]), ALU.mult))
            step(dve.tensor_scalar(ang[1][:, :, :], ang[0][:, :, :], 1.0 / TWO_PI, ROUND, ALU.mult, ALU.add))
            step(dve.tensor_scalar(ang[2][:, :, :], ang[1][:, :, :], -ROUND, None, ALU.add))
            step(dve.scalar_tensor_tensor(out=ang[3][:, :, :], in0=ang[2][:, :, :], scalar=-C1, in1=ang[0][:, :, :], op0=ALU.mult, op1=ALU.add))
            step(dve.scalar_tensor_tensor(out=ang[5][:, :, :], in0=ang[2][:, :, :], scalar=-C2, in1=ang[3][:, :, :], op0=ALU.mult, op1=ALU.add))
            step(dve.scalar_tensor_tensor(out=ang[1][:, :, :], in0=ang[2][:, :, :], scalar=-C3, in1=ang[5][:, :, :], op0=ALU.mult, op1=ALU.add))
            step(dve.tensor_scalar(ang[4][:, :, :], ang[1][:, :, :], PI_SAFE, -PI_SAFE, ALU.min, ALU.max))
            step(dve.tensor_scalar(ang[3][:, :, :], ang[1][:, :, :], float(np.pi / 2), None, ALU.add))
            step(dve.tensor_scalar(ang[5][:, :, :], ang[3][:, :, :], float(np.pi), -TWO_PI, ALU.is_gt, ALU.mult))
            step(dve.tensor_tensor(ang[2][:, :, :], ang[3][:, :, :], ang[5][:, :, :], ALU.add))
            step(dve.tensor_scalar(ang[6][:, :, :], ang[2][:, :, :], PI_SAFE, -PI_SAFE, ALU.min, ALU.max))
            dve.wait_ge(ang_act, 2)
            step(dve.tensor_copy(trig[:, 0, :, :, :], ang[8][:, :, :].rearrange("p t (f o) -> p t f o", o=1).broadcast_to([P, NT, DK // 2, 2])))
            step(dve.tensor_scalar(trig[:, 1, :, :, 0], ang[7][:, :, :], -1.0, None, ALU.mult))
            step(dve.tensor_scalar(trig[:, 1, :, :, 1], ang[7][:, :, :], 1.0, None, ALU.mult))
            for w in range(2):
                dve.tensor_copy(trig8[:, w, :, :, :], trig[:, w, :, :, :].rearrange("p t (o f) e -> p t o (f e)", o=1).broadcast_to([P, NT, P // DK, DK]))\
                    .then_inc(trig_ready, 1)
            dve.wait_ge(rel_in_s, 16)
            dve.tensor_reduce(rel_max[:, :], rel_in[:, :], AX_X, ALU.max).then_inc(rel_ready, 1)
            dve.wait_ge(rel_ready, 1)
            dve.tensor_scalar(rel_s[:, :], rel_in[:, :], rel_max[:, 0:1], 1.0 / RAW_SCALE, ALU.subtract, ALU.mult).then_inc(rel_ready, 1)
            dve.wait_ge(rel_ready, 2)
            dve.tensor_copy(rel_hl[:, 0, :], rel_s[:, :]).then_inc(rel_ready, 1)
            dve.wait_ge(rel_ready, 3)
            dve.tensor_tensor(rel_hl[:, 1, :], rel_s[:, :], rel_hl[:, 0, :].bitcast(F32), ALU.subtract).then_inc(rel_ready, 1)

            def layer_norm(n, dst, b):
                s = pj[n]
                for k in range(TB):
                    t = TB * b + k
                    dve.bn_stats(stats[:, t, :], X[:, t, :]).then_inc(s["stat"], 1)
                for k in range(TB):
                    t = TB * b + k
                    dve.wait_ge(s["stat"], t + 1)
                    dve.bn_aggr(mv[:, t, :], stats[:, t, :]).then_inc(s["mv"], 1)
                tiles = slice(TB * b, TB * (b + 1))
                dve.wait_ge(s["mv"], TB * (b + 1))
                dve.tensor_scalar(vare[:, tiles], mv[:, tiles, 1], EPS, None, ALU.add).then_inc(s["var"], 1)

            def normalise(n, dst, b):
                s = pj[n]
                dve.wait_ge(s["rstd"], b + 1)
                for k in range(TB):
                    t = TB * b + k
                    dve.tensor_scalar(dst[:, t, :], X[:, t, :], mv[:, t, 0:1], rstd[:, t:t + 1], ALU.subtract, ALU.mult).then_inc(s["xn"], 1)

            def rotate(n, b):
                s = pj[n]
                for m in range(NC):
                    dve.wait_ge(s["kf"], NC * b + m + 1)
                    wait(dve, s["lo"], NC * (b - 1) + m + 1)
                    dve.stream_shuffle(swap[:, m, :], kf[:, m, :], [p ^ 1 for p in range(32)]).then_inc(s["swap"], 1)
                for m in range(NC):
                    dve.wait_ge(s["swap"], NC * b + m + 1)
                    dve.tensor_tensor(rot2[:, m, :], swap[:, m, :], sin_t[:, b * S:(b + 1) * S], ALU.mult).then_inc(s["rot2"], 1)
                for m in range(NC):
                    dve.wait_ge(s["rot2"], NC * b + m + 1)
                    dve.wait_ge(s["rot1"], NC * b + m + 1)
                    dve.tensor_tensor(swap[:, m, :], rot1[:, m, :], rot2[:, m, :], ALU.add).then_inc(s["rot"], 1)

            def low_rot(n, b):
                s = pj[n]
                for m in range(NC):
                    dve.wait_ge(s["hi"], NC * b + m + 1)
                    dve.tensor_tensor(hl[:, m, 1, :], swap[:, m, :], hl[:, m, 0, :].bitcast(F32), ALU.subtract).then_inc(s["lo"], 1)

            def values(n, row, b, first_bank):
                s = pj[n]
                for k in range(2):
                    dve.wait_ge(s["v"], 2 * b + k + 1)
                    wait(dve, s["vsent"][2 * k], 16 * b)
                    wait(dve, s["vsent"][2 * k + 1], 16 * b)
                    dve.tensor_tensor(vt[:, 2 * k:2 * k + 2, :, 0:DK], bank[:, first_bank + k, :].rearrange("p (t h d) -> p t h d", t=2, h=H),
                                      row[:, :].rearrange("p (o h d) -> p o h d", o=1, h=H).broadcast_to([P, 2, H, DK]), ALU.add).then_inc(s["vt"], 1)

            dve.wait_ge(trig_out, 2 * NT)
            dve.wait_ge(vt_init, 1)
            dve.wait_ge(ctx_w_in, 64)
            for b in range(B):
                rotate("ctx", b)
                if b == 0:
                    dve.wait_ge(x_in, 16)
                layer_norm("self", XN, b)
                values("ctx", bxv_row, b, 2)
                low_rot("ctx", b)
                normalise("self", XN, b)
            dve.wait_ge(w_in, 16 * 10)
            s = pj["self"]
            for b in range(B):
                for m in range(4):
                    dve.wait_ge(s["hi"], 4 * b + m + 1)
                    dve.scalar_tensor_tensor(out=hl[:, m, 1, :], in0=bank[:, m, :], scalar=bqk_col[:, m:m + 1], in1=hl[:, m, 0, :].bitcast(F32),
                                             op0=ALU.add, op1=ALU.subtract).then_inc(s["lo"], 1)
                values("self", bv_row, b, 6)

            def outputs(a, u, n, slot_bank, dst):
                s = a["s"]
                dve.wait_ge(s["swrote"], n)
                dve.wait_ge(s["sread"], n - 1)
                src = bank[:, slot_bank, :].rearrange("p (q h e) -> p q h e", q=TB, h=HG)
                dve.reciprocal(R[:, :].rearrange("p (q h) -> p q h", q=TB), src[:, :, :, DK]).then_inc(s["recip"], 1)
                dve.wait_ge(s["recip"], u + 1)
                g, b = u // B, u % B
                to = unit_columns(dst, b * (TB * D) + g * GW)
                dve.tensor_tensor(to, src[:, :, :, 0:DK],
                                  R[:, :].rearrange("p (q h o) -> p q h o", q=TB, o=1).broadcast_to([P, TB, HG, DK]), ALU.mult).then_inc(s["sread"], 1)

            def unit_columns(dst, col):
                full = dst[:, 0:TB, 0:GW].rearrange("p t (h d) -> p t h d", h=HG)
                return bass.AP(full.tensor, full.offset + col, full.ap)

            def row_max(a, n, slot_bank, c):
                s = a["s"]
                keys = P * (c % TB + 1) if a["causal"] else S
                dve.wait_ge(s["swrote"], n)
                dve.tensor_reduce(M[:, 0, c:c + 1], bank[:, slot_bank, 0:keys], AX_X, ALU.max).then_inc(s["sread"], 1)

            def shift_rows(a, u, n, slot_bank):
                s = a["s"]
                dve.wait_ge(s["swrote"], n)
                if not (isinstance(u, int) and u == 0):
                    dve.wait_ge(s["expd"], TAUS * (u - 1) + 1)
                dve.tensor_scalar(MR[:, 0, :], bank[0:HG * TB, slot_bank, 0:P], -1.0, None, ALU.mult).then_inc(s["sread"], 1)

            def unit(a, u, j, dst):
                first = isinstance(u, int) and u == 0
                last = isinstance(u, int) and u == U - 1
                n = done = 0
                for kind in "".join(a["uses"]):
                    if (kind == "o" and first) or (kind != "o" and last):
                        continue
                    count, src = first_use(u) + (n + 1), slot_of(u, n)
                    if kind == "o":
                        outputs(a, u - 1, count, src, dst)
                    elif kind == "r":
                        row_max(a, count, src, done)
                        done += 1
                    else:
                        shift_rows(a, u + 1, count, src)
                    n += 1

            def attention(a, dst):
                for c in range(HG * TB):
                    row_max(a, c + 1, slot(c), c)
                shift_rows(a, 0, HG * TB + 1, slot(HG * TB))
                units(dve, lambda u, j: unit(a, u, j, dst))
                outputs(a, U - 1, first_use(U - 1) + 2, slot_of(U - 1, 1), dst)

            def residual(n, b):
                s = out_s[n]
                if b == 0:
                    dve.wait_ge(s["bias"], 1)
                for k in range(2):
                    t = TB * b + 2 * k
                    dve.wait_ge(s["mm"], 2 * b + k + 1)
                    dve.tensor_tensor(X[:, t:t + 2, :], X[:, t:t + 2, :], bank[:, 2 + k, :].rearrange("p (t d) -> p t d", t=2), ALU.add).then_inc(s["add"], 1)

            def residual_norm(o, n, b):
                residual(o, b)
                dve.wait_ge(out_s[o]["add"], 2 * b + 2)
                layer_norm(n, XN, b)
                normalise(n, XN, b)

            attention(a1, XN)
            residual_norm("o1", "xq", 0)
            for b in range(B):
                if b + 1 < B:
                    residual_norm("o1", "xq", b + 1)
                rotate("xq", b)
                low_rot("xq", b)
            attention(a2, XN)
            for b in range(B):
                residual_norm("o2", "moe", b)

            steps = {"n": 0}

            def route(ins):
                steps["n"] += 1
                ins.then_inc(mo["route"], 1)
                dve.wait_ge(mo["route"], steps["n"])

            def tiles_route(make):
                for t in range(NT):
                    steps["n"] += 1
                    make(t).then_inc(mo["route"], 1)
                dve.wait_ge(mo["route"], steps["n"])

            def one_hot(sel, idx, k, n):
                return dve.tensor_tensor(sel[:, :, :, :], iota_e[:, 0:n].rearrange("p (a b n) -> p a b n", a=1, b=1).broadcast_to([P, NT, k, n]),
                                         idx[:, :, 0:k].rearrange("p t (k o) -> p t k o", o=1).broadcast_to([P, NT, k, n]), ALU.is_equal)

            dve.wait_ge(mo["iota"], 1)
            dve.wait_ge(a2["s"]["oevac"], U)
            route(dve.tensor_copy(iota_e[:, :], iota_i[:, :]))
            dve.wait_ge(mo["score"], B)
            dve.wait_ge(mo["gate_in"], 16)
            route(dve.tensor_tensor(sfc[:, :, :], score[:, :, :], bias_e[:, :].rearrange("p (o e) -> p o e", o=1).broadcast_to([P, NT, E]), ALU.add))
            route(dve.tensor_reduce(gmax[:, :, :], sfc[:, :, :].rearrange("p t (g e) -> p t g e", g=NGROUP), AX_X, ALU.max))
            tiles_route(lambda t: dve.max(gtop[:, t, :], gmax[:, t, :]))
            tiles_route(lambda t: dve.max_index(gidx[:, t, :], gtop[:, t, :], gmax[:, t, :]))
            route(dve.tensor_copy(gidx_f[:, :, :], gidx[:, :, :]))
            route(one_hot(gsel, gidx_f, TOPG, NGROUP))
            route(dve.tensor_reduce(gmask[:, :, :], gsel[:, :, :, :].rearrange("p t k g -> p t g k"), AX_X, ALU.add))
            route(dve.tensor_tensor(masked[:, :, :].rearrange("p t (g e) -> p t g e", g=NGROUP), sfc[:, :, :].rearrange("p t (g e) -> p t g e", g=NGROUP),
                                    gmask[:, :, :].rearrange("p t (g o) -> p t g o", o=1).broadcast_to([P, NT, NGROUP, GE]), ALU.mult))
            tiles_route(lambda t: dve.max(etop[:, t, :], masked[:, t, :]))
            tiles_route(lambda t: dve.max_index(eidx[:, t, :], etop[:, t, :], masked[:, t, :]))
            route(dve.tensor_copy(eidx_f[:, :, :], eidx[:, :, :]))
            route(one_hot(esel, eidx_f, TOPK, E))
            route(dve.tensor_reduce(chosen[:, :, :], esel[:, :, :, :].rearrange("p t k e -> p t e k"), AX_X, ALU.add))
            route(dve.tensor_tensor(picked[:, :, :], chosen[:, :, :], score[:, :, :], ALU.mult))
            route(dve.tensor_reduce(tws[:, :], picked[:, :, :], AX_X, ALU.add))
            route(dve.tensor_scalar(twe[:, :], tws[:, :], 1e-20, None, ALU.add))
            route(dve.reciprocal(twr[:, :], twe[:, :]))
            route(dve.scalar_tensor_tensor(out=comb[:, SHARED * NT:].rearrange("p (e t) -> p t e", t=NT), in0=picked[:, :, :], scalar=ROUTED_SCALE,
                                           in1=twr[:, :].rearrange("p (t o) -> p t o", o=1).broadcast_to([P, NT, E]), op0=ALU.mult, op1=ALU.mult))
            dve.wait_ge(mo["ones"], 1)

            def accumulate(st, j, ej, b, first):
                dve.wait_ge(mo["down"], st + 1)
                if not first:
                    dve.wait_ge(mo["acc"], TB * (st - (B - 1)))
                for k in range(TB):
                    t = TB * b + k
                    dve.scalar_tensor_tensor(out=X[:, t, :], in0=bank[:, 4 + 2 * j + k // 2, (k % 2) * D:(k % 2 + 1) * D], scalar=csel[ej][:, t:t + 1],
                                             in1=X[:, t, :], op0=ALU.mult, op1=ALU.add).then_inc(mo["acc"], 1)

            def expert_pair(i, first=False):
                for n in range(2 * B):
                    st, j = 2 * B * i + n, n % 2
                    dve.wait_ge(mo["silu"], st + 1)
                    if not (first and n < 2):
                        dve.wait_ge(mo["hi"], st - 1)
                    dve.tensor_tensor(hid[j][:, :], sg[j][:, :], bank[:, 2 + j, :], ALU.mult).then_inc(mo["h"], 1)
                    if not (first and n == 0):
                        accumulate(st - 1, (j + 1) % 2, ((n - 1) % (2 * B)) // B, (n - 1) % B, first and n <= B)
                    if n % B == 0:
                        e = 2 * i + n // B
                        if not first:
                            dve.wait_ge(mo["acc"], TB * B * (e - 1))
                        dve.tensor_copy(csel[n // B][:, :], comb[:, bass.ds(e * NT, NT)]).then_inc(mo["sel"], 1)
                        dve.wait_ge(mo["sel"], e + 1)
                    dve.wait_ge(mo["hi"], st + 1)
                    dve.tensor_tensor(hhl[j][:, 1, :], hid[j][:, :], hhl[j][:, 0, :].bitcast(F32), ALU.subtract).then_inc(mo["lo"], 1)

            expert_pair(0, first=True)
            with dve.Fori(1, EA // 2) as i:
                expert_pair(i)
            accumulate(B * EA - 1, 1, 1, B - 1, False)


def kernel(**inputs):
    import numpy as _np
    import concourse.bacc as _bacc
    from concourse import mybir as _mybir
    from concourse.bass_utils import run_bass_kernel_spmd as _run

    def f(name):
        return _np.asarray(inputs[name])

    gate_up = _np.concatenate([_np.stack([f("L0_ffn_shared_gate_w"), f("L0_ffn_shared_up_w")]).reshape(2, SHARED, I, NC, P).transpose(1, 0, 2, 3, 4),
                               f("L0_ffn_experts_gate_up").reshape(E, 2, I, NC, P)])
    down = _np.concatenate([f("L0_ffn_shared_down_w").reshape(D, SHARED, I).transpose(1, 0, 2), f("L0_ffn_experts_down")])
    laid = {
        "x": f("x"),
        "ctx_t": f("ctx_1024").reshape(B * S, D).T,
        "pos": f("pos_BxS2"),
        "w_qkv": f("L0_attn_W_qkv"),
        "b_qkv_col": f("L0_attn_b_qkv")[0:2 * D].reshape(2 * NC, P).T,
        "b_v": f("L0_attn_b_qkv")[2 * D:],
        "w_out": f("L0_attn_W_out"),
        "b_out": f("L0_attn_b_out"),
        "rel_pad": _np.pad(f("L0_attn_rel_bias").T, ((0, 0), (MAX_REL - 1, RPW - (2 * MAX_REL + 1) - (MAX_REL - 1))), mode="edge"),
        "xw_q": f("L0_xattn_w_q"), "xb_q": f("L0_xattn_b_q").reshape(NC, P).T,
        "xw_k": f("L0_xattn_w_k"), "xb_k": f("L0_xattn_b_k").reshape(NC, P).T,
        "xw_v": f("L0_xattn_w_v"), "xb_v": f("L0_xattn_b_v"),
        "xw_o": f("L0_xattn_w_o"), "xb_o": f("L0_xattn_b_o"),
        "w_gate": f("L0_ffn_gate_weight").reshape(E, NC, P).transpose(2, 1, 0),
        "e_bias": f("L0_ffn_e_score_correction_bias"),
        "w_exp": _np.concatenate([gate_up.transpose(0, 4, 3, 1, 2).reshape(EA, P, NC * 2 * I), down.transpose(0, 2, 1)], axis=2),
    }
    nc = _bacc.Bacc("TRN2", target_bir_lowering=False, num_devices=1)
    arrays, args = {}, []
    for name, a in laid.items():
        a = _np.ascontiguousarray(a)
        arrays[f"in_{name}"] = a
        args.append(nc.dram_tensor(f"in_{name}", a.shape, _mybir.dt.from_np(a.dtype), kind="ExternalInput").ap())
    args.append(nc.dram_tensor("out_x", (B, S, D), _mybir.dt.float32, kind="ExternalOutput").ap())
    program(nc, *args)
    r = _run(nc, [arrays], core_ids=[0])
    return r.results[0]["out_x"]
```

```python
from contextlib import ExitStack

import numpy as np

import concourse.bass as bass
from concourse import mybir

F32 = mybir.dt.float32
F32R = mybir.dt.float32r
I32 = mybir.dt.int32
U32 = mybir.dt.uint32
ALU = mybir.AluOpType
ACT = mybir.ActivationFunctionType
AX_X = mybir.AxisListType.X

P = 128
B, S, D = 4, 512, 256
H, DK = 16, 16
NC = D // P
TB = S // P
NT = B * TB
HG = 4
G = H // HG
GW = HG * DK
U = G * B
MAX_REL = 256
TW = S - P + S
RPW = 1024
RAW_SCALE = float(DK) ** -0.5
EPS = 1e-5
BIG = 1e30
USES = HG * TB + 2
RING = 3
LOOPS = (U - 2) // RING
LOADS = 10
TAUS = 2 * TB
VECTOR_TILES = (1, 2, 4, 5, 6)
POOL_SHARE = [1 if t in VECTOR_TILES else 2 for t in range(TAUS)]
SHIFT_ROW = 64
THETA = 10000.0
INV_FREQ = (np.float32(THETA) ** (-(np.arange(DK // 2, dtype=np.float32) * np.float32(2.0)) / np.float32(DK))).astype(np.float32)
TWO_PI = 2.0 * np.pi
C1 = 6.28125
C2 = float(np.float32(TWO_PI - C1))
C3 = float(np.float32(TWO_PI - C1 - float(np.float32(TWO_PI - C1))))
ROUND = 1.5 * 2.0 ** 23
PI_SAFE = 3.1415925


E, TOPK, NGROUP, TOPG = 32, 6, 8, 4
GE = E // NGROUP
I = 128
SHARED = 2
EA = SHARED + E
WW = NC * 2 * I + D
ROUTED_SCALE = 2.5


def program(nc, x, ctx_t, pos, w_qkv, b_qkv_col, b_v, w_out, b_out, rel_pad, xw_q, xb_q, xw_k, xb_k, xw_v, xb_v, xw_o, xb_o, w_gate, e_bias, w_exp, out):
    with ExitStack() as stack:
        def sb(name, shape, dt=F32):
            return stack.enter_context(nc.sbuf_tensor(name, shape, dt))

        KB = 1024
        ARENA_AT = -(-nc.sbuf_base // KB) * KB
        stack.enter_context(nc.sbuf_tensor("arena", [P, 176 * KB + ARENA_AT - nc.sbuf_base], mybir.dt.uint8))

        def at(name, shape, kb, dt=F32):
            return nc.alloc_sbuf_tensor_at(name, shape, dt, offset=ARENA_AT + int(kb * KB))

        def sem(name):
            return stack.enter_context(nc.semaphore(name))

        def dram(name, shape):
            return nc.dram_tensor(name, shape, F32, kind="Internal")

        qk_hbm = {n: dram(f"{n}_hbm", (2, D, B * S)) for n in ("q1", "k1", "q2", "k2")}
        v_hbm = {n: dram(f"{n}_hbm", (B, G, P, TB, HG * 32)) for n in ("v1", "v2")}
        zero_hbm = dram("zero_hbm", (1, HG * S))
        rel_hbm = dram("rel_hbm", (H, RPW))

        bank = stack.enter_context(nc.psum_tensor("bank", [P, 8, 512], F32))

        X = at("X", [P, NT, D], 0)
        XN = at("XN", [P, NT, D], 16)
        ctx_sb = at("ctx_sb", [P, NC, B * S], 160)
        wqkv = sb("wqkv", [P, NC, 3 * D])
        wout = sb("wout", [P, NC, D])
        wxq = sb("wxq", [P, NC, D])
        wxk = sb("wxk", [P, NC, D])
        wxv = sb("wxv", [P, NC, D])
        wxo = sb("wxo", [P, NC, D])
        bqk_col = sb("bqk_col", [P, 4])
        bxq_col = sb("bxq_col", [P, NC])
        bxk_col = sb("bxk_col", [P, NC])
        bv_row = sb("bv_row", [P, D])
        bo_row = sb("bo_row", [P, D])
        bxv_row = sb("bxv_row", [P, D])
        bxo_row = sb("bxo_row", [P, D])
        ident = sb("ident", [P, P])
        flip = sb("flip", [P, P])
        ident_r = sb("ident_r", [P, P], F32R)
        mask_f = sb("mask_f", [P, 2, P])
        mask_r = sb("mask_r", [P, 2, P], F32R)
        pos_i = sb("pos_i", [P, NT], I32)
        pos_f = sb("pos_f", [P, NT])
        freq = sb("freq", [P, DK // 2])
        ang = [at(f"ang{n}", [P, NT, DK // 2], 152 + n / 2) for n in range(9)]
        trig = at("trig", [P, 2, NT, DK // 2, 2], 157)
        trig8 = at("trig8", [P, 2, NT, P // DK, DK], 120)
        cos_t = at("cos_t", [P, B * S], 32)
        sin_t = at("sin_t", [P, B * S], 40)
        stats = sb("stats", [P, NT, 6])
        mv = sb("mv", [P, NT, 2])
        vare = sb("vare", [P, NT])
        neghalf = sb("neghalf", [P, NT])
        rstd = sb("rstd", [P, NT])
        nT = at("nT", [P, NC, S], 112)
        oT = at("oT", [P, NC, S], 136)
        kf = at("kf", [P, NC, S], 48)
        swap = [at(f"swap{j}", [P, NC, S], (52, 120)[j]) for j in range(2)]
        rot1 = at("rot1", [P, NC, S], 56)
        rot2 = at("rot2", [P, NC, S], 60)
        hl = at("hl", [P, 4, 2, S], 88, F32R)
        nTq = at("nTq", [P, NC, S], 132)
        hlq = at("hlq", [P, NC, 2, S], 124, F32R)
        parts = {"ctx": hl, "self": hl, "xq": hlq}
        vt = at("vt", [P, TB, H, 32], 104)
        rel_in = at("rel_in", [H, RPW], 136)
        rel_max = sb("rel_max", [H, 1])
        rel_s = at("rel_s", [H, RPW], 140)
        rel_e = at("rel_e", [H, RPW], 144)
        nTf = at("nTf", [P, NC, S], 48)
        QU = [at(f"QU{j}", [P, HG, S], (66, 88, 104)[j], F32R) for j in range(RING)]
        KU = [at(f"KU{j}", [P, HG, S], (74, 96, 112)[j], F32R) for j in range(RING)]
        VU = [at(f"VU{j}", [P, TB, HG, 32], 82 + 2 * j) for j in range(RING)]
        toep = at("toep", [P, H * TW], 120)
        PT = at("PT", [P, 4, 2, S], 48)
        OS = at("OS", [P, S], 64)
        M = sb("M", [P, HG * TB])
        MR = sb("MR", [HG * TB, P], F32R)
        R = sb("R", [P, TB * HG])
        wgate = sb("wgate", [P, NC, E])
        iota_i = sb("iota_i", [P, E], I32)
        nT3 = at("nT3", [P, NC, S], 32)
        nhl = at("nhl", [P, NC, 2, B * S], 140, F32R)
        bias_e = at("bias_e", [P, E], 36)
        iota_e = at("iota_e", [P, E], 36.5)
        score = at("score", [P, NT, E], 37)
        sfc = at("sfc", [P, NT, E], 39)
        masked = at("masked", [P, NT, E], 41)
        gmax = at("gmax", [P, NT, NGROUP], 43)
        gtop = at("gtop", [P, NT, 8], 43.5)
        gidx = at("gidx", [P, NT, 8], 44, U32)
        gidx_f = at("gidx_f", [P, NT, 8], 44.5)
        gmask = at("gmask", [P, NT, NGROUP], 45)
        etop = at("etop", [P, NT, 8], 45.5)
        eidx = at("eidx", [P, NT, 8], 46, U32)
        eidx_f = at("eidx_f", [P, NT, 8], 46.5)
        tws = at("tws", [P, NT], 47)
        twe = at("twe", [P, NT], 47.125)
        twr = at("twr", [P, NT], 47.25)
        gsel = at("gsel", [P, NT, TOPG, NGROUP], 48)
        esel = at("esel", [P, NT, TOPK, E], 50)
        chosen = at("chosen", [P, NT, E], 62)
        picked = at("picked", [P, NT, E], 64)
        comb = at("comb", [P, EA * NT], 100)
        csel = [at(f"csel{j}", [P, NT], 102.5 + j / 4) for j in range(2)]
        wraw = [at(f"wraw{j}", [P, WW], 104 + 3 * j) for j in range(2)]
        whl = [at(f"whl{j}", [P, 2, WW], 110 + 6 * j, F32R) for j in range(2)]
        sg = [at(f"sg{j}", [P, S], 122 + 2 * j) for j in range(2)]
        hid = [at(f"hid{j}", [P, S], 126 + 2 * j) for j in range(2)]
        hhl = [at(f"hhl{j}", [P, 2, S], 130 + 4 * j, F32R) for j in range(2)]

        x_in, pos_in, rel_in_s = sem("x_in"), sem("pos_in"), sem("rel_in_s")
        w_in, ctx_in, ctx_w_in = sem("w_in"), sem("ctx_in"), sem("ctx_w_in")
        const_a, const_b, const_m = sem("const_a"), sem("const_b"), sem("const_m")
        ang_s, ang_act, trig_ready, trig_mm, trig_out = sem("ang_s"), sem("ang_act"), sem("trig_ready"), sem("trig_mm"), sem("trig_out")
        stack_zero, stack_init, zero_out = sem("stack_zero"), sem("stack_init"), sem("zero_out")
        rel_ready, rel_out, t_loaded = sem("rel_ready"), sem("rel_out"), sem("t_loaded")
        vt_init = sem("vt_init")

        NORM = ("stat", "mv", "var", "rstd", "xn", "tr", "trev")
        ROPE = ("kf", "swap", "rot1", "rot2", "rot")

        def sems(n, kinds):
            return {k: sem(f"{n}_{k}") for k in kinds}

        def sent(n, chunks, tiles=0):
            return {"sent": [sem(f"{n}_sent{m}") for m in range(chunks)], "vsent": [sem(f"{n}_vsent{k}") for k in range(tiles)]}

        pj = {
            "ctx": sent("ctx", NC, TB) | sems("ctx", ROPE + ("qk", "hi", "lo", "v", "vt")),
            "self": sent("self", 2 * NC, TB) | sems("self", NORM + ("trf", "trfev", "qk", "hi", "lo", "v", "vt")),
            "xq": sent("xq", NC) | sems("xq", NORM + ROPE + ("qk", "hi", "lo")),
            "moe": sems("moe", NORM),
        }
        out_s = {n: sems(n, ("tr", "trev", "mm", "add", "bias")) for n in ("o1", "o2")}

        def attn_sems(n):
            d = {k: sem(f"{n}_{k}") for k in ("swrote", "sread", "scored", "expd", "biased_p", "biased_v", "pvd", "oevac", "recip")}
            d["loaded"] = [sem(f"{n}_loaded{j}") for j in range(RING)]
            d["shift"] = [sem(f"{n}_shift{j}") for j in range(RING)]
            return d

        USES_SELF = ("rr", "rr", "rrr", "rr", "orr", "r", "m", "nnnn")
        USES_CAUSAL = ("rr", "rr", "rrr", "orr", "r", "m", "nnn", "nnn")

        a1 = {"s": attn_sems("a1"), "causal": False, "lag": 4, "uses": USES_SELF,  "q": qk_hbm["q1"], "k": qk_hbm["k1"], "v": v_hbm["v1"]}
        a2 = {"s": attn_sems("a2"), "causal": True, "lag": 2, "uses": USES_CAUSAL,  "q": qk_hbm["q2"], "k": qk_hbm["k2"], "v": v_hbm["v2"]}
        done_s = sem("done_s")
        mo = sems("moe", ("gate_in", "iota", "logits", "score", "nhi", "nlo", "route", "ones", "w_hi", "w_lo", "sel", "gu", "silu", "h", "hi", "lo", "down", "acc"))
        mo["w_raw"] = [sem(f"moe_w_raw{j}") for j in range(2)]

        block = stack.enter_context(nc.Block())

        x_tiles = x.rearrange("b (t p) d -> p (b t) d", p=P)
        out_tiles = out.rearrange("b (t p) d -> p (b t) d", p=P)

        def bcast(v):
            return v.rearrange("(a n) -> a n", a=1).broadcast_to([P, D])

        def wait(eng, s, value):
            if value > 0:
                eng.wait_ge(s, value)

        def wait_sent(eng, n, batches):
            for m in range({"ctx": NC, "self": 2 * NC, "xq": NC}[n]):
                wait(eng, pj[n]["sent"][m], 16 * batches)
            if n != "xq":
                for k in range(TB):
                    wait(eng, pj[n]["vsent"][k], 16 * batches)

        def batch(t, b):
            return t[:, :, b * S:(b + 1) * S]

        def is_unit(u, n):
            return isinstance(u, int) and u == n

        def ahead(a):
            return "".join(a["uses"]).count("n")

        def uses_of(a, u, tau):
            kinds = a["uses"][tau]
            if is_unit(u, 0):
                kinds = ("r" * ahead(a) if tau == 1 else "") + kinds.replace("o", "")
            if is_unit(u, U - 2):
                kinds = kinds.replace("n", "")
            if is_unit(u, U - 1):
                kinds = "o" if "o" in kinds else ""
            return kinds

        def first_use(a, u):
            if is_unit(u, 0):
                return USES - 1
            return USES * u + (USES - 2) + (0 if is_unit(u, U - 1) else ahead(a))

        def use_at(a, u, kind):
            before = "".join(uses_of(a, u, tau) for tau in range(TAUS)).index(kind)
            return first_use(a, u) + (before + 1)

        def slot(n):
            return 4 + n % RING

        def slot_of(a, u, n):
            if isinstance(u, int):
                return slot(first_use(a, u) + n)
            return slot(USES - 2 + ahead(a) + n)

        def add_relative(eng, a, u, tau, x, done):
            kb, h = tau // 2, 2 * (tau % 2) + x
            row = (u // B) * (HG * TW) + (h * TW + S - P - kb * P)
            e = PT[:, tau % 4, x, :]
            eng.tensor_tensor(e, e, toep[:, bass.ds(row, S)], ALU.mult).then_inc(done, 1)

        def units(eng, body):
            body(0, 0)
            with eng.Fori(0, LOOPS) as i:
                for r in range(1, RING + 1):
                    body(RING * i + r, r % RING)
            for u in range(RING * LOOPS + 1, U):
                body(u, u % RING)

        def norm_power(pool, n, b):
            s = pj[n]
            pool.wait_ge(s["var"], b + 1)
            pool.tensor_tensor(rstd[:, b * TB:(b + 1) * TB], vare[:, b * TB:(b + 1) * TB], neghalf[:, 0:TB], ALU.pow).then_inc(s["rstd"], 1)

        @block.sync
        def _(sp):
            sp.dma_start(pos_i[:, :], pos.rearrange("b (t p) -> p (b t)", p=P), allow_slow_non_contiguous=True).then_inc(pos_in, 16)
            for t, w in ((wxk, xw_k), (wxv, xw_v)):
                sp.dma_start(t[:, :, :], w.rearrange("(c p) n -> p c n", p=P)).then_inc(ctx_w_in, 16)
            sp.dma_start(bxk_col[:, :], xb_k).then_inc(ctx_w_in, 16)
            sp.dma_start(bxv_row[:, :], bcast(xb_v)).then_inc(ctx_w_in, 16)
            sp.dma_start(ctx_sb[:, :, :], ctx_t.rearrange("(c p) n -> p c n", p=P)).then_inc(ctx_in, 16)
            sp.dma_start(X[:, :, :], x_tiles).then_inc(x_in, 16)
            sp.dma_start(rel_in[:, :], rel_pad).then_inc(rel_in_s, 16)
            sp.dma_start(wqkv[:, :, :], w_qkv.rearrange("(c p) n -> p c n", p=P)).then_inc(w_in, 16)
            for t, w in ((wout, w_out), (wxq, xw_q), (wxo, xw_o)):
                sp.dma_start(t[:, :, :], w.rearrange("(c p) n -> p c n", p=P)).then_inc(w_in, 16)
            sp.dma_start(wgate[:, :, :], w_gate).then_inc(w_in, 16)
            for t, w in ((bqk_col, b_qkv_col), (bxq_col, xb_q)):
                sp.dma_start(t[:, :], w).then_inc(w_in, 16)
            for t, w in ((bv_row, b_v), (bo_row, b_out), (bxo_row, xb_o)):
                sp.dma_start(t[:, :], bcast(w)).then_inc(w_in, 16)
            sp.wait_ge(rel_ready, 3)
            sp.dma_start(rel_hbm.ap(), rel_e[:, :]).then_inc(rel_out, 16)

            def send_qk(n, names, b):
                s = pj[n]
                chunks = NC * len(names)
                for m in range(chunks):
                    sp.wait_ge(s["lo"], chunks * b + m + 1)
                    c = m % NC
                    dst = qk_hbm[names[m // NC]].ap()[:, c * P:(c + 1) * P, b * S:(b + 1) * S].rearrange("s p t -> p s t")
                    sp.dma_start(dst, parts[n][:, m, :, :].bitcast(F32)).then_inc(s["sent"][m], 16)

            def send_v(n, name, b):
                s = pj[n]
                for k in range(TB):
                    sp.wait_ge(s["vt"], 2 * b + k // 2 + 1)
                    sp.dma_start(v_hbm[name].ap()[b, :, :, k, :].rearrange("g p c -> p g c"),
                                 vt[:, k, :, :].rearrange("p (g h) e -> p g (h e)", g=G)).then_inc(s["vsent"][k], 16)

            def load_unit(a, u, j):
                s = a["s"]
                if not (isinstance(u, int) and u < RING):
                    sp.wait_ge(s["scored"], TAUS * (u - (RING - 1)))
                g, b = u // B, u % B

                def part(hbm, half):
                    ap = hbm.ap()[half].rearrange("(g h d) t -> d g h t", g=G, h=HG)
                    return ap[:, bass.ds(g, 1), :, bass.ds(b * S, S)].rearrange("d o h t -> d (o h) t")

                sp.dma_start(QU[j][SHIFT_ROW:SHIFT_ROW + 1, :, :].rearrange("o h t -> o (h t)").bitcast(F32), zero_hbm.ap()).then_inc(s["loaded"][j], 16)
                for row, half in enumerate((0, 0, 1, 1)):
                    sp.dma_start(QU[j][DK * row:DK * row + DK, :, :].bitcast(F32), part(a["q"], half)).then_inc(s["loaded"][j], 16)
                for row, half in enumerate((0, 1, 0, 1)):
                    sp.dma_start(KU[j][DK * row:DK * row + DK, :, :].bitcast(F32), part(a["k"], half)).then_inc(s["loaded"][j], 16)
                if not (isinstance(u, int) and u < RING):
                    sp.wait_ge(s["pvd"], TAUS * (u - (RING - 1)))
                v_src = a["v"].ap().rearrange("b g p k c -> p (b g) (k c)")[:, bass.ds(b * G + g, 1), :]
                sp.dma_start(VU[j][:, :, :, :].rearrange("p k h e -> p (k h e)"), v_src.rearrange("p o n -> p (o n)")).then_inc(s["loaded"][j], 16)

            def send_shift(a, u, j):
                s = a["s"]
                sp.wait_ge(s["sread"], USES - 1 if is_unit(u, 0) else use_at(a, u - 1, "m"))
                sp.dma_start(QU[j][SHIFT_ROW:SHIFT_ROW + 1, :, :].rearrange("o h (q t) -> o (h q) t", q=TB).bitcast(F32),
                             MR[:, :].bitcast(F32)).then_inc(s["shift"][j], 16)

            def attention(a):
                for u in range(1, RING):
                    sp.wait_ge(stack_init, 1 + u)
                    load_unit(a, u, u)
                    if u == 1:
                        send_shift(a, 0, 0)
                with sp.Fori(0, LOOPS) as i:
                    for r in range(RING):
                        send_shift(a, RING * i + (r + 1), (r + 1) % RING)
                        load_unit(a, RING * i + (r + RING), r)
                for u in range(RING * LOOPS, U):
                    if u + 1 < U:
                        send_shift(a, u + 1, (u + 1) % RING)
                    if u + RING < U:
                        load_unit(a, u + RING, u % RING)

            sp.wait_ge(stack_init, 1)
            sp.dma_start(zero_hbm.ap(), QU[0][SHIFT_ROW + 1:SHIFT_ROW + 2, :, :].rearrange("o h t -> o (h t)").bitcast(F32)).then_inc(zero_out, 16)
            for b in range(B):
                send_qk("ctx", ["k2"], b)
                send_v("ctx", "v2", b)
            for b in range(B):
                if b == B - 1:
                    wait_sent(sp, "self", 1)
                    sp.wait_ge(zero_out, 16)
                    load_unit(a1, 0, 0)
                send_qk("self", ["q1", "k1"], b)
                send_v("self", "v1", b)
            wait_sent(sp, "self", B)
            sp.wait_ge(pj["self"]["v"], 2 * B)
            attention(a1)
            wait_sent(sp, "ctx", B)
            sp.wait_ge(a1["s"]["pvd"], TAUS * U)
            for b in range(B):
                if b == B - 1:
                    wait_sent(sp, "xq", 1)
                    load_unit(a2, 0, 0)
                send_qk("xq", ["q2"], b)
            wait_sent(sp, "xq", B)
            sp.wait_ge(pj["xq"]["qk"], NC * B)
            attention(a2)
            sp.wait_ge(a2["s"]["oevac"], U)
            sp.dma_start(bias_e[:, :], e_bias.rearrange("(a n) -> a n", a=1).broadcast_to([P, E])).then_inc(mo["gate_in"], 16)
            w_src = w_exp.rearrange("e p n -> p e n")

            def load_expert(e, j, first=False):
                if not first:
                    sp.wait_ge(mo["w_hi"], e - 1)
                    sp.wait_ge(mo["w_lo"], e - 1)
                sp.dma_start(wraw[j][:, :], w_src[:, bass.ds(e, 1), :].rearrange("p o n -> p (o n)")).then_inc(mo["w_raw"][j], 16)

            for j in range(2):
                load_expert(j, j, first=True)
            with sp.Fori(1, EA // 2) as i:
                for j in range(2):
                    load_expert(2 * i + j, j)
            sp.wait_ge(mo["acc"], TB * B * EA)
            sp.dma_start(out_tiles, X[:, :, :]).then_inc(done_s, 16)
            sp.wait_ge(done_s, 16)

        @block.gpsimd
        def _(pool):
            for n, f in enumerate(INV_FREQ):
                pool.memset(freq[:, n:n + 1], float(f)).then_inc(const_m, 1)
            pool.memset(neghalf[:, :], -0.5).then_inc(const_m, 1)
            pool.iota(iota_i[:, :], pattern=[[1, E]], base=0, channel_multiplier=0).then_inc(mo["iota"], 1)
            pool.memset(ident[:, :], 0.0).then_inc(const_a, 1)
            pool.memset(mask_f[:, :, :], 0.0).then_inc(const_a, 1)
            pool.memset(flip[:, :], 0.0).then_inc(const_a, 1)
            pool.wait_ge(const_a, 3)
            pool.affine_select(out=flip[:, :], in_=flip[:, :], compare_op=ALU.not_equal, fill=1.0, base=-(P - 1),
                               pattern=[[1, P]], channel_multiplier=1).then_inc(const_b, 1)
            pool.affine_select(out=ident[:, :], in_=ident[:, :], compare_op=ALU.not_equal, fill=1.0, base=0,
                               pattern=[[-1, P]], channel_multiplier=1).then_inc(const_b, 1)
            pool.affine_select(out=mask_f[:, 0, :], in_=mask_f[:, 0, :], compare_op=ALU.is_ge, fill=-BIG, base=0,
                               pattern=[[-1, P]], channel_multiplier=1).then_inc(const_b, 1)
            pool.affine_select(out=mask_f[:, 1, :], in_=mask_f[:, 1, :], compare_op=ALU.is_ge, fill=-BIG, base=0,
                               pattern=[[1, P]], channel_multiplier=-1).then_inc(const_b, 1)
            pool.memset(vt[:, :, :, :], 1.0).then_inc(vt_init, 1)

            def rotate_cos(n, b):
                s = pj[n]
                for m in range(NC):
                    wait(pool, s["kf"], NC * b + m + 1)
                    wait(pool, s["rot"], NC * (b - 1) + m + 1)
                    pool.tensor_tensor(rot1[:, m, :], kf[:, m, :], cos_t[:, b * S:(b + 1) * S], ALU.mult).then_inc(s["rot1"], 1)

            inits = {"n": 0}

            def init_stack(j):
                wait(pool, stack_init, inits["n"])
                pool.memset(KU[j][64:P, :, :].bitcast(F32), 0.0).then_inc(stack_zero, 1)
                pool.memset(QU[j][64:P, :, :].bitcast(F32), 0.0).then_inc(stack_zero, 1)
                inits["n"] += 1
                pool.wait_ge(stack_zero, 2 * inits["n"])
                pool.memset(KU[j][SHIFT_ROW:SHIFT_ROW + 1, :, :].bitcast(F32), 1.0).then_inc(stack_init, 1)

            pool.wait_ge(const_m, 1 + DK // 2)
            pool.wait_ge(vt_init, 1)
            pool.wait_ge(const_b, 4)
            init_stack(0)
            pool.wait_ge(stack_init, 1)
            for b in range(B):
                rotate_cos("ctx", b)
                norm_power(pool, "self", b)

            def add_bias(n, row):
                pool.tensor_tensor(X[:, :, :], X[:, :, :], row[:, :].rearrange("p (o d) -> p o d", o=1).broadcast_to([P, NT, D]), ALU.add)\
                    .then_inc(out_s[n]["bias"], 1)

            def load_toeplitz(g):
                src = bass.AP(rel_hbm, g * (HG * RPW), [[1, P], [RPW, HG], [1, TW]])
                dst = toep[:, g * (HG * TW):(g + 1) * (HG * TW)]
                pool.dma_start(dst.rearrange("p (r y) -> p r y", y=TW), src).then_inc(t_loaded, 16)

            pool.wait_ge(rel_out, 16)
            pool.wait_ge(trig_mm, 2 * B)
            wait_sent(pool, "ctx", B)
            for g in range(G):
                wait_sent(pool, "self", max(g - 1, 0))
                load_toeplitz(g)
            pool.wait_ge(pj["self"]["xn"], NT)
            pool.wait_ge(w_in, 16 * 10)
            for m in range(2 * NC):
                pool.wait_ge(pj["self"]["sent"][m], 16 * B)
            init_stack(1)
            wait_sent(pool, "self", B)
            pool.wait_ge(pj["self"]["v"], 2 * B)
            init_stack(2)
            pool.wait_ge(stack_init, RING)
            pool.wait_ge(t_loaded, 16 * G)

            def relative_bias(u):
                s = a1["s"]
                for tau in range(TAUS):
                    pool.wait_ge(s["expd"], TAUS * u + (tau + 1))
                    for x in range(POOL_SHARE[tau]):
                        add_relative(pool, a1, u, tau, x, s["biased_p"])

            units(pool, lambda u, j: relative_bias(u))
            add_bias("o1", bo_row)
            norm_power(pool, "xq", 0)
            for b in range(B):
                if b + 1 < B:
                    norm_power(pool, "xq", b + 1)
                rotate_cos("xq", b)
            wait_sent(pool, "xq", B)
            add_bias("o2", bxo_row)
            pool.wait_ge(a2["s"]["oevac"], U)
            pool.memset(comb[:, 0:SHARED * NT], 1.0).then_inc(mo["ones"], 1)
            for b in range(B):
                norm_power(pool, "moe", b)
                for c in range(NC):
                    pool.wait_ge(mo["nhi"], NC * b + c + 1)
                    pool.tensor_tensor(nhl[:, c, 1, b * S:(b + 1) * S], nT3[:, c, :], nhl[:, c, 0, b * S:(b + 1) * S].bitcast(F32), ALU.subtract).then_inc(mo["nlo"], 1)

            def split_low(e, j):
                pool.wait_ge(mo["w_hi"], e + 1)
                pool.tensor_tensor(whl[j][:, 1, :], wraw[j][:, :], whl[j][:, 0, :].bitcast(F32), ALU.subtract).then_inc(mo["w_lo"], 1)

            with pool.Fori(0, EA // 2) as i:
                for j in range(2):
                    split_low(2 * i + j, j)

        @block.scalar
        def _(act):
            act.wait_ge(const_b, 4)
            act.activation(ident_r[:, :], ident[:, :], ACT.Copy).then_inc(const_m, 1)
            act.activation(mask_r[:, :, :], mask_f[:, :, :], ACT.Copy).then_inc(const_m, 1)
            act.wait_ge(ang_s, 8)
            act.activation(ang[7][:, :, :], ang[4][:, :, :], ACT.Sin).then_inc(ang_act, 1)
            act.wait_ge(ang_s, 12)
            act.activation(ang[8][:, :, :], ang[6][:, :, :], ACT.Sin).then_inc(ang_act, 1)
            for b in range(B):
                for w, dst in ((0, cos_t), (1, sin_t)):
                    n = 2 * b + w
                    act.wait_ge(trig_mm, n + 1)
                    act.activation(dst[:, b * S:(b + 1) * S], bank[:, n, :], ACT.Copy).then_inc(trig_out, 1)

            act.wait_ge(rel_ready, 2)
            act.activation(rel_e[:, :], rel_s[:, :], ACT.Exp).then_inc(rel_ready, 1)

            def kf_evac(n, b, col, first_bank):
                s = pj[n]
                for m in range(NC):
                    act.wait_ge(s["qk"], NC * b + m + 1)
                    wait(act, s["rot"], NC * (b - 1) + m + 1)
                    act.activation(kf[:, m, :], bank[:, first_bank + m, :], ACT.Identity, bias=col[:, m:m + 1]).then_inc(s["kf"], 1)

            def hi_rot(n, b):
                s = pj[n]
                for m in range(NC):
                    act.wait_ge(s["rot"], NC * b + m + 1)
                    wait(act, s["sent"][m], 16 * b)
                    act.activation(parts[n][:, m, 0, :], swap[b % 2][:, m, :], ACT.Copy).then_inc(s["hi"], 1)

            act.wait_ge(ctx_w_in, 64)
            for b in range(B):
                kf_evac("ctx", b, bxk_col, 0)
                hi_rot("ctx", b)
            s = pj["self"]
            act.wait_ge(w_in, 16 * 10)
            for b in range(B):
                for c in range(NC):
                    act.wait_ge(s["tr"], NC * b + c + 1)
                    act.activation(nT[:, c, :], bank[:, 4 + c, :], ACT.Copy).then_inc(s["trev"], 1)
                if b == 0:
                    wait_sent(act, "ctx", B)
                for c in range(NC):
                    act.wait_ge(s["trf"], NC * b + c + 1)
                    wait(act, s["v"], 2 * b)
                    act.activation(nTf[:, c, :], bank[:, 4 + c, :], ACT.Copy).then_inc(s["trfev"], 1)
                for m in range(4):
                    act.wait_ge(s["qk"], 4 * b + m + 1)
                    wait(act, s["sent"][m], 16 * b)
                    act.activation(hl[:, m, 0, :], bank[:, m, :], ACT.Identity, bias=bqk_col[:, m:m + 1]).then_inc(s["hi"], 1)

            def o_evac(a, u):
                s = a["s"]
                act.wait_ge(s["pvd"], TAUS * u + TAUS)
                if not (isinstance(u, int) and u == 0):
                    act.wait_ge(s["swrote"], use_at(a, u, "o"))
                act.activation(OS[:, :], bank[:, 7, :], ACT.Copy).then_inc(s["oevac"], 1)

            def unit(a, u, j):
                s = a["s"]
                first = isinstance(u, int) and u == 0
                for tau in range(TAUS):
                    if tau == a["lag"] - 1 and not first:
                        o_evac(a, u - 1)
                    q0 = (tau // 2) * P if a["causal"] else 0
                    act.wait_ge(s["scored"], TAUS * u + (tau + 1))
                    if not (first and tau < 4):
                        act.wait_ge(s["pvd"], TAUS * u + (tau - 3))
                    act.activation(PT[:, tau % 4, :, q0:S], bank[:, 2 * (tau % 2):2 * (tau % 2) + 2, q0:S], ACT.Exp, scale=RAW_SCALE).then_inc(s["expd"], 1)

            def attention(a):
                units(act, lambda u, j: unit(a, u, j))
                o_evac(a, U - 1)

            def out_evac(n, b):
                s = out_s[n]
                for c in range(NC):
                    act.wait_ge(s["tr"], NC * b + c + 1)
                    wait(act, s["mm"], 2 * b)
                    act.activation(oT[:, c, :], bank[:, c, :], ACT.Copy).then_inc(s["trev"], 1)

            attention(a1)

            def query_evac(b):
                s = pj["xq"]
                for c in range(NC):
                    act.wait_ge(s["tr"], NC * b + c + 1)
                    wait(act, s["qk"], NC * b)
                    act.activation(nTq[:, c, :], bank[:, 4 + c, :], ACT.Copy).then_inc(s["trev"], 1)
                kf_evac("xq", b, bxq_col, 6)

            def moe_evac(b):
                s = pj["moe"]
                for c in range(NC):
                    act.wait_ge(s["tr"], NC * b + c + 1)
                    wait(act, mo["logits"], b)
                    wait(act, mo["nlo"], NC * (b - 1) + c + 1)
                    act.activation(nT3[:, c, :], bank[:, 4 + c, :], ACT.Copy).then_inc(s["trev"], 1)
                for c in range(NC):
                    act.wait_ge(s["trev"], NC * b + c + 1)
                    act.activation(nhl[:, c, 0, b * S:(b + 1) * S], nT3[:, c, :], ACT.Copy).then_inc(mo["nhi"], 1)
                act.wait_ge(mo["logits"], b + 1)
                act.activation(score[:, b * TB:(b + 1) * TB, :], bank[:, 6 + b % 2, 0:P].rearrange("p (t e) -> p t e", e=E), ACT.Sigmoid).then_inc(mo["score"], 1)

            out_evac("o1", 0)
            for b in range(B):
                if b + 1 < B:
                    out_evac("o1", b + 1)
                if b >= 1:
                    hi_rot("xq", b - 1)
                query_evac(b)
            hi_rot("xq", B - 1)
            attention(a2)
            out_evac("o2", 0)
            for b in range(B):
                if b + 1 < B:
                    out_evac("o2", b + 1)
                moe_evac(b)

            def split_high(e, j, k, first=False):
                act.wait_ge(mo["w_raw"][j], 16 * k + 16)
                if not first:
                    act.wait_ge(mo["down"], B * (e - 1))
                act.activation(whl[j][:, 0, :], wraw[j][:, :], ACT.Copy).then_inc(mo["w_hi"], 1)

            def expert_pair(i, first=False, last=False):
                for n in range(2 * B):
                    st, j = 2 * B * i + n, n % 2
                    young = first and n < 2
                    act.wait_ge(mo["gu"], 2 * st + 1)
                    if not young:
                        act.wait_ge(mo["h"], st - 1)
                    act.activation(sg[j][:, :], bank[:, j, :], ACT.Silu).then_inc(mo["silu"], 1)
                    act.wait_ge(mo["h"], st + 1)
                    if not young:
                        act.wait_ge(mo["down"], st - 1)
                    act.activation(hhl[j][:, 0, :], hid[j][:, :], ACT.Copy).then_inc(mo["hi"], 1)
                    if n == 1 and not first:
                        split_high(2 * i + 1, 1, i)
                    if n == B + 1 and not last:
                        split_high(2 * i + 2, 0, i + 1)

            split_high(0, 0, 0, first=True)
            split_high(1, 1, 0, first=True)
            expert_pair(0, first=True)
            with act.Fori(1, EA // 2 - 1) as i:
                expert_pair(i)
            expert_pair(EA // 2 - 1, last=True)

        @block.tensor
        def _(pe):
            pe.wait_ge(const_b, 4)
            pe.wait_ge(trig_ready, 2)
            for b in range(B):
                for w in range(2):
                    for t in range(TB):
                        tr = pe.transpose(bank[:, 2 * b + w, t * P:(t + 1) * P], trig8[:, w, TB * b + t, :, :].rearrange("p r f -> p (r f)"), ident[:, :])
                    tr.then_inc(trig_mm, 1)

            def feature_major(n, wt, col0, chunks, src, b, first_bank, freed, part=None):
                s = pj[n]
                for m in part or range(chunks):
                    wait(pe, freed, chunks * (b - 1) + m + 1)
                    for c in range(NC):
                        mm = pe.matmul(bank[:, first_bank + m, :], wt[:, c, col0 + m * P:col0 + (m + 1) * P], src[:, c, :], start=(c == 0), stop=(c == NC - 1))
                    mm.then_inc(s["qk"], 1)

            def token_major(done, wt, col0, src, b, first_bank, freed):
                for k in range(2):
                    wait(pe, freed, 2 * (b - 1) + k + 1)
                    for t in range(2):
                        tok = (2 * k + t) * P
                        for c in range(NC):
                            mm = pe.matmul(bank[:, first_bank + k, t * D:(t + 1) * D], src[:, c, tok:tok + P], wt[:, c, col0:col0 + D],
                                           start=(c == 0), stop=(c == NC - 1))
                    mm.then_inc(done, 1)

            def transposes(src, b, first_bank, done, ready, per_tile, freed, perm=ident, before=1):
                for c in range(NC):
                    wait(pe, freed, NC * (b - before) + c + 1)
                    for t in range(TB):
                        if c == 0 and per_tile:
                            pe.wait_ge(ready, TB * b + t + 1)
                        tr = pe.transpose(bank[:, first_bank + c, t * P:(t + 1) * P], src[:, b * TB + t, c * P:(c + 1) * P], perm[:, :])
                    tr.then_inc(done, 1)

            pe.wait_ge(trig_out, 2 * B)
            pe.wait_ge(ctx_in, 16)
            pe.wait_ge(ctx_w_in, 64)
            for b in range(B):
                feature_major("ctx", wxk, 0, NC, batch(ctx_sb, b), b, 0, pj["ctx"]["kf"])
                token_major(pj["ctx"]["v"], wxv, 0, batch(ctx_sb, b), b, 2, pj["ctx"]["vt"])
            s = pj["self"]
            pe.wait_ge(w_in, 16 * 10)
            for b in range(B):
                transposes(XN, b, 4, s["tr"], s["xn"], True, s["trfev"])
                pe.wait_ge(s["trev"], NC * b + 2)
                if b == 0:
                    pe.wait_ge(pj["ctx"]["kf"], NC * B)
                    pe.wait_ge(pj["ctx"]["vt"], 2 * B)
                feature_major("self", wqkv, 0, 4, nT, b, 0, s["lo"], part=[0])
                transposes(XN, b, 4, s["trf"], None, False, s["trev"], perm=flip, before=0)
                feature_major("self", wqkv, 0, 4, nT, b, 0, s["lo"], part=[1])
                pe.wait_ge(s["trfev"], NC * b + 2)
                feature_major("self", wqkv, 0, 4, nTf, b, 0, s["lo"], part=[2, 3])
                token_major(s["v"], wqkv, 2 * D, nTf, b, 6, s["vt"])

            def row_scores(a, dst, j, h, qb):
                keys = P * (qb + 1) if a["causal"] else S
                q = slice(qb * P, (qb + 1) * P)
                mm = pe.matmul(dst[:, 0:keys], QU[j][:, h, q], KU[j][:, h, 0:keys], start=True, stop=not a["causal"])
                if a["causal"]:
                    mm = pe.matmul(dst[:, q], ident_r[:, :], mask_r[:, 0, :], start=False, stop=True)
                mm.then_inc(a["s"]["swrote"], 1)

            def maxima_rows(a, dst):
                pe.transpose(dst[0:HG * TB, 0:P], M[:, :], ident[:, :]).then_inc(a["s"]["swrote"], 1)

            def outputs_token_major(a, u, dst):
                pe.wait_ge(a["s"]["oevac"], u + 1)
                for qb in range(TB):
                    tr = pe.transpose(dst[:, qb * P:(qb + 1) * P], OS[:, qb * P:(qb + 1) * P], ident[:, :])
                tr.then_inc(a["s"]["swrote"], 1)

            def key_scores(a, u, tau, x, j):
                s = a["s"]
                kb, h = tau // 2, 2 * (tau % 2) + x
                q0 = kb * P if a["causal"] else 0
                if x == 0 and not (isinstance(u, int) and u == 0 and tau < 2):
                    pe.wait_ge(s["expd"], TAUS * u + (tau - 1))
                dst = bank[:, 2 * (tau % 2) + x, :]
                mm = pe.matmul(dst[:, q0:S], KU[j][:, h, kb * P:(kb + 1) * P], QU[j][:, h, q0:S], start=True, stop=not a["causal"])
                if a["causal"]:
                    mm = pe.matmul(dst[:, q0:q0 + P], ident_r[:, :], mask_r[:, 1, :], start=False, stop=True)
                if x == 1:
                    mm.then_inc(s["scored"], 1)

            def weigh(a, u, tau, j):
                s = a["s"]
                kb, half = tau // 2, tau % 2
                q0 = kb * P if a["causal"] else 0
                if tau == 0 and not (isinstance(u, int) and u == 0):
                    pe.wait_ge(s["oevac"], u)
                if a["causal"]:
                    pe.wait_ge(s["expd"], TAUS * u + (tau + 1))
                else:
                    pe.wait_ge(s["biased_p"], sum(POOL_SHARE) * u + sum(POOL_SHARE[:tau + 1]))
                    shared = sum(t <= tau for t in VECTOR_TILES)
                    if not (isinstance(u, int) and u == 0 and shared == 0):
                        pe.wait_ge(s["biased_v"], len(VECTOR_TILES) * u + shared)
                for x in range(2):
                    h = 2 * half + x
                    mm = pe.matmul(bank[32 * h:32 * h + 32, 7, q0:S], VU[j][:, kb, h, :], PT[:, tau % 4, x, q0:S],
                                   start=(kb == 0), stop=(kb == TB - 1), tile_position=(0, 32 * h))
                mm.then_inc(s["pvd"], 1)

            def unit(a, u, j):
                s = a["s"]
                first = isinstance(u, int) and u == 0
                last = isinstance(u, int) and u == U - 1
                n = 0
                done = {"r": 0 if first else ahead(a), "n": 0}
                later = {"r": 1, "n": 2}

                def ring_use(kind):
                    nonlocal n
                    pe.wait_ge(s["sread"], first_use(a, u) + (n - (RING - 1)))
                    dst = bank[:, slot_of(a, u, n), :]
                    if kind == "o":
                        outputs_token_major(a, u - 1, dst)
                    elif kind == "m":
                        pe.wait_ge(s["sread"], first_use(a, u) + n)
                        maxima_rows(a, dst)
                    else:
                        v, jv = u + later[kind], (j + later[kind]) % RING
                        if done[kind] == 0:
                            pe.wait_ge(s["loaded"][jv], 16 * LOADS * (v // RING) + 16 * LOADS)
                        row_scores(a, dst, jv, done[kind] // TB, done[kind] % TB)
                        done[kind] += 1
                    n += 1

                for tau in range(TAUS):
                    uses = list(uses_of(a, u, tau))
                    if tau >= a["lag"]:
                        weigh(a, u, tau - a["lag"], j)
                    elif not first:
                        weigh(a, u - 1, TAUS + tau - a["lag"], (j - 1) % RING)
                    if tau == 0:
                        pe.wait_ge(s["shift"][j], 16 * (u // RING) + 16)
                    key_scores(a, u, tau, 0, j)
                    if uses:
                        ring_use(uses.pop(0))
                    key_scores(a, u, tau, 1, j)
                    for kind in uses:
                        ring_use(kind)
                if last:
                    for tau in range(TAUS - a["lag"], TAUS):
                        weigh(a, u, tau, j)

            def attention(a):
                s = a["s"]
                pe.wait_ge(s["loaded"][0], 16 * LOADS)
                for n in range(HG * TB):
                    wait(pe, s["sread"], n - (RING - 1))
                    row_scores(a, bank[:, slot(n), :], 0, n // TB, n % TB)
                pe.wait_ge(s["sread"], HG * TB)
                maxima_rows(a, bank[:, slot(HG * TB), :])
                units(pe, lambda u, j: unit(a, u, j))
                outputs_token_major(a, U - 1, bank[:, slot_of(a, U - 1, 1), :])

            pe.wait_ge(s["lo"], 4 * B)
            pe.wait_ge(s["vt"], 2 * B)
            pe.wait_ge(const_m, 3 + DK // 2)
            pe.wait_ge(stack_init, 1)
            attention(a1)

            def out_projection(n, wt, b):
                o = out_s[n]
                transposes(XN, b, 0, o["tr"], None, False, o["trev"])
                pe.wait_ge(o["trev"], NC * b + 2)
                token_major(o["mm"], wt, 0, oT, b, 2, o["add"])

            def queries(b):
                s = pj["xq"]
                transposes(XN, b, 4, s["tr"], s["xn"], True, s["trev"])
                pe.wait_ge(s["trev"], NC * b + 2)
                feature_major("xq", wxq, 0, NC, nTq, b, 6, s["kf"])

            def routing_logits(b):
                transposes(XN, b, 4, pj["moe"]["tr"], pj["moe"]["xn"], True, pj["moe"]["trev"])
                wait(pe, mo["score"], b - 1)
                for k in range(TB):
                    for c in range(NC):
                        pe.wait_ge(pj["moe"]["trev"], NC * b + c + 1)
                        mm = pe.matmul(bank[:, 6 + b % 2, k * E:(k + 1) * E], nT3[:, c, k * P:(k + 1) * P], wgate[:, c, :],
                                       start=(c == 0), stop=(c == NC - 1))
                mm.then_inc(mo["logits"], 1)

            pe.wait_ge(a1["s"]["sread"], USES * U)
            out_projection("o1", wout, 0)
            for b in range(B):
                if b + 1 < B:
                    out_projection("o1", wout, b + 1)
                queries(b)
            pe.wait_ge(pj["xq"]["kf"], NC * B)
            attention(a2)
            pe.wait_ge(a2["s"]["sread"], USES * U)
            out_projection("o2", wxo, 0)
            for b in range(B):
                if b + 1 < B:
                    out_projection("o2", wxo, b + 1)
                routing_logits(b)

            PRODUCTS = ((0, 0), (0, 1), (1, 0))

            def gate_up(st, j, wj, b, first):
                if not first:
                    pe.wait_ge(mo["h"], st - 1)
                for half in range(2):
                    n = 0
                    for c in range(NC):
                        for x, y in PRODUCTS:
                            col = c * 2 * I + half * I
                            mm = pe.matmul(bank[:, 2 * half + j, :], whl[wj][:, x, col:col + I], nhl[:, c, y, b * S:(b + 1) * S],
                                           start=(n == 0), stop=(n == 3 * NC - 1))
                            n += 1
                    mm.then_inc(mo["gu"], 1)

            def down(st, j, wj, first):
                pe.wait_ge(mo["hi"], st + 1)
                pe.wait_ge(mo["lo"], st + 1)
                if not first:
                    pe.wait_ge(mo["acc"], TB * (st - 1))
                for k in range(TB):
                    for n, (x, y) in enumerate(PRODUCTS):
                        mm = pe.matmul(bank[:, 4 + 2 * j + k // 2, (k % 2) * D:(k % 2 + 1) * D], hhl[j][:, x, k * P:(k + 1) * P],
                                       whl[wj][:, y, NC * 2 * I:WW], start=(n == 0), stop=(n == 2))
                mm.then_inc(mo["down"], 1)

            def expert_pair(i, first=False):
                for n in range(2 * B):
                    st, j = 2 * B * i + n, n % 2
                    if n % B == 0:
                        pe.wait_ge(mo["w_hi"], 2 * i + (n // B + 1))
                        pe.wait_ge(mo["w_lo"], 2 * i + (n // B + 1))
                    gate_up(st, j, n // B, n % B, first and n < 2)
                    if not (first and n == 0):
                        down(st - 1, (j + 1) % 2, ((n - 1) % (2 * B)) // B, first and n < 3)

            pe.wait_ge(mo["nlo"], NC * B)
            pe.wait_ge(mo["score"], B)
            pe.wait_ge(out_s["o2"]["add"], 2 * B)
            expert_pair(0, first=True)
            with pe.Fori(1, EA // 2) as i:
                expert_pair(i)
            down(B * EA - 1, 1, 1, False)

        @block.vector
        def _(dve):
            count = {"ang": 0}

            def step(ins):
                count["ang"] += 1
                ins.then_inc(ang_s, 1)
                dve.wait_ge(ang_s, count["ang"])

            dve.wait_ge(pos_in, 16)
            step(dve.tensor_copy(pos_f[:, :], pos_i[:, :]))
            dve.wait_ge(const_m, 1 + DK // 2)
            step(dve.tensor_tensor(ang[0][:, :, :], pos_f[:, :].rearrange("p (t o) -> p t o", o=1).broadcast_to([P, NT, DK // 2]),
                                   freq[:, :].rearrange("p (o f) -> p o f", o=1).broadcast_to([P, NT, DK // 2]), ALU.mult))
            step(dve.tensor_scalar(ang[1][:, :, :], ang[0][:, :, :], 1.0 / TWO_PI, ROUND, ALU.mult, ALU.add))
            step(dve.tensor_scalar(ang[2][:, :, :], ang[1][:, :, :], -ROUND, None, ALU.add))
            step(dve.scalar_tensor_tensor(out=ang[3][:, :, :], in0=ang[2][:, :, :], scalar=-C1, in1=ang[0][:, :, :], op0=ALU.mult, op1=ALU.add))
            step(dve.scalar_tensor_tensor(out=ang[5][:, :, :], in0=ang[2][:, :, :], scalar=-C2, in1=ang[3][:, :, :], op0=ALU.mult, op1=ALU.add))
            step(dve.scalar_tensor_tensor(out=ang[1][:, :, :], in0=ang[2][:, :, :], scalar=-C3, in1=ang[5][:, :, :], op0=ALU.mult, op1=ALU.add))
            step(dve.tensor_scalar(ang[4][:, :, :], ang[1][:, :, :], PI_SAFE, -PI_SAFE, ALU.min, ALU.max))
            step(dve.tensor_scalar(ang[3][:, :, :], ang[1][:, :, :], float(np.pi / 2), None, ALU.add))
            step(dve.tensor_scalar(ang[5][:, :, :], ang[3][:, :, :], float(np.pi), -TWO_PI, ALU.is_gt, ALU.mult))
            step(dve.tensor_tensor(ang[2][:, :, :], ang[3][:, :, :], ang[5][:, :, :], ALU.add))
            step(dve.tensor_scalar(ang[6][:, :, :], ang[2][:, :, :], PI_SAFE, -PI_SAFE, ALU.min, ALU.max))
            dve.wait_ge(ang_act, 2)
            step(dve.tensor_copy(trig[:, 0, :, :, :], ang[8][:, :, :].rearrange("p t (f o) -> p t f o", o=1).broadcast_to([P, NT, DK // 2, 2])))
            step(dve.tensor_scalar(trig[:, 1, :, :, 0], ang[7][:, :, :], -1.0, None, ALU.mult))
            step(dve.tensor_scalar(trig[:, 1, :, :, 1], ang[7][:, :, :], 1.0, None, ALU.mult))
            for w in range(2):
                dve.tensor_copy(trig8[:, w, :, :, :], trig[:, w, :, :, :].rearrange("p t (o f) e -> p t o (f e)", o=1).broadcast_to([P, NT, P // DK, DK]))\
                    .then_inc(trig_ready, 1)
            dve.wait_ge(rel_in_s, 16)
            dve.tensor_reduce(rel_max[:, :], rel_in[:, :], AX_X, ALU.max).then_inc(rel_ready, 1)
            dve.wait_ge(rel_ready, 1)
            dve.tensor_scalar(rel_s[:, :], rel_in[:, :], rel_max[:, 0:1], None, ALU.subtract).then_inc(rel_ready, 1)

            def layer_norm(n, dst, b):
                s = pj[n]
                for k in range(TB):
                    t = TB * b + k
                    dve.bn_stats(stats[:, t, :], X[:, t, :]).then_inc(s["stat"], 1)
                for k in range(TB):
                    t = TB * b + k
                    dve.wait_ge(s["stat"], t + 1)
                    dve.bn_aggr(mv[:, t, :], stats[:, t, :]).then_inc(s["mv"], 1)
                tiles = slice(TB * b, TB * (b + 1))
                dve.wait_ge(s["mv"], TB * (b + 1))
                dve.tensor_scalar(vare[:, tiles], mv[:, tiles, 1], EPS, None, ALU.add).then_inc(s["var"], 1)

            def normalise(n, dst, b):
                s = pj[n]
                dve.wait_ge(s["rstd"], b + 1)
                for k in range(TB):
                    t = TB * b + k
                    dve.tensor_scalar(dst[:, t, :], X[:, t, :], mv[:, t, 0:1], rstd[:, t:t + 1], ALU.subtract, ALU.mult).then_inc(s["xn"], 1)

            def rotate(n, b):
                s = pj[n]
                for m in range(NC):
                    dve.wait_ge(s["kf"], NC * b + m + 1)
                    wait(dve, s["lo"], NC * (b - 2) + m + 1)
                    dve.stream_shuffle(swap[b % 2][:, m, :], kf[:, m, :], [p ^ 1 for p in range(32)]).then_inc(s["swap"], 1)
                for m in range(NC):
                    dve.wait_ge(s["swap"], NC * b + m + 1)
                    dve.tensor_tensor(rot2[:, m, :], swap[b % 2][:, m, :], sin_t[:, b * S:(b + 1) * S], ALU.mult).then_inc(s["rot2"], 1)
                for m in range(NC):
                    dve.wait_ge(s["rot2"], NC * b + m + 1)
                    dve.wait_ge(s["rot1"], NC * b + m + 1)
                    dve.tensor_tensor(swap[b % 2][:, m, :], rot1[:, m, :], rot2[:, m, :], ALU.add).then_inc(s["rot"], 1)

            def low_rot(n, b):
                s = pj[n]
                for m in range(NC):
                    dve.wait_ge(s["hi"], NC * b + m + 1)
                    dve.tensor_tensor(parts[n][:, m, 1, :], swap[b % 2][:, m, :], parts[n][:, m, 0, :].bitcast(F32), ALU.subtract).then_inc(s["lo"], 1)

            def values(n, row, b, first_bank):
                s = pj[n]
                for k in range(2):
                    dve.wait_ge(s["v"], 2 * b + k + 1)
                    wait(dve, s["vsent"][2 * k], 16 * b)
                    wait(dve, s["vsent"][2 * k + 1], 16 * b)
                    dve.tensor_tensor(vt[:, 2 * k:2 * k + 2, :, 0:DK], bank[:, first_bank + k, :].rearrange("p (t h d) -> p t h d", t=2, h=H),
                                      row[:, :].rearrange("p (o h d) -> p o h d", o=1, h=H).broadcast_to([P, 2, H, DK]), ALU.add).then_inc(s["vt"], 1)

            dve.wait_ge(trig_out, 2 * B)
            dve.wait_ge(vt_init, 1)
            dve.wait_ge(ctx_w_in, 64)
            for b in range(B):
                rotate("ctx", b)
                if b == 0:
                    dve.wait_ge(x_in, 16)
                layer_norm("self", XN, b)
                values("ctx", bxv_row, b, 2)
                low_rot("ctx", b)
                normalise("self", XN, b)
            dve.wait_ge(w_in, 16 * 10)
            s = pj["self"]
            for b in range(B):
                for m in range(4):
                    dve.wait_ge(s["hi"], 4 * b + m + 1)
                    dve.scalar_tensor_tensor(out=hl[:, m, 1, :], in0=bank[:, m, :], scalar=bqk_col[:, m:m + 1], in1=hl[:, m, 0, :].bitcast(F32),
                                             op0=ALU.add, op1=ALU.subtract).then_inc(s["lo"], 1)
                values("self", bv_row, b, 6)

            def outputs(a, u, n, slot_bank, dst):
                s = a["s"]
                dve.wait_ge(s["swrote"], n)
                dve.wait_ge(s["sread"], n - 1)
                src = bank[:, slot_bank, :].rearrange("p (q h e) -> p q h e", q=TB, h=HG)
                dve.reciprocal(R[:, :].rearrange("p (q h) -> p q h", q=TB), src[:, :, :, DK]).then_inc(s["recip"], 1)
                dve.wait_ge(s["recip"], u + 1)
                g, b = u // B, u % B
                to = unit_columns(dst, b * (TB * D) + g * GW)
                dve.tensor_tensor(to, src[:, :, :, 0:DK],
                                  R[:, :].rearrange("p (q h o) -> p q h o", q=TB, o=1).broadcast_to([P, TB, HG, DK]), ALU.mult).then_inc(s["sread"], 1)

            def unit_columns(dst, col):
                full = dst[:, 0:TB, 0:GW].rearrange("p t (h d) -> p t h d", h=HG)
                return bass.AP(full.tensor, full.offset + col, full.ap)

            def row_max(a, n, slot_bank, c):
                s = a["s"]
                keys = P * (c % TB + 1) if a["causal"] else S
                dve.wait_ge(s["swrote"], n)
                dve.tensor_reduce(M[:, c:c + 1], bank[:, slot_bank, 0:keys], AX_X, ALU.max).then_inc(s["sread"], 1)

            def shift_rows(a, u, n, slot_bank):
                s = a["s"]
                dve.wait_ge(s["swrote"], n)
                if not (isinstance(u, int) and u == 0):
                    dve.wait_ge(s["expd"], TAUS * (u - 1) + 1)
                dve.tensor_scalar(MR[:, :], bank[0:HG * TB, slot_bank, 0:P], -1.0, None, ALU.mult).then_inc(s["sread"], 1)

            def unit(a, u, j, dst):
                n = 0
                done = {"r": 0 if is_unit(u, 0) else ahead(a), "n": 0}
                for tau in range(TAUS):
                    for kind in uses_of(a, u, tau):
                        count, src = first_use(a, u) + (n + 1), slot_of(a, u, n)
                        if kind == "o":
                            outputs(a, u - 1, count, src, dst)
                        elif kind == "m":
                            shift_rows(a, u + 1, count, src)
                        else:
                            row_max(a, count, src, done[kind])
                            done[kind] += 1
                        n += 1
                    if not a["causal"] and tau - 1 in VECTOR_TILES:
                        dve.wait_ge(a["s"]["expd"], TAUS * u + tau)
                        if is_unit(u, 0) and tau - 1 == VECTOR_TILES[0]:
                            dve.wait_ge(t_loaded, 16 * G)
                        add_relative(dve, a, u, tau - 1, 1, a["s"]["biased_v"])

            def attention(a, dst):
                for c in range(HG * TB):
                    row_max(a, c + 1, slot(c), c)
                shift_rows(a, 0, HG * TB + 1, slot(HG * TB))
                units(dve, lambda u, j: unit(a, u, j, dst))
                outputs(a, U - 1, first_use(a, U - 1) + 2, slot_of(a, U - 1, 1), dst)

            def residual(n, b):
                s = out_s[n]
                if b == 0:
                    dve.wait_ge(s["bias"], 1)
                for k in range(2):
                    t = TB * b + 2 * k
                    dve.wait_ge(s["mm"], 2 * b + k + 1)
                    dve.tensor_tensor(X[:, t:t + 2, :], X[:, t:t + 2, :], bank[:, 2 + k, :].rearrange("p (t d) -> p t d", t=2), ALU.add).then_inc(s["add"], 1)

            def residual_norm(o, n, b):
                residual(o, b)
                dve.wait_ge(out_s[o]["add"], 2 * b + 2)
                layer_norm(n, XN, b)
                normalise(n, XN, b)

            attention(a1, XN)
            residual_norm("o1", "xq", 0)
            for b in range(B):
                if b + 1 < B:
                    residual_norm("o1", "xq", b + 1)
                if b >= 1:
                    low_rot("xq", b - 1)
                rotate("xq", b)
            low_rot("xq", B - 1)
            attention(a2, XN)
            for b in range(B):
                residual_norm("o2", "moe", b)

            steps = {"n": 0}

            def route(ins):
                steps["n"] += 1
                ins.then_inc(mo["route"], 1)
                dve.wait_ge(mo["route"], steps["n"])

            def tiles_route(make):
                for t in range(NT):
                    steps["n"] += 1
                    make(t).then_inc(mo["route"], 1)
                dve.wait_ge(mo["route"], steps["n"])

            def one_hot(sel, idx, k, n):
                return dve.tensor_tensor(sel[:, :, :, :], iota_e[:, 0:n].rearrange("p (a b n) -> p a b n", a=1, b=1).broadcast_to([P, NT, k, n]),
                                         idx[:, :, 0:k].rearrange("p t (k o) -> p t k o", o=1).broadcast_to([P, NT, k, n]), ALU.is_equal)

            dve.wait_ge(mo["iota"], 1)
            dve.wait_ge(a2["s"]["oevac"], U)
            route(dve.tensor_copy(iota_e[:, :], iota_i[:, :]))

            def choose_groups():
                dve.wait_ge(mo["score"], B)
                dve.wait_ge(mo["gate_in"], 16)
                route(dve.tensor_tensor(sfc[:, :, :], score[:, :, :], bias_e[:, :].rearrange("p (o e) -> p o e", o=1).broadcast_to([P, NT, E]), ALU.add))
                route(dve.tensor_reduce(gmax[:, :, :], sfc[:, :, :].rearrange("p t (g e) -> p t g e", g=NGROUP), AX_X, ALU.max))
                tiles_route(lambda t: dve.max(gtop[:, t, :], gmax[:, t, :]))
                tiles_route(lambda t: dve.max_index(gidx[:, t, :], gtop[:, t, :], gmax[:, t, :]))
                route(dve.tensor_copy(gidx_f[:, :, :], gidx[:, :, :]))
                route(one_hot(gsel, gidx_f, TOPG, NGROUP))
                route(dve.tensor_reduce(gmask[:, :, :], gsel[:, :, :, :].rearrange("p t k g -> p t g k"), AX_X, ALU.add))
                route(dve.tensor_tensor(masked[:, :, :].rearrange("p t (g e) -> p t g e", g=NGROUP), sfc[:, :, :].rearrange("p t (g e) -> p t g e", g=NGROUP),
                                        gmask[:, :, :].rearrange("p t (g o) -> p t g o", o=1).broadcast_to([P, NT, NGROUP, GE]), ALU.mult))

            def choose_experts():
                tiles_route(lambda t: dve.max(etop[:, t, :], masked[:, t, :]))
                tiles_route(lambda t: dve.max_index(eidx[:, t, :], etop[:, t, :], masked[:, t, :]))
                route(dve.tensor_copy(eidx_f[:, :, :], eidx[:, :, :]))
                route(one_hot(esel, eidx_f, TOPK, E))

            def count_choices():
                route(dve.tensor_reduce(chosen[:, :, :], esel[:, :, :, :].rearrange("p t k e -> p t e k"), AX_X, ALU.add))

            def combine_weights():
                route(dve.tensor_tensor(picked[:, :, :], chosen[:, :, :], score[:, :, :], ALU.mult))
                route(dve.tensor_reduce(tws[:, :], picked[:, :, :], AX_X, ALU.add))
                route(dve.tensor_scalar(twe[:, :], tws[:, :], 1e-20, None, ALU.add))
                route(dve.reciprocal(twr[:, :], twe[:, :]))
                route(dve.scalar_tensor_tensor(out=comb[:, SHARED * NT:].rearrange("p (e t) -> p t e", t=NT), in0=picked[:, :, :], scalar=ROUTED_SCALE,
                                               in1=twr[:, :].rearrange("p (t o) -> p t o", o=1).broadcast_to([P, NT, E]), op0=ALU.mult, op1=ALU.mult))

            dve.wait_ge(mo["ones"], 1)

            def accumulate(st, j, ej, b, first, tiles):
                dve.wait_ge(mo["down"], st + 1)
                if not first:
                    dve.wait_ge(mo["acc"], TB * (st - (B - 1)))
                for k in tiles:
                    t = TB * b + k
                    dve.scalar_tensor_tensor(out=X[:, t, :], in0=bank[:, 4 + 2 * j + k // 2, (k % 2) * D:(k % 2 + 1) * D], scalar=csel[ej][:, t:t + 1],
                                             in1=X[:, t, :], op0=ALU.mult, op1=ALU.add).then_inc(mo["acc"], 1)

            def expert_pair(i, first=False):
                for n in range(2 * B):
                    st, j = 2 * B * i + n, n % 2
                    dve.wait_ge(mo["silu"], st + 1)
                    dve.wait_ge(mo["gu"], 2 * st + 2)
                    if not (first and n < 2):
                        dve.wait_ge(mo["hi"], st - 1)
                    dve.tensor_tensor(hid[j][:, :], sg[j][:, :], bank[:, 2 + j, :], ALU.mult).then_inc(mo["h"], 1)
                    before = (st - 1, (j + 1) % 2, ((n - 1) % (2 * B)) // B, (n - 1) % B, first and n <= B)
                    if not (first and n == 0):
                        accumulate(*before, range(TB // 2))
                    if n % B == 0:
                        e = 2 * i + n // B
                        if not first:
                            dve.wait_ge(mo["acc"], TB * B * (e - 1))
                        dve.tensor_copy(csel[n // B][:, :], comb[:, bass.ds(e * NT, NT)]).then_inc(mo["sel"], 1)
                    dve.wait_ge(mo["hi"], st + 1)
                    dve.tensor_tensor(hhl[j][:, 1, :], hid[j][:, :], hhl[j][:, 0, :].bitcast(F32), ALU.subtract).then_inc(mo["lo"], 1)
                    if not (first and n == 0):
                        accumulate(*before, range(TB // 2, TB))
                    if n % B == 0:
                        dve.wait_ge(mo["sel"], e + 1)
                    if first and n == 0:
                        choose_groups()
                    if first and n == 1:
                        choose_experts()
                    if first and n == 2:
                        count_choices()
                    if first and n == 3:
                        combine_weights()

            expert_pair(0, first=True)
            with dve.Fori(1, EA // 2) as i:
                expert_pair(i)
            accumulate(B * EA - 1, 1, 1, B - 1, False, range(TB))


def kernel(**inputs):
    import numpy as _np
    import concourse.bacc as _bacc
    from concourse import mybir as _mybir
    from concourse.bass_utils import run_bass_kernel_spmd as _run

    def f(name):
        return _np.asarray(inputs[name])

    gate_up = _np.concatenate([_np.stack([f("L0_ffn_shared_gate_w"), f("L0_ffn_shared_up_w")]).reshape(2, SHARED, I, NC, P).transpose(1, 0, 2, 3, 4),
                               f("L0_ffn_experts_gate_up").reshape(E, 2, I, NC, P)])
    down = _np.concatenate([f("L0_ffn_shared_down_w").reshape(D, SHARED, I).transpose(1, 0, 2), f("L0_ffn_experts_down")])
    laid = {
        "x": f("x"),
        "ctx_t": f("ctx_1024").reshape(B * S, D).T,
        "pos": f("pos_BxS2"),
        "w_qkv": f("L0_attn_W_qkv"),
        "b_qkv_col": f("L0_attn_b_qkv")[0:2 * D].reshape(2 * NC, P).T,
        "b_v": f("L0_attn_b_qkv")[2 * D:],
        "w_out": f("L0_attn_W_out"),
        "b_out": f("L0_attn_b_out"),
        "rel_pad": _np.pad(f("L0_attn_rel_bias").T, ((0, 0), (MAX_REL - 1, RPW - (2 * MAX_REL + 1) - (MAX_REL - 1))), mode="edge"),
        "xw_q": f("L0_xattn_w_q"), "xb_q": f("L0_xattn_b_q").reshape(NC, P).T,
        "xw_k": f("L0_xattn_w_k"), "xb_k": f("L0_xattn_b_k").reshape(NC, P).T,
        "xw_v": f("L0_xattn_w_v"), "xb_v": f("L0_xattn_b_v"),
        "xw_o": f("L0_xattn_w_o"), "xb_o": f("L0_xattn_b_o"),
        "w_gate": f("L0_ffn_gate_weight").reshape(E, NC, P).transpose(2, 1, 0),
        "e_bias": f("L0_ffn_e_score_correction_bias"),
        "w_exp": _np.concatenate([gate_up.transpose(0, 4, 3, 1, 2).reshape(EA, P, NC * 2 * I), down.transpose(0, 2, 1)], axis=2),
    }
    nc = _bacc.Bacc("TRN2", target_bir_lowering=False, num_devices=1)
    arrays, args = {}, []
    for name, a in laid.items():
        a = _np.ascontiguousarray(a)
        arrays[f"in_{name}"] = a
        args.append(nc.dram_tensor(f"in_{name}", a.shape, _mybir.dt.from_np(a.dtype), kind="ExternalInput").ap())
    args.append(nc.dram_tensor("out_x", (B, S, D), _mybir.dt.float32, kind="ExternalOutput").ap())
    program(nc, *args)
    r = _run(nc, [arrays], core_ids=[0])
    return r.results[0]["out_x"]
```
